# Optimizing a Trainium2 kernel written in Bass

```python
import numpy as np
import jax
import jax.numpy as jnp

def _softmax(x, axis=-1):
    return jax.nn.softmax(x, axis=axis)

def _gelu(x):
    return jax.nn.gelu(x, approximate=True)

def _silu(x):
    return jax.nn.silu(x)

def _sigmoid(x):
    return jax.nn.sigmoid(x)

def _layernorm(x, axis=-1, eps=1e-05):
    m = jnp.mean(x, axis=axis, keepdims=True)
    v = jnp.var(x, axis=axis, keepdims=True)
    return (x - m) / jnp.sqrt(v + eps)

def _scatter_add(tgt, idx, src, axis=0):
    return tgt.at[idx].add(src)

def _segment_sum(src, seg, n):
    return jax.ops.segment_sum(src, seg, n)
kernel_name = 'mk_flamingo_gated_d2_seqx_r4_c38122'

def setup_inputs(seed: int=0):
    np.random.seed(seed)
    _w = jnp.asarray

    def _rec_inputs():
        import jax
        import jax.numpy as jnp
        _rk = jax.random.key(seed)
        x = -0.0002928 + 1 * jax.random.normal(jax.random.fold_in(_rk, 1), (1, 2048, 256), jnp.float32)
        _lenS = 2048 - jax.random.randint(jax.random.fold_in(_rk, 7), (1,), 0, max(1, 2048 // 4) + 1, jnp.int32)
        _lenS2 = 1601 - jax.random.randint(jax.random.fold_in(_rk, 8), (1,), 0, max(1, 1601 // 4) + 1, jnp.int32)
        _ctx_1024P = jax.random.normal(jax.random.fold_in(_rk, 11), (1, 16, 256), jnp.float32)
        _ctx_1024c = jax.random.dirichlet(jax.random.fold_in(_rk, 511), 0.3 * jnp.ones((16,), jnp.float32), (1, 1601))
        _ctx_1024t = jnp.einsum('bsk,bkd->bsd', _ctx_1024c, _ctx_1024P)
        _ctx_1024t = _ctx_1024t * jax.lax.rsqrt(jnp.mean(jnp.square(_ctx_1024t)) + 1e-12) * 0.953939
        ctx_1024 = -1.39393e-06 + 0.999914 * (_ctx_1024t + 0.3 * jax.random.normal(jax.random.fold_in(_rk, 611), (1, 1601, 256), jnp.float32))
        _validS = jnp.arange(2048)[None, :] < _lenS[:, None]
        _validS2 = jnp.arange(1601)[None, :] < _lenS2[:, None]
        _causal = jnp.tril(jnp.ones((2048, 2048), dtype=bool))
        mask_BxSxS2_ik0 = jnp.where(jnp.broadcast_to(_validS2[:, None, :], (1, 2048, 1601)), 0, 1).astype(jnp.int32)
        _g = jax.random.normal(jax.random.fold_in(_rk, 9001), (2, 2), jnp.float32)
        _g = jnp.sign(_g) * jnp.maximum(jnp.abs(_g), 1.0) + (_g == 0) * 1.0
        g_xattn = _g[0]
        g_ffn = _g[1]
        return (x, ctx_1024, mask_BxSxS2_ik0, g_xattn, g_ffn)
    x, ctx_1024, mask_BxSxS2_ik0, g_xattn, g_ffn = _rec_inputs()

    def _L0_xattn_setup():
        import jax, jax.numpy as jnp
        import numpy as np
        B, S, D, H = (2, 512, 256, 16)
        DK = D // H

        def _proj(x, w, b):
            y = jnp.einsum('bsd,ed->bse', x, w) + b
            return y.reshape(x.shape[0], -1, H, DK).transpose(0, 2, 1, 3)
        key = jax.random.key(seed)
        ks = jax.random.split(key, 12)
        scale = 1.0 / np.sqrt(D)
        inp = {'query': jax.random.normal(ks[0], (B, S, D), dtype=jnp.float32), 'key': jax.random.normal(ks[1], (B, S, D), dtype=jnp.float32), 'value': jax.random.normal(ks[2], (B, S, D), dtype=jnp.float32), 'mask': jnp.broadcast_to(jnp.tril(jnp.ones((S, S), dtype=jnp.int32)), (B, S, S)), 'wq': jax.random.normal(ks[3], (D, D), dtype=jnp.float32) * scale, 'bq': jnp.zeros((D,), dtype=jnp.float32), 'wk': jax.random.normal(ks[4], (D, D), dtype=jnp.float32) * scale, 'bk': jnp.zeros((D,), dtype=jnp.float32), 'wv': jax.random.normal(ks[5], (D, D), dtype=jnp.float32) * scale, 'bv': jnp.zeros((D,), dtype=jnp.float32), 'wo': jax.random.normal(ks[6], (D, D), dtype=jnp.float32) * scale, 'bo': jnp.zeros((D,), dtype=jnp.float32)}
        return inp
    _L0_xattn_all = _L0_xattn_setup()
    _L0_xattn_in = {k: v for k, v in _L0_xattn_all.items() if k in ('wq', 'bq', 'wk', 'bk', 'wv', 'bv', 'wo', 'bo')}
    del _L0_xattn_all

    def _L0_ffn_setup():
        import jax, jax.numpy as jnp
        import numpy as np
        HIDDEN = 256
        INTER = 1024
        N_EXPERTS = 8

        def geglu(x, w1, w2, w3):
            return jax.nn.gelu(x @ w1, approximate=False) * (x @ w2) @ w3
        key = jax.random.key(seed)
        ks = jax.random.split(key, 8)
        s = 0.02
        x = jax.random.normal(ks[0], (2, 512, HIDDEN), dtype=jnp.float32)
        w1s = jax.random.normal(ks[1], (HIDDEN, INTER), dtype=jnp.float32) * s
        w2s = jax.random.normal(ks[2], (HIDDEN, INTER), dtype=jnp.float32) * s
        w3s = jax.random.normal(ks[3], (INTER, HIDDEN), dtype=jnp.float32) * s
        W1 = jax.random.normal(ks[4], (N_EXPERTS, HIDDEN, INTER), dtype=jnp.float32) * s
        W2 = jax.random.normal(ks[5], (N_EXPERTS, HIDDEN, INTER), dtype=jnp.float32) * s
        W3 = jax.random.normal(ks[6], (N_EXPERTS, INTER, HIDDEN), dtype=jnp.float32) * s
        Wg = jax.random.normal(ks[7], (HIDDEN, N_EXPERTS), dtype=jnp.float32) * s
        return {'x': x, 'w1s': w1s, 'w2s': w2s, 'w3s': w3s, 'W1': W1, 'W2': W2, 'W3': W3, 'Wg': Wg}
    _L0_ffn_all = _L0_ffn_setup()
    _L0_ffn_in = {k: v for k, v in _L0_ffn_all.items() if k in ('w1s', 'w2s', 'w3s', 'W1', 'W2', 'W3', 'Wg')}
    del _L0_ffn_all

    def _L1_xattn_setup():
        import jax, jax.numpy as jnp
        import numpy as np
        D_MODEL = 256
        NUM_HEADS = 16
        DEPTH = D_MODEL // NUM_HEADS

        def _split_heads(x, B):
            return x.reshape(B, -1, NUM_HEADS, DEPTH).transpose(0, 2, 1, 3)
        key = jax.random.key(seed)
        ks = jax.random.split(key, 10)
        B, LQ, LK = (4, 512, 512)
        bound = float(np.sqrt(6.0 / (D_MODEL + D_MODEL)))

        def w(k):
            return jax.random.uniform(k, (D_MODEL, D_MODEL), jnp.float32, -bound, bound)
        return {'query': jax.random.normal(ks[0], (B, LQ, D_MODEL), jnp.float32), 'value': jax.random.normal(ks[1], (B, LK, D_MODEL), jnp.float32), 'wq': w(ks[2]), 'bq': jnp.zeros((D_MODEL,), jnp.float32), 'wk': w(ks[3]), 'bk': jnp.zeros((D_MODEL,), jnp.float32), 'wv': w(ks[4]), 'bv': jnp.zeros((D_MODEL,), jnp.float32), 'wo': w(ks[5]), 'bo': jnp.zeros((D_MODEL,), jnp.float32)}
    _L1_xattn_all = _L1_xattn_setup()
    _L1_xattn_in = {k: v for k, v in _L1_xattn_all.items() if k in ('wq', 'bq', 'wk', 'bk', 'wv', 'bv', 'wo', 'bo')}
    del _L1_xattn_all

    def _L1_ffn_setup():
        import jax, jax.numpy as jnp
        import numpy as np
        TOP_K = 2
        ROUTE_SCALE = 1.0
        EPS = 1e-20
        B, S, D = (2, 128, 256)
        E = 8
        F = 192
        FS = 192 * 1
        key = jax.random.key(seed)
        ks = jax.random.split(key, 9)
        s = 0.02
        return {'hidden_states': jax.random.normal(ks[0], (B, S, D), dtype=jnp.float32), 'W_gate_router': jax.random.normal(ks[1], (D, E), dtype=jnp.float32) * s, 'expert_bias': jnp.zeros((E,), dtype=jnp.float32), 'Wg': jax.random.normal(ks[2], (E, D, F), dtype=jnp.float32) * s, 'Wu': jax.random.normal(ks[3], (E, D, F), dtype=jnp.float32) * s, 'Wd': jax.random.normal(ks[4], (E, F, D), dtype=jnp.float32) * s, 'Wg_s': jax.random.normal(ks[5], (D, FS), dtype=jnp.float32) * s, 'Wu_s': jax.random.normal(ks[6], (D, FS), dtype=jnp.float32) * s, 'Wd_s': jax.random.normal(ks[7], (FS, D), dtype=jnp.float32) * s}
    _L1_ffn_all = _L1_ffn_setup()
    _L1_ffn_in = {k: v for k, v in _L1_ffn_all.items() if k in ('W_gate_router', 'expert_bias', 'Wg', 'Wu', 'Wd', 'Wg_s', 'Wu_s', 'Wd_s')}
    del _L1_ffn_all
    return {'x': x, 'ctx_1024': ctx_1024, 'mask_BxSxS2_ik0': mask_BxSxS2_ik0, 'g_xattn': g_xattn, 'g_ffn': g_ffn, 'L0_xattn_wq': _L0_xattn_in['wq'], 'L0_xattn_bq': _L0_xattn_in['bq'], 'L0_xattn_wk': _L0_xattn_in['wk'], 'L0_xattn_bk': _L0_xattn_in['bk'], 'L0_xattn_wv': _L0_xattn_in['wv'], 'L0_xattn_bv': _L0_xattn_in['bv'], 'L0_xattn_wo': _L0_xattn_in['wo'], 'L0_xattn_bo': _L0_xattn_in['bo'], 'L0_ffn_w1s': _L0_ffn_in['w1s'], 'L0_ffn_w2s': _L0_ffn_in['w2s'], 'L0_ffn_w3s': _L0_ffn_in['w3s'], 'L0_ffn_W1': _L0_ffn_in['W1'], 'L0_ffn_W2': _L0_ffn_in['W2'], 'L0_ffn_W3': _L0_ffn_in['W3'], 'L0_ffn_Wg': _L0_ffn_in['Wg'], 'L1_xattn_wq': _L1_xattn_in['wq'], 'L1_xattn_bq': _L1_xattn_in['bq'], 'L1_xattn_wk': _L1_xattn_in['wk'], 'L1_xattn_bk': _L1_xattn_in['bk'], 'L1_xattn_wv': _L1_xattn_in['wv'], 'L1_xattn_bv': _L1_xattn_in['bv'], 'L1_xattn_wo': _L1_xattn_in['wo'], 'L1_xattn_bo': _L1_xattn_in['bo'], 'L1_ffn_W_gate_router': _L1_ffn_in['W_gate_router'], 'L1_ffn_expert_bias': _L1_ffn_in['expert_bias'], 'L1_ffn_Wg': _L1_ffn_in['Wg'], 'L1_ffn_Wu': _L1_ffn_in['Wu'], 'L1_ffn_Wd': _L1_ffn_in['Wd'], 'L1_ffn_Wg_s': _L1_ffn_in['Wg_s'], 'L1_ffn_Wu_s': _L1_ffn_in['Wu_s'], 'L1_ffn_Wd_s': _L1_ffn_in['Wd_s']}

def reference(x, ctx_1024, mask_BxSxS2_ik0, g_xattn, g_ffn, L0_xattn_wq, L0_xattn_bq, L0_xattn_wk, L0_xattn_bk, L0_xattn_wv, L0_xattn_bv, L0_xattn_wo, L0_xattn_bo, L0_ffn_w1s, L0_ffn_w2s, L0_ffn_w3s, L0_ffn_W1, L0_ffn_W2, L0_ffn_W3, L0_ffn_Wg, L1_xattn_wq, L1_xattn_bq, L1_xattn_wk, L1_xattn_bk, L1_xattn_wv, L1_xattn_bv, L1_xattn_wo, L1_xattn_bo, L1_ffn_W_gate_router, L1_ffn_expert_bias, L1_ffn_Wg, L1_ffn_Wu, L1_ffn_Wd, L1_ffn_Wg_s, L1_ffn_Wu_s, L1_ffn_Wd_s):
    import jax
    import jax.numpy as jnp

    def _L0_xattn_ref(query, key, value, mask, wq, bq, wk, bk, wv, bv, wo, bo):
        import jax, jax.numpy as jnp
        import numpy as np
        B, S, D, H = (2, 512, 256, 16)
        DK = D // H

        def _proj(x, w, b):
            y = jnp.einsum('bsd,ed->bse', x, w) + b
            return y.reshape(x.shape[0], -1, H, DK).transpose(0, 2, 1, 3)
        q = _proj(query, wq, bq)
        k = _proj(key, wk, bk)
        v = _proj(value, wv, bv)
        scores = jnp.einsum('bhqd,bhkd->bhqk', q, k) / jnp.sqrt(jnp.float32(DK))
        scores = jnp.where(mask[:, None, :, :] == 0, -jnp.inf, scores)
        p_attn = jax.nn.softmax(scores, axis=-1)
        x = jnp.einsum('bhqk,bhkd->bhqd', p_attn, v)
        x = x.transpose(0, 2, 1, 3).reshape(query.shape[0], -1, H * DK)
        return jnp.einsum('bsd,ed->bse', x, wo) + bo

    def _L0_ffn_ref(x, w1s, w2s, w3s, W1, W2, W3, Wg):
        import jax, jax.numpy as jnp
        import numpy as np
        HIDDEN = 256
        INTER = 1024
        N_EXPERTS = 8

        def geglu(x, w1, w2, w3):
            return jax.nn.gelu(x @ w1, approximate=False) * (x @ w2) @ w3
        B, T, C = x.shape
        xf = x.reshape(-1, C)
        shared = geglu(xf, w1s, w2s, w3s)
        logits = xf @ Wg
        idx = jnp.argmax(logits, axis=-1)
        final = jnp.zeros_like(xf)
        for e in range(N_EXPERTS):
            y = geglu(xf, W1[e], W2[e], W3[e])
            final = final + jnp.where((idx == e)[:, None], y, 0.0)
        return (shared + final).reshape(B, T, C)

    def _L1_xattn_ref(query, value, wq, bq, wk, bk, wv, bv, wo, bo):
        import jax, jax.numpy as jnp
        import numpy as np
        D_MODEL = 256
        NUM_HEADS = 16
        DEPTH = D_MODEL // NUM_HEADS

        def _split_heads(x, B):
            return x.reshape(B, -1, NUM_HEADS, DEPTH).transpose(0, 2, 1, 3)
        B = query.shape[0]
        q = _split_heads(query @ wq.T + bq, B)
        k = _split_heads(value @ wk.T + bk, B)
        v = _split_heads(value @ wv.T + bv, B)
        scale = jnp.sqrt(jnp.asarray(DEPTH, dtype=q.dtype))
        scores = jnp.einsum('bhqd,bhkd->bhqk', q, k) / scale
        attn = jax.nn.softmax(scores, axis=-1)
        ctx = jnp.einsum('bhqk,bhkd->bhqd', attn, v)
        ctx = ctx.transpose(0, 2, 1, 3).reshape(B, -1, D_MODEL)
        return ctx @ wo.T + bo

    def _L1_ffn_ref(hidden_states, W_gate_router, expert_bias, Wg, Wu, Wd, Wg_s, Wu_s, Wd_s):
        import jax, jax.numpy as jnp
        import numpy as np
        TOP_K = 2
        ROUTE_SCALE = 1.0
        EPS = 1e-20
        B, S, D = (2, 128, 256)
        E = 8
        F = 192
        FS = 192 * 1
        b, s, d = hidden_states.shape
        x = hidden_states.reshape(-1, d)
        T = x.shape[0]
        logits = x @ W_gate_router
        scores = jax.nn.sigmoid(logits.astype(jnp.float32))
        _, sel = jax.lax.top_k(scores + expert_bias, TOP_K)
        top_scores = jnp.take_along_axis(scores, sel, axis=1)
        top_scores = top_scores / (top_scores.sum(-1, keepdims=True) + EPS)
        top_scores = top_scores * ROUTE_SCALE
        shared = jax.nn.silu(x @ Wg_s) * (x @ Wu_s) @ Wd_s
        tok = jnp.repeat(jnp.arange(T), TOP_K)
        exp = sel.reshape(-1)
        w = top_scores.reshape(-1)
        xr = x[tok]
        h = jax.nn.silu(jnp.einsum('nd,edf->enf', xr, Wg)) * jnp.einsum('nd,edf->enf', xr, Wu)
        out_all = jnp.einsum('enf,efd->end', h, Wd)
        routed = out_all[exp, jnp.arange(exp.shape[0])]
        routed = (routed.astype(jnp.float32) * w[:, None]).astype(hidden_states.dtype)
        out = shared.at[tok].add(routed)
        return out.reshape(b, s, d)
    x = x + jnp.tanh(g_xattn[0]) * _L0_xattn_ref(_layernorm(x, axis=-1), ctx_1024, ctx_1024, mask_BxSxS2_ik0, L0_xattn_wq, L0_xattn_bq, L0_xattn_wk, L0_xattn_bk, L0_xattn_wv, L0_xattn_bv, L0_xattn_wo, L0_xattn_bo)
    x = x + jnp.tanh(g_ffn[0]) * _L0_ffn_ref(_layernorm(x, axis=-1), L0_ffn_w1s, L0_ffn_w2s, L0_ffn_w3s, L0_ffn_W1, L0_ffn_W2, L0_ffn_W3, L0_ffn_Wg)
    x = x + jnp.tanh(g_xattn[1]) * _L1_xattn_ref(_layernorm(x, axis=-1), ctx_1024, L1_xattn_wq, L1_xattn_bq, L1_xattn_wk, L1_xattn_bk, L1_xattn_wv, L1_xattn_bv, L1_xattn_wo, L1_xattn_bo)
    x = x + jnp.tanh(g_ffn[1]) * _L1_ffn_ref(_layernorm(x, axis=-1), L1_ffn_W_gate_router, L1_ffn_expert_bias, L1_ffn_Wg, L1_ffn_Wu, L1_ffn_Wd, L1_ffn_Wg_s, L1_ffn_Wu_s, L1_ffn_Wd_s)
    return x

_drawn_inputs = setup_inputs


def setup_inputs(seed=0):
    import zlib

    import numpy as np

    out = dict(_drawn_inputs(seed))
    spreads = {'g_ffn': (-1.0, 0.6),
     'L0_xattn_bq': (0.0, 0.563),
     'L0_xattn_bk': (0.0, 0.8),
     'L0_xattn_bv': (0.0, 0.1),
     'L0_xattn_bo': (0.0, 0.1),
     'L1_xattn_bq': (0.0, 0.48),
     'L1_xattn_bk': (0.0, 0.8),
     'L1_xattn_bv': (0.0, 0.1),
     'L1_xattn_bo': (0.0, 0.1),
     'L1_ffn_expert_bias': (0.0, 0.8)}
    factors = {'L0_ffn_Wg': 2.719,
     'L1_ffn_W_gate_router': 8.0,
     'L1_ffn_Wg': 8.0,
     'L1_ffn_Wu': 7.742,
     'L1_ffn_Wd': 7.918,
     'L1_ffn_Wg_s': 5.722,
     'L1_ffn_Wu_s': 5.821,
     'L1_ffn_Wd_s': 5.727}
    for name, (base, spread) in spreads.items():
        noise = np.random.default_rng([zlib.crc32(name.encode()), seed]).standard_normal(out[name].shape)
        drawn = base * np.exp(spread * noise) if base else spread * noise
        out[name] = jnp.asarray(drawn.astype(out[name].dtype))
    for name, factor in factors.items():
        out[name] = (out[name] * factor).astype(out[name].dtype)
    return out
```

```python
from contextlib import ExitStack

import concourse.bass as bass
from concourse import mybir

F32 = mybir.dt.float32
BF16 = mybir.dt.bfloat16
I32 = mybir.dt.int32
ALU = mybir.AluOpType
ACT = mybir.ActivationFunctionType
AX = mybir.AxisListType

P = 128
T = 2048
D = 256
S = 1601
H = 16
DK = D // H
DB = D // P
QT = T // P
KT = -(-S // P)
CH = 512
NC = T // CH
HALF = 1024
PART = 3
ROWS = 6 * DK
AUG = ROWS + PART
PIECES = [(0, 401), (401, 400), (801, 400), (1201, 400)]
NP = len(PIECES)
VW = 32
NEG = -1.0e30
LATE = 3
E = 8
RING = 3
assert sum(n for _, n in PIECES) == S


def keys_of(kt):
    return min(P, S - kt * P)


def wait(eng, sem, value, apart=False):
    if isinstance(value, int):
        if value > 0:
            eng.wait_ge(sem, value)
    else:
        eng.wait_ge(sem, value)
        if apart:
            eng.nop(nofuse=True)


class Scope:

    used = []

    def __init__(self, nc, ctx, stage):
        self.nc, self.ctx, self.stage = nc, ctx, stage

    def sb(self, name, shape, dt):
        return self.ctx.enter_context(self.nc.sbuf_tensor(f"{self.stage}_{name}", shape, dt))

    def ps(self, name, shape, dt):
        return self.ctx.enter_context(self.nc.psum_tensor(f"{self.stage}_{name}", shape, dt))

    def sem(self, name):
        made = self.ctx.enter_context(self.nc.semaphore(f"{self.stage}_{name}"))
        Scope.used.append(made.num)
        return made


def clear_semaphores(nc):
    numbers = sorted(set(Scope.used))
    Scope.used.clear()
    runs = []
    for n in numbers:
        if runs and runs[-1][1] == n:
            runs[-1][1] = n + 1
        else:
            runs.append([n, n + 1])
    with nc.Block() as block:
        @block.gpsimd
        def _(pool):
            for first, end in runs:
                pool.sem_clear(range(first, end))


def make_constants(nc, io, const):
    with ExitStack() as ctx:
        sc = Scope(nc, ctx, "const")
        filled, made, gates_in, gated = sc.sem("filled"), sc.sem("made"), sc.sem("gates_in"), sc.sem("gated")
        raw = sc.sb("raw_gates", [P, 4], F32)
        block = ctx.enter_context(nc.Block())

        @block.gpsimd
        def _(pool):
            pool.memset(const["ident"][:, :], 0.0).then_inc(filled, 1)
            pool.memset(const["ident_bf"][:, :], 0.0).then_inc(filled, 1)
            for n, m in enumerate((const["ident"], const["ident_bf"])):
                pool.wait_ge(filled, n + 1)
                pool.affine_select(out=m[:, :], in_=m[:, :], compare_op=ALU.not_equal, fill=1.0, base=0,
                                   pattern=[[-1, P]], channel_multiplier=1).then_inc(made, 1)
            for e in range(E):
                pool.memset(const["expert_no"][:, :, e:e + 1], float(e)).then_inc(made, 1)

        @block.sync
        def _(sp):
            for n, g in enumerate(("g_xattn", "g_ffn")):
                sp.dma_start(raw[:, 2 * n:2 * n + 2],
                             io[g].rearrange("(a n) -> a n", a=1).broadcast_to([P, 2])).then_inc(gates_in, 16)

        @block.scalar
        def _(act):
            act.wait_ge(gates_in, 32)
            act.activation(const["gates"][:, :], raw[:, :], ACT.Tanh).then_inc(gated, 1)


def prepare_context(nc, io, const, scratch):
    with ExitStack() as ctx:
        sc = Scope(nc, ctx, "ctx")
        names = [f"L{l}_xattn_w{w}" for l in range(2) for w in "qkvo"]
        NW = len(names)
        w_nat = sc.sb("w_nat", [P, NW, DB, D], F32)
        b_nat = sc.sb("b_nat", [2 * DB * 2, P], F32)
        c_nat = sc.sb("c_nat", [P, KT, D], F32)
        c_t = sc.sb("c_t", [P, DB, S], F32)
        wk_t = sc.sb("wk_t", [P, 2, DB, D], F32)
        wv_t = sc.sb("wv_t", [P, DB, 2, D], F32)
        bv = sc.sb("bv", [P, 2, D], F32)
        k_full = sc.sb("k_full", [P, DB, S], F32)
        k_rest = sc.sb("k_rest", [P, DB, S], F32)
        k_part = sc.sb("k_part", [P, PART, DB, S], BF16)
        v_out = sc.sb("v_out", [P, KT, 2, D], F32)
        bank = [sc.ps(f"bank{n}", [P, CH], F32) for n in range(8)]
        w_in, b_in, c_in, bv_in = sc.sem("w_in"), sc.sem("b_in"), sc.sem("c_in"), sc.sem("bv_in")
        turned, copied = sc.sem("turned"), sc.sem("copied")
        c_turned, c_copied = sc.sem("c_turned"), sc.sem("c_copied")
        k_ready, k_copied = sc.sem("k_ready"), sc.sem("k_copied")
        v_ready, v_added = sc.sem("v_ready"), sc.sem("v_added")
        split, stored = sc.sem("split"), sc.sem("stored")
        block = ctx.enter_context(nc.Block())
        KCH = PIECES

        @block.sync
        def _(sp):
            for n, name in enumerate(names):
                sp.dma_start(w_nat[:, n], io[name].rearrange("(b p) d -> p b d", p=P)).then_inc(w_in, 16)
            for n, name in enumerate(["L0_xattn_bq", "L0_xattn_bk", "L1_xattn_bq", "L1_xattn_bk"]):
                sp.dma_start(b_nat[DB * n:DB * n + DB, :], io[name].rearrange("(b p) -> b p", p=P)).then_inc(b_in, 16)
            for l in range(2):
                for part in range(PART):
                    sp.wait_ge(split, 5 * l + (1, 3, 5)[part])
                    for b in range(DB):
                        sp.dma_start(scratch["k"][l, part, b * P:(b + 1) * P, :], k_part[:, part, b]).then_inc(stored, 16)
            sp.wait_ge(v_added, KT)
            for l in range(2):
                sp.dma_start(scratch["v"][l, 0:(KT - 1) * P, :].rearrange("(t p) d -> p t d", p=P),
                             v_out[:, 0:KT - 1, l]).then_inc(stored, 16)
                sp.dma_start(scratch["v"][l, (KT - 1) * P:S, :], v_out[0:keys_of(KT - 1), KT - 1, l]).then_inc(stored, 16)
            sp.wait_ge(stored, 16 * (2 * PART * DB + 4))

        def k_tiles():
            return [(l, b, c) for l in range(2) for b in range(DB) for c in range(len(KCH))]

        @block.tensor
        def _(pe):
            pe.wait_ge(w_in, 16 * NW)
            for n in range(NW):
                if n >= 2:
                    pe.wait_ge(copied, n - 1)
                for db in range(DB):
                    for eb in range(DB):
                        last = pe.transpose(bank[n % 2][:, db * D + eb * P:db * D + (eb + 1) * P],
                                            w_nat[:, n, eb, db * P:(db + 1) * P], const["ident"][:, :])
                last.then_inc(turned, 1)
            pe.wait_ge(b_in, 64)
            last = pe.transpose(bank[2][:, 0:4 * DB], b_nat[:, :], const["ident"][0:4 * DB, 0:4 * DB]).then_inc(turned, 1)
            pe.wait_ge(c_in, 32)
            for kt in range(KT):
                if kt >= 2:
                    pe.wait_ge(c_copied, kt - 1)
                kn = keys_of(kt)
                for db in range(DB):
                    last = pe.transpose(bank[4 + kt % 2][:, db * P:db * P + kn], c_nat[0:kn, kt, db * P:(db + 1) * P],
                                        const["ident"][0:kn, 0:kn])
                last.then_inc(c_turned, 1)
            pe.wait_ge(copied, NW + 1)
            pe.wait_ge(c_copied, KT)
            for n, (l, b, c) in enumerate(k_tiles()):
                if n >= 2:
                    pe.wait_ge(k_copied, n - 1)
                k0, kn = KCH[c]
                for db in range(DB):
                    last = pe.matmul(bank[n % 2][:, 0:kn], wk_t[:, l, db, b * P:(b + 1) * P], c_t[:, db, k0:k0 + kn],
                                     start=(db == 0), stop=(db == DB - 1))
                last.then_inc(k_ready, 1)
            for kt in range(KT):
                if kt >= 2:
                    pe.wait_ge(v_added, kt - 1)
                kn = keys_of(kt)
                for db in range(DB):
                    last = pe.matmul(bank[6 + kt % 2][0:kn, :], c_t[:, db, kt * P:kt * P + kn],
                                     wv_t[:, db].rearrange("p l d -> p (l d)"), start=(db == 0), stop=(db == DB - 1))
                last.then_inc(v_ready, 1)

        @block.scalar
        def _(act):
            act.dma_start(c_nat[:, 0:KT - 1], io["ctx_1024"][0, 0:(KT - 1) * P, :].rearrange("(t p) d -> p t d", p=P))\
                .then_inc(c_in, 16)
            act.dma_start(c_nat[0:keys_of(KT - 1), KT - 1], io["ctx_1024"][0, (KT - 1) * P:S, :]).then_inc(c_in, 16)
            for l in range(2):
                for dst, name in ((bv[:, l], f"L{l}_xattn_bv"), (const["bo"][:, l], f"L{l}_xattn_bo")):
                    act.dma_start(dst, io[name].rearrange("(a n) -> a n", a=1).broadcast_to([P, D])).then_inc(bv_in, 16)
            for n in range(NW):
                l, w = divmod(n, 4)
                dst = (const["wq_t"][:, l], wk_t[:, l], wv_t[:, :, l], const["wo_t"][:, l])[w]
                act.wait_ge(turned, n + 1)
                act.activation(dst, bank[n % 2][:, :].rearrange("p (b d) -> p b d", b=DB), ACT.Copy).then_inc(copied, 1)
            act.wait_ge(turned, NW + 1)
            act.activation(const["bqk"][:, :], bank[2][:, 0:4 * DB], ACT.Copy).then_inc(copied, 1)
            act.wait_ge(copied, NW + 1)
            for n, (l, b, c) in enumerate(k_tiles()):
                k0, kn = KCH[c]
                act.wait_ge(k_ready, n + 1)
                if c == 0 and b == 0 and l == 1:
                    act.wait_ge(split, 2)
                act.activation(k_full[:, b, k0:k0 + kn], bank[n % 2][:, 0:kn], ACT.Identity,
                               bias=const["bqk"][:, (2 * l + 1) * DB + b:(2 * l + 1) * DB + b + 1]).then_inc(k_copied, 1)

        @block.vector
        def _(dve):
            for kt in range(KT):
                kn = keys_of(kt)
                dve.wait_ge(c_turned, kt + 1)
                dve.tensor_copy(c_t[:, :, kt * P:kt * P + kn],
                                bank[4 + kt % 2][:, 0:DB * P].rearrange("p (b k) -> p b k", b=DB)[:, :, 0:kn])\
                    .then_inc(c_copied, 1)

            def split_keys(l):
                dve.wait_ge(k_copied, 2 * 4 * (l + 1))
                if l:
                    dve.wait_ge(stored, 16 * PART * DB)
                split_parts(dve, k_full[:, :, :], k_rest[:, :, :], [k_part[:, n] for n in range(PART)], split, 5 * l)

            split_keys(0)
            dve.wait_ge(bv_in, 64)
            split_keys(1)
            for kt in range(KT):
                kn = keys_of(kt)
                dve.wait_ge(v_ready, kt + 1)
                dve.tensor_tensor(v_out[0:kn, kt].rearrange("p l d -> p (l d)"), bank[6 + kt % 2][0:kn, :],
                                  bv[0:kn].rearrange("p l d -> p (l d)"), ALU.add).then_inc(v_added, 1)


def split_parts(dve, full, rest, parts, split, base):
    dve.tensor_copy(parts[0], full).then_inc(split, 1)
    dve.wait_ge(split, base + 1)
    dve.tensor_tensor(rest, full, parts[0], ALU.subtract).then_inc(split, 1)
    dve.wait_ge(split, base + 2)
    dve.tensor_copy(parts[1], rest).then_inc(split, 1)
    dve.wait_ge(split, base + 3)
    dve.tensor_tensor(rest, rest, parts[1], ALU.subtract).then_inc(split, 1)
    dve.wait_ge(split, base + 4)
    dve.tensor_copy(parts[2], rest).then_inc(split, 1)


def prepare_mask(nc, io, const, mask_q, mask_k):
    with ExitStack() as ctx:
        sc = Scope(nc, ctx, "mask")
        raw = sc.sb("raw", [P, 2, S], I32)
        FIRST = 8
        turn = [sc.ps(f"turn{n}", [P, 2 * FIRST * P], BF16) for n in range(2)]
        landed = [sc.sem("landed0"), sc.sem("landed1")]
        made, turned, copied = sc.sem("made"), sc.sem("turned"), sc.sem("copied")
        block = ctx.enter_context(nc.Block())
        kl = keys_of(KT - 1)

        @block.sync
        def _(sp):
            for t in range(QT):
                if t >= 2:
                    sp.wait_ge(made, t - 1)
                sp.dma_start(raw[:, t % 2], io["mask_BxSxS2_ik0"][0, t * P:(t + 1) * P, :]).then_inc(landed[t % 2], 16)

        @block.vector
        def _(dve):
            for t in range(QT):
                dve.wait_ge(landed[t % 2], 16 * (t // 2 + 1))
                dve.tensor_scalar(mask_q[:, t], raw[:, t % 2], 0.0, NEG, ALU.is_equal, ALU.mult).then_inc(made, 1)

        @block.tensor
        def _(pe):
            for t in range(QT):
                pe.wait_ge(made, t + 1)
                if t >= 2:
                    pe.wait_ge(copied, 3 * (t - 1))
                for kt in range(KT):
                    kn = keys_of(kt)
                    last = pe.transpose(turn[t % 2][0:kn, kt * P:(kt + 1) * P], mask_q[:, t, kt * P:kt * P + kn],
                                        const["ident_bf"][:, :])
                last.then_inc(turned, 1)

        @block.scalar
        def _(act):
            for t in range(QT):
                act.wait_ge(turned, t + 1)
                src = turn[t % 2][:, :].rearrange("p (k q) -> p k q", q=P)
                for p, a, b in ((P, 0, FIRST), (P, FIRST, KT - 1), (kl, KT - 1, KT)):
                    act.activation(mask_k[0:p, a:b, t * P:(t + 1) * P], src[0:p, a:b], ACT.Copy).then_inc(copied, 1)


def normalise(nc, const, stage, src, x_nt, x_norm_dram=None):
    with ExitStack() as ctx:
        sc = Scope(nc, ctx, stage)
        LD = 4
        x_in = sc.sb("x_in", [P, QT, D], F32)
        x_n = sc.sb("x_n", [P, QT, D], F32)
        stats = sc.sb("stats", [P, QT, 6], F32)
        mv = sc.sb("mv", [P, QT, 2], F32)
        var = sc.sb("var", [P, QT], F32)
        std = sc.sb("std", [P, QT], F32)
        inv = sc.sb("inv", [P, QT], F32)
        bank = [sc.ps(f"bank{n}", [P, CH], F32) for n in range(4)]
        landed = [sc.sem(f"landed{n}") for n in range(LD)]
        counted, spread, stable, rooted, inverted = (sc.sem(n) for n in ("counted", "spread", "stable", "rooted", "inverted"))
        scaled, turned = sc.sem("scaled"), sc.sem("turned")
        copied = [sc.sem("copied_dve"), sc.sem("copied_act")]
        stored = sc.sem("stored")
        block = ctx.enter_context(nc.Block())
        x_tiles = src.rearrange("(t p) d -> p t d", p=P)
        per = QT // LD

        @block.sync
        def _(sp):
            for n in range(LD):
                sp.dma_start(x_in[:, n * per:(n + 1) * per], x_tiles[:, n * per:(n + 1) * per]).then_inc(landed[n], 16)
            if x_norm_dram is not None:
                sp.wait_ge(scaled, QT)
                sp.dma_start(x_norm_dram.rearrange("(t p) d -> p t d", p=P), x_n[:, :, :]).then_inc(stored, 16)
                sp.wait_ge(stored, 16)

        def copy_out(n, copy, eng):
            eng.wait_ge(turned, n + 1)
            copy(x_nt[:, :, 2 * n * P:2 * (n + 1) * P].rearrange("p b (t q) -> p t b q", t=2),
                 bank[n % 4][:, :].rearrange("p (t b q) -> p t b q", t=2, b=DB)).then_inc(copied[n % 2], 1)

        @block.vector
        def _(dve):
            for t in range(QT):
                if t % per == 0:
                    dve.wait_ge(landed[t // per], 16)
                dve.bn_stats(stats[:, t], x_in[:, t]).then_inc(counted, 1)
            for t in range(QT):
                dve.wait_ge(counted, t + 1)
                dve.bn_aggr(mv[:, t], stats[:, t]).then_inc(spread, 1)
            dve.wait_ge(spread, QT)
            dve.tensor_scalar(var[:, :], mv[:, :, 1], 1e-5, None, ALU.add).then_inc(stable, 1)
            dve.wait_ge(rooted, 1)
            dve.reciprocal(inv[:, :], std[:, :]).then_inc(inverted, 1)
            dve.wait_ge(inverted, 1)
            for t in range(QT):
                dve.tensor_scalar(x_n[:, t], x_in[:, t], mv[:, t, 0:1], inv[:, t:t + 1], ALU.subtract, ALU.mult)\
                    .then_inc(scaled, 1)
            for n in range(0, QT // 2, 2):
                copy_out(n, dve.tensor_copy, dve)

        @block.scalar
        def _(act):
            act.wait_ge(stable, 1)
            act.activation(std[:, :], var[:, :], ACT.Sqrt).then_inc(rooted, 1)
            for n in range(1, QT // 2, 2):
                copy_out(n, lambda o, i: act.activation(o, i, ACT.Copy), act)

        @block.tensor
        def _(pe):
            for n in range(QT // 2):
                if n >= 4:
                    pe.wait_ge(copied[n % 2], (n - 4) // 2 + 1)
                for t in (2 * n, 2 * n + 1):
                    pe.wait_ge(scaled, t + 1)
                    for b in range(DB):
                        last = pe.transpose(bank[n % 4][:, ((t % 2) * DB + b) * P:((t % 2) * DB + b + 1) * P],
                                            x_n[:, t, b * P:(b + 1) * P], const["ident"][:, :])
                last.then_inc(turned, 1)


def project_queries(nc, const, scratch, l, x_nt):
    with ExitStack() as ctx:
        sc = Scope(nc, ctx, f"q{l}")
        full = sc.sb("full", [P, DB, T], F32)
        rest = sc.sb("rest", [P, DB, T], F32)
        part = sc.sb("part", [P, PART, DB, T], BF16)
        bank = [sc.ps(f"bank{n}", [P, CH], F32) for n in range(4)]
        ready, added, split, stored = sc.sem("ready"), sc.sem("added"), sc.sem("split"), sc.sem("stored")
        block = ctx.enter_context(nc.Block())
        tiles = [(b, c) for b in range(DB) for c in range(NC)]
        scale = float(DK) ** -0.5

        @block.tensor
        def _(pe):
            for n, (b, c) in enumerate(tiles):
                if n >= 4:
                    pe.wait_ge(added, n - 3)
                for db in range(DB):
                    last = pe.matmul(bank[n % 4][:, :], const["wq_t"][:, l, db, b * P:(b + 1) * P],
                                     x_nt[:, db, c * CH:(c + 1) * CH], start=(db == 0), stop=(db == DB - 1))
                last.then_inc(ready, 1)

        @block.vector
        def _(dve):
            for n, (b, c) in enumerate(tiles):
                dve.wait_ge(ready, n + 1)
                dve.tensor_scalar(full[:, b, c * CH:(c + 1) * CH], bank[n % 4][:, :],
                                  const["bqk"][:, 2 * l * DB + b:2 * l * DB + b + 1], scale, ALU.add, ALU.mult)\
                    .then_inc(added, 1)
            for b in range(DB):
                dve.wait_ge(added, NC * (b + 1))
                split_parts(dve, full[:, b], rest[:, b], [part[:, n, b] for n in range(PART)], split, 5 * b)

        @block.sync
        def _(sp):
            for b in range(DB):
                for n in range(PART):
                    sp.wait_ge(split, 5 * b + (1, 3, 5)[n])
                    sp.dma_start(scratch["q"][n, b * P:(b + 1) * P, :], part[:, n, b]).then_inc(stored, 16)
            sp.wait_ge(stored, 16 * DB * PART)


def attend(nc, const, scratch, l, attn, row_max, mask_q=None, mask_k=None):
    masked = mask_q is not None
    with ExitStack() as ctx:
        sc = Scope(nc, ctx, f"attend{l}")
        k_st = sc.sb("k_st", [AUG, RING, S], BF16)
        q_st = sc.sb("q_st", [AUG, RING, T], BF16)
        values = sc.sb("values", [P, KT, D], F32)
        v_st = sc.sb("v_st", [P, RING, KT, VW], F32)
        probs = sc.sb("probs", [P, RING, T], F32)
        piece_max = sc.sb("piece_max", [P, RING, QT, NP], F32)
        junk = sc.sb("junk", [P, 2, 401], BF16)
        m_rest = sc.sb("m_rest", [QT, P], F32)
        m_part = sc.sb("m_part", [QT, RING, PART, P], BF16)
        o_sb = sc.sb("o_sb", [P, CH], F32)
        inv_sum = sc.sb("inv_sum", [P, NC, NC], F32)
        s_bank = [sc.ps(f"s_bank{n}", [P, HALF], F32) for n in range(2)]
        p_bank = [sc.ps(f"p_bank{n}", [P, CH], F32) for n in range(2)]
        o_bank = sc.ps("o_bank", [P, CH], F32)
        t_bank = sc.ps("t_bank", [P, CH], F32)

        stack_in = [sc.sem(f"stack_in{n}") for n in range(RING)]
        values_in = sc.sem("values_in")
        tail_zero = sc.sem("tail_zero")
        fixed = sc.sem("fixed")
        v_ready = sc.sem("v_ready")
        piece_ready = sc.sem("piece_ready")
        piece_done = sc.sem("piece_done")
        max_ready = sc.sem("max_ready")
        max_turned = sc.sem("max_turned")
        max_split = sc.sem("max_split")
        max_in = sc.sem("max_in")
        score_ready = sc.sem("score_ready")
        exp_done = sc.sem("exp_done")
        pv_done = sc.sem("pv_done")
        o_copied = sc.sem("o_copied")
        o_turned = sc.sem("o_turned")
        normed = sc.sem("normed")
        block = ctx.enter_context(nc.Block())

        LOADS = 9
        GROUPS_K = [(0, 3), (3, 2), (5, 1)]
        GROUPS_Q = [(0, 0), (1, 0), (2, 0), (3, 1), (4, 1), (5, 2)]
        PER = QT * NP
        cuts = [PER * s // KT for s in range(KT + 1)]

        def iterations(eng, body):
            def once(i):
                body(i, i % RING, i < H, i >= 2, 1 <= i <= H)
            for i in range(4):
                once(i)
            with eng.Fori(4, H - RING + 1, RING) as j:
                for u in range(RING):
                    body(j + u, (4 + u) % RING, True, True, True)
            for i in range(H, H + 2):
                once(i)

        def score_step(i, slot, s, tail, fresh):
            if s < LATE:
                return (i - 2, (slot - 2) % RING, KT - LATE + s) if tail else None
            return (i - 1, (slot - 1) % RING, s - LATE) if fresh and s < KT else None

        def pv_step(i, slot, s, tail, fresh):
            if s <= LATE:
                return (i - 2, (slot - 2) % RING, KT - LATE + s - 1) if tail else None
            return (i - 1, (slot - 1) % RING, s - 1 - LATE) if fresh else None

        @block.sync
        def _(sp):
            def load(h, slot):
                ch = bass.ds(h * DK, DK)
                for g, n in GROUPS_K:
                    sp.dma_start(k_st[g * DK:(g + n) * DK, slot], scratch["k"][l, 0:n, ch, :]).then_inc(stack_in[slot], 16)
                for g, n in GROUPS_Q:
                    sp.dma_start(q_st[g * DK:(g + 1) * DK, slot], scratch["q"][n, ch, :]).then_inc(stack_in[slot], 16)

            load(0, 0)
            sp.dma_start(values[:, 0:KT - 1], scratch["v"][l, 0:(KT - 1) * P, :].rearrange("(t p) d -> p t d", p=P))\
                .then_inc(values_in, 16)
            sp.wait_ge(tail_zero, 1)
            sp.dma_start(values[0:keys_of(KT - 1), KT - 1], scratch["v"][l, (KT - 1) * P:S, :]).then_inc(values_in, 16)

            def body(i, slot, mx, tail, fresh):
                if fresh:
                    wait(sp, max_split, i * 4)
                    prev = (slot - 1) % RING
                    for n in range(PART):
                        sp.dma_start(q_st[ROWS + n:ROWS + n + 1, prev].rearrange("a (t q) -> a t q", q=P),
                                     m_part[:, prev, n, :]).then_inc(max_in, 16)
                if not isinstance(i, int) or i + 1 < H:
                    if tail:
                        wait(sp, score_ready, (i - 1) * (2 * KT), apart=True)
                    load(i + 1, (slot + 1) % RING)

            def loop_body(i, slot, mx, tail, fresh):
                body(i, slot, mx, tail, fresh)

            for i in range(4):
                body(i, i % RING, True, i >= 2, i >= 1)
            with sp.Fori(4, H - RING, RING) as j:
                for u in range(RING):
                    body(j + u, (4 + u) % RING, True, True, True)
            for i in range(H - RING, H + 1):
                body(i, i % RING, True, True, True)

        @block.gpsimd
        def _(pool):
            pool.memset(values[:, KT - 1], 0.0).then_inc(tail_zero, 1)
            pool.wait_ge(tail_zero, 1)
            pool.memset(k_st[ROWS:AUG, :, :], 1.0).then_inc(fixed, 1)
            pool.wait_ge(fixed, 1)
            pool.memset(v_st[:, :, :, DK:DK + 1], 1.0).then_inc(fixed, 1)
            pool.memset(v_st[:, :, :, DK + 1:VW], 0.0).then_inc(fixed, 1)
            pool.wait_ge(values_in, 32)
            pool.wait_ge(tail_zero, 1)

            def body(i, slot, mx, tail, fresh):
                if mx:
                    if not isinstance(i, int) or i >= RING:
                        wait(pool, pv_done, (i - 2) * KT, apart=True)
                    pool.tensor_copy(v_st[:, slot, :, 0:DK], values[:, :, bass.ds(i * DK, DK)]).then_inc(v_ready, 1)

            iterations(pool, body)

        @block.tensor
        def _(pe):
            pe.wait_ge(fixed, 3)

            def piece(i, slot, n):
                t, c = divmod(n, NP)
                k0, kn = PIECES[c]
                if not isinstance(i, int) or i * PER + n >= 2:
                    wait(pe, piece_done, i * PER + (n - 1))
                pe.matmul(p_bank[n % 2][:, 0:kn], q_st[0:ROWS, slot, t * P:(t + 1) * P], k_st[0:ROWS, slot, k0:k0 + kn],
                          start=True, stop=True).then_inc(piece_ready, 1)

            def scores(h, hs, kt, half):
                kn = keys_of(kt)
                if not isinstance(h, int) or 2 * (KT * h + kt) + half >= 2:
                    wait(pe, exp_done, h * (2 * KT) + (2 * kt + half - 1))
                for c in range(2):
                    q0 = half * HALF + c * CH
                    out = s_bank[half][0:kn, c * CH:(c + 1) * CH]
                    last = pe.matmul(out, k_st[:, hs, kt * P:kt * P + kn], q_st[:, hs, q0:q0 + CH],
                                     start=True, stop=not masked)
                    if masked:
                        last = pe.matmul(out, const["ident_bf"][0:kn, 0:kn], mask_k[0:kn, kt, q0:q0 + CH],
                                         start=False, stop=True)
                last.then_inc(score_ready, 1)

            def times_values(h, hs, kt):
                kn = keys_of(kt)
                if kt == 0:
                    wait(pe, v_ready, h + 1)
                    if not isinstance(h, int) or h >= 1:
                        wait(pe, o_copied, h)
                wait(pe, exp_done, h * (2 * KT) + (2 * kt + 2))
                for c in range(NC):
                    last = pe.matmul(o_bank[c * VW:(c + 1) * VW, :], v_st[0:kn, hs, kt, :],
                                     probs[0:kn, (kt + hs) % RING, c * CH:(c + 1) * CH],
                                     start=(kt == 0), stop=(kt == KT - 1), tile_position=(0, c * VW))
                last.then_inc(pv_done, 1)

            def body(i, slot, mx, tail, fresh):
                if mx:
                    wait(pe, stack_in[slot], (i - slot) * (16 * LOADS // RING) + 16 * LOADS)
                for s in range(KT):
                    now, before = score_step(i, slot, s, tail, fresh), pv_step(i, slot, s, tail, fresh)
                    todo = list(range(cuts[s], cuts[s + 1])) if mx else []
                    if now and now[2] == 0:
                        wait(pe, max_in, i * (16 * PART))
                    if now:
                        scores(*now, 0)
                    for n in todo[0:2]:
                        piece(i, slot, n)
                    if now:
                        scores(*now, 1)
                    for n in todo[2:3]:
                        piece(i, slot, n)
                    if before:
                        times_values(*before)
                    for n in todo[3:]:
                        piece(i, slot, n)
                    if s == 1 and fresh:
                        wait(pe, max_ready, i)
                        if not isinstance(i, int) or i >= 3:
                            wait(pe, normed, (i - 2) * 2)
                        else:
                            wait(pe, max_split, (i - 1) * 4)
                        pe.transpose(t_bank[0:QT, 0:P], row_max[:, (slot - 1) % RING, :], const["ident"][:, :])\
                            .then_inc(max_turned, 1)
                    if s == LATE + 2 and tail:
                        wait(pe, o_copied, i - 1)
                        if fresh:
                            wait(pe, max_split, i * 4)
                        else:
                            wait(pe, normed, (i - 2) * 2)
                        for b in range(NC):
                            last = pe.transpose(t_bank[:, b * P:(b + 1) * P], o_sb[:, b * P:(b + 1) * P],
                                                const["ident"][:, :])
                        last.then_inc(o_turned, 1)

            iterations(pe, body)

        @block.scalar
        def _(act):
            def body(i, slot, mx, tail, fresh):
                for s in range(KT):
                    now = score_step(i, slot, s, tail, fresh)
                    if now:
                        h, hs, kt = now
                        kn = keys_of(kt)
                        if not isinstance(h, int) or KT * h + kt >= RING:
                            wait(act, pv_done, h * KT + (kt - 2))
                        for half in range(2):
                            wait(act, score_ready, h * (2 * KT) + (2 * kt + half + 1))
                            act.activation(probs[0:kn, (kt + hs) % RING, half * HALF:(half + 1) * HALF],
                                           s_bank[half][0:kn, :], ACT.Exp).then_inc(exp_done, 1)
                    if s == LATE + 1 and tail:
                        wait(act, pv_done, (i - 1) * KT)
                        if not isinstance(i, int) or i >= 3:
                            wait(act, o_turned, i - 2)
                        act.activation(o_sb[:, :], o_bank[:, :], ACT.Copy).then_inc(o_copied, 1)

            iterations(act, body)

        @block.vector
        def _(dve):
            def piece(i, slot, n):
                t, c = divmod(n, NP)
                k0, kn = PIECES[c]
                dst = piece_max[:, slot, t, c:c + 1]
                wait(dve, piece_ready, i * PER + (n + 1), apart=masked)
                if masked:
                    dve.tensor_tensor_reduce(junk[:, n % 2, 0:kn], p_bank[n % 2][:, 0:kn], mask_q[:, t, k0:k0 + kn],
                                             1.0, -3.0e38, ALU.add, ALU.max, dst).then_inc(piece_done, 1)
                else:
                    dve.tensor_reduce(dst, p_bank[n % 2][:, 0:kn], AX.X, ALU.max).then_inc(piece_done, 1)

            def split_max(i, prev):
                wait(dve, max_turned, i)
                turned = t_bank[0:QT, 0:P]
                dve.tensor_scalar(m_part[:, prev, 0], turned, -1.0, None, ALU.mult).then_inc(max_split, 1)
                wait(dve, max_split, (i - 1) * 4 + 1)
                dve.scalar_tensor_tensor(out=m_rest[:, :], in0=turned, scalar=-1.0, in1=m_part[:, prev, 0],
                                         op0=ALU.mult, op1=ALU.subtract).then_inc(max_split, 1)
                wait(dve, max_split, (i - 1) * 4 + 2)
                dve.tensor_copy(m_part[:, prev, 1], m_rest[:, :]).then_inc(max_split, 1)
                wait(dve, max_split, (i - 1) * 4 + 3)
                dve.tensor_tensor(m_part[:, prev, 2], m_rest[:, :], m_part[:, prev, 1], ALU.subtract)\
                    .then_inc(max_split, 1)

            def norm(i):
                wait(dve, o_turned, i - 1)
                sums = t_bank[:, :].rearrange("p (b c v) -> p b c v", b=NC, v=VW)
                dve.reciprocal(inv_sum[:, :, :], sums[:, :, :, DK]).then_inc(normed, 1)
                wait(dve, normed, (i - 2) * 2 + 1, apart=True)
                out = attn[:, :, bass.ds((i - 2) * DK, DK)].rearrange("p (c b) d -> p b c d", b=NC)
                dve.tensor_tensor(out, sums[:, :, :, 0:DK], inv_sum[:, :, :].unsqueeze(3).to_broadcast([P, NC, NC, DK]),
                                  ALU.mult).then_inc(normed, 1)

            def body(i, slot, mx, tail, fresh):
                for s in range(KT):
                    if mx:
                        for n in range(cuts[s], cuts[s + 1]):
                            piece(i, slot, n)
                    if s == 1 and fresh:
                        split_max(i, (slot - 1) % RING)
                    if s == LATE + 2 and tail:
                        norm(i)
                if mx:
                    wait(dve, piece_done, i * PER + PER)
                    dve.tensor_reduce(row_max[:, slot, :], piece_max[:, slot], AX.X, ALU.max).then_inc(max_ready, 1)

            iterations(dve, body)


def project_out(nc, const, l, attn, row_max, x_src, x_dst):
    with ExitStack() as ctx:
        sc = Scope(nc, ctx, f"out{l}")
        x_in = sc.sb("x_in", [P, QT, D], F32)
        a_t = sc.sb("a_t", [P, DB, T], F32)
        biased = sc.sb("biased", [P, 2, D], F32)
        x_out = sc.sb("x_out", [P, QT, D], F32)
        lost = sc.sb("lost", [P, 3, QT], F32)
        t_bank = [sc.ps(f"t_bank{n}", [P, CH], F32) for n in range(4)]
        y_bank = [sc.ps(f"y_bank{n}", [P, D], F32) for n in range(4)]
        landed, marked, turned = sc.sem("landed"), sc.sem("marked"), sc.sem("turned")
        copied = sc.sem("copied")
        ready, with_bias, added, stored = sc.sem("ready"), sc.sem("with_bias"), sc.sem("added"), sc.sem("stored")
        block = ctx.enter_context(nc.Block())
        last_head = (H - 1) % RING

        @block.sync
        def _(sp):
            sp.dma_start(x_in[:, :, :], x_src.rearrange("(t p) d -> p t d", p=P)).then_inc(landed, 16)
            for n in range(4):
                sp.wait_ge(added, 4 * (n + 1))
                sp.dma_start(x_dst.rearrange("(t p) d -> p t d", p=P)[:, 4 * n:4 * n + 4],
                             x_out[:, 4 * n:4 * n + 4]).then_inc(stored, 16)
            sp.wait_ge(stored, 64)

        @block.tensor
        def _(pe):
            def turn(n):
                if n >= 4:
                    pe.wait_ge(copied, n - 3)
                for t in (2 * n, 2 * n + 1):
                    for b in range(DB):
                        last = pe.transpose(t_bank[n % 4][:, ((t % 2) * DB + b) * P:((t % 2) * DB + b + 1) * P],
                                            attn[:, t, b * P:(b + 1) * P], const["ident"][:, :])
                last.then_inc(turned, 1)

            turn(0)
            for n in range(QT // 2):
                if n + 1 < QT // 2:
                    turn(n + 1)
                pe.wait_ge(copied, n + 1)
                for t in (2 * n, 2 * n + 1):
                    if t >= 4:
                        pe.wait_ge(with_bias, t - 3)
                    for b in range(DB):
                        last = pe.matmul(y_bank[t % 4][:, :], a_t[:, b, t * P:(t + 1) * P], const["wo_t"][:, l, b],
                                         start=(b == 0), stop=(b == DB - 1))
                    last.then_inc(ready, 1)

        @block.scalar
        def _(act):
            for n in range(QT // 2):
                act.wait_ge(turned, n + 1)
                act.activation(a_t[:, :, 2 * n * P:2 * (n + 1) * P].rearrange("p b (t q) -> p t b q", t=2),
                               t_bank[n % 4][:, :].rearrange("p (t b q) -> p t b q", t=2, b=DB), ACT.Copy)\
                    .then_inc(copied, 1)

        @block.vector
        def _(dve):
            if l == 0:
                dve.tensor_scalar(lost[:, 0], row_max[:, last_head], NEG / 2, 3.0e38, ALU.is_lt, ALU.mult)\
                    .then_inc(marked, 1)
                dve.wait_ge(marked, 1)
                dve.tensor_scalar(lost[:, 1], lost[:, 0], 3.0e38, None, ALU.mult).then_inc(marked, 1)
                dve.wait_ge(marked, 2)
                dve.tensor_tensor(lost[:, 2], lost[:, 1], lost[:, 1], ALU.subtract).then_inc(marked, 1)
            else:
                dve.memset(lost[:, 2], 0.0).then_inc(marked, 3)
            dve.wait_ge(marked, 3)
            dve.wait_ge(landed, 16)
            for t in range(QT):
                dve.wait_ge(ready, t + 1)
                dve.scalar_tensor_tensor(out=biased[:, t % 2], in0=y_bank[t % 4][:, :], scalar=lost[:, 2, t:t + 1],
                                         in1=const["bo"][:, l], op0=ALU.add, op1=ALU.add).then_inc(with_bias, 1)
                dve.wait_ge(with_bias, t + 1)
                dve.scalar_tensor_tensor(out=x_out[:, t], in0=biased[:, t % 2], scalar=const["gates"][:, l:l + 1],
                                         in1=x_in[:, t], op0=ALU.mult, op1=ALU.add).then_inc(added, 1)


def experts(nc, io, const, l, x_nt, x_src, x_dst):
    F, FW = (1024, 128) if l == 0 else (192, 96)
    FT = F // FW
    pre = f"L{l}_ffn_"
    up = [("w1s", "W1"), ("w2s", "W2")] if l == 0 else [("Wg_s", "Wg"), ("Wu_s", "Wu")]
    down = ("w3s", "W3") if l == 0 else ("Wd_s", "Wd")
    router = "Wg" if l == 0 else "W_gate_router"
    func = ACT.Gelu if l == 0 else ACT.Silu
    with ExitStack() as ctx:
        sc = Scope(nc, ctx, f"ffn{l}")
        w_up = sc.sb("w_up", [P, 2, 2, DB, F], F32)
        w_dn = sc.sb("w_dn", [FW, 2, FT, D], F32)
        w_rt = sc.sb("w_rt", [P, DB, E], F32)
        bias = sc.sb("bias", [P, E], F32)
        scores = sc.sb("scores", [P, QT, E], F32)
        tmp = sc.sb("tmp", [P, 6, QT, E], F32)
        best = sc.sb("best", [P, 4, QT], F32)
        coef = sc.sb("coef", [P, QT, E + 1], F32)
        gate_e = sc.sb("gate_e", [P, 2, QT], F32)
        g_act = sc.sb("g_act", [FW, 2, CH], F32)
        hid = sc.sb("hid", [FW, 2, FT, CH], F32)
        acc = sc.sb("acc", [P, QT, D], F32)
        x_in = sc.sb("x_in", [P, QT, D], F32)
        a_bank = [sc.ps(f"a_bank{n}", [P, CH], F32) for n in range(2)]
        b_bank = [sc.ps(f"b_bank{n}", [P, CH], F32) for n in range(2)]
        y_bank = [sc.ps(f"y_bank{n}", [P, D], F32) for n in range(2)]
        r_bank = sc.ps("r_bank", [P, QT, E], F32)
        router_in, x_landed, zeroed = sc.sem("router_in"), sc.sem("x_landed"), sc.sem("zeroed")
        w_in = [sc.sem("w_in0"), sc.sem("w_in1")]
        logits_ready, logits_act, picked = sc.sem("logits_ready"), sc.sem("logits_act"), sc.sem("picked")
        gate_ready = sc.sem("gate_ready")
        up_ready, activated, hid_ready = sc.sem("up_ready"), sc.sem("activated"), sc.sem("hid_ready")
        y_ready, y_added, final, stored = sc.sem("y_ready"), sc.sem("y_added"), sc.sem("final"), sc.sem("stored")
        block = ctx.enter_context(nc.Block())
        PF, PY = NC * FT, NC * 4
        LOADS = 3

        def turns(eng, body):
            body(0, 0)
            with eng.Fori(0, E - 1, 2) as j:
                for u in range(2):
                    body(j + (u + 1), (u + 1) % 2)

        @block.sync
        def _(sp):
            sp.dma_start(w_rt[:, :, :], io[pre + router].rearrange("(b p) e -> p b e", p=P)).then_inc(router_in, 16)
            if l == 1:
                sp.dma_start(bias[:, :], io[pre + "expert_bias"].rearrange("(a n) -> a n", a=1).broadcast_to([P, E]))\
                    .then_inc(router_in, 16)
            sp.dma_start(x_in[:, :, :], x_src.rearrange("(t p) d -> p t d", p=P)).then_inc(x_landed, 16)

            def load(turn, slot):
                def src(names):
                    if isinstance(turn, int) and turn == 0:
                        return io[pre + names[0]]
                    return io[pre + names[1]][bass.ds(turn - 1, 1)].rearrange("a k n -> (a k) n")
                for n in range(2):
                    sp.dma_start(w_up[:, slot, n], src(up[n]).rearrange("(b p) f -> p b f", p=P)).then_inc(w_in[slot], 16)
                sp.dma_start(w_dn[:, slot], src(down).rearrange("(b p) f -> p b f", p=FW)).then_inc(w_in[slot], 16)

            load(0, 0)
            load(1, 1)

            def body(turn, slot):
                wait(sp, y_ready, (turn - 1) * PY, apart=True)
                load(turn, slot)

            body(2, 0)
            with sp.Fori(2, E - 1, 2) as j:
                for u in range(2):
                    body(j + (u + 1), (u + 1) % 2)
            for n in range(4):
                sp.wait_ge(final, 4 * (n + 1))
                sp.dma_start(x_dst.rearrange("(t p) d -> p t d", p=P)[:, 4 * n:4 * n + 4],
                             acc[:, 4 * n:4 * n + 4]).then_inc(stored, 16)
            sp.wait_ge(stored, 64)

        @block.gpsimd
        def _(pool):
            pool.memset(acc[:, :, :], 0.0).then_inc(zeroed, 1)
            pool.memset(coef[:, :, 0:1], 1.0).then_inc(zeroed, 1)
            pool.wait_ge(zeroed, 2)
            pool.wait_ge(picked, 20)

            def body(turn, slot):
                if not isinstance(turn, int) or turn >= 2:
                    wait(pool, y_added, (turn - 1) * PY, apart=True)
                pool.tensor_copy(gate_e[:, slot].unsqueeze(2), coef[:, :, bass.ds(turn, 1)]).then_inc(gate_ready, 1)

            turns(pool, body)

        @block.tensor
        def _(pe):
            pe.wait_ge(router_in, 16 * (l + 1))
            for t in range(QT):
                for b in range(DB):
                    last = pe.matmul(r_bank[:, t], x_nt[:, b, t * P:(t + 1) * P], w_rt[:, b], start=(b == 0),
                                     stop=(b == DB - 1))
            last.then_inc(logits_ready, 1)

            def body(turn, slot):
                wait(pe, w_in[slot], ((turn - slot) // 2 + 1) * 16 * LOADS if isinstance(turn, int)
                     else (turn - slot) * (8 * LOADS) + 16 * LOADS)
                for c in range(NC):
                    for f in range(FT):
                        n = c * FT + f
                        for which, bank in ((0, a_bank), (1, b_bank)):
                            if not isinstance(turn, int) or turn * PF + n >= 2:
                                wait(pe, (activated, hid_ready)[which], turn * PF + (n - 1))
                            for b in range(DB):
                                last = pe.matmul(bank[n % 2][0:FW, :], w_up[:, slot, which, b, f * FW:(f + 1) * FW],
                                                 x_nt[:, b, c * CH:(c + 1) * CH], start=(b == 0), stop=(b == DB - 1))
                            last.then_inc(up_ready, 1)
                    for t in range(4):
                        n = c * 4 + t
                        wait(pe, hid_ready, turn * PF + FT * (c + 1))
                        if not isinstance(turn, int) or turn * PY + n >= 2:
                            wait(pe, y_added, turn * PY + (n - 1))
                        for f in range(FT):
                            last = pe.matmul(y_bank[n % 2][:, :], hid[:, c % 2, f, t * P:(t + 1) * P], w_dn[:, slot, f],
                                             start=(f == 0), stop=(f == FT - 1))
                        last.then_inc(y_ready, 1)

            turns(pe, body)

        @block.scalar
        def _(act):
            act.wait_ge(logits_ready, 1)
            act.activation(scores[:, :, :], r_bank[:, :, :], ACT.Copy if l == 0 else ACT.Sigmoid).then_inc(logits_act, 1)

            def body(turn, slot):
                for n in range(PF):
                    wait(act, up_ready, turn * (2 * PF) + (2 * n + 1))
                    if not isinstance(turn, int) or turn * PF + n >= 2:
                        wait(act, hid_ready, turn * PF + (n - 1))
                    act.activation(g_act[:, n % 2], a_bank[n % 2][0:FW, :], func).then_inc(activated, 1)

            turns(act, body)

        @block.vector
        def _(dve):
            step = [0]

            def then(ins):
                ins.then_inc(picked, 1)
                step[0] += 1
                dve.wait_ge(picked, step[0])

            eno = const["expert_no"][:, :, :]

            def first_best(vals, k):
                wide = [P, QT, E]
                then(dve.tensor_reduce(best[:, 0], vals, AX.X, ALU.max))
                then(dve.tensor_tensor(tmp[:, 5], vals, best[:, 0].unsqueeze(2).to_broadcast(wide), ALU.is_lt))
                then(dve.scalar_tensor_tensor(out=tmp[:, 5], in0=tmp[:, 5], scalar=float(2 * E), in1=eno,
                                              op0=ALU.mult, op1=ALU.add))
                then(dve.tensor_reduce(best[:, 1], tmp[:, 5], AX.X, ALU.min))
                then(dve.tensor_tensor(tmp[:, k], eno, best[:, 1].unsqueeze(2).to_broadcast(wide), ALU.is_equal))

            dve.wait_ge(logits_act, 1)
            if l == 0:
                first_best(scores[:, :, :], 0)
                then(dve.tensor_copy(coef[:, :, 1:E + 1], tmp[:, 0]))
            else:
                dve.wait_ge(router_in, 32)
                then(dve.tensor_tensor(tmp[:, 0], scores[:, :, :], bias[:, :].unsqueeze(1).to_broadcast([P, QT, E]),
                                       ALU.add))
                first_best(tmp[:, 0], 1)
                then(dve.scalar_tensor_tensor(out=tmp[:, 0], in0=tmp[:, 1], scalar=-1.0e30, in1=tmp[:, 0],
                                              op0=ALU.mult, op1=ALU.add))
                first_best(tmp[:, 0], 2)
                then(dve.tensor_tensor(tmp[:, 1], tmp[:, 1], tmp[:, 2], ALU.add))
                then(dve.tensor_tensor(tmp[:, 1], tmp[:, 1], scores[:, :, :], ALU.mult))
                then(dve.tensor_reduce(best[:, 2], tmp[:, 1], AX.X, ALU.add))
                then(dve.tensor_scalar(best[:, 2], best[:, 2], 1.0e-20, None, ALU.add))
                then(dve.reciprocal(best[:, 3], best[:, 2]))
                then(dve.tensor_tensor(coef[:, :, 1:E + 1], tmp[:, 1],
                                       best[:, 3].unsqueeze(2).to_broadcast([P, QT, E]), ALU.mult))
            while step[0] < 20:
                then(dve.tensor_copy(best[:, 2], best[:, 0]))
            dve.wait_ge(zeroed, 2)

            def body(turn, slot):
                wait(dve, gate_ready, turn + 1)
                for c in range(NC):
                    for f in range(FT):
                        n = c * FT + f
                        wait(dve, activated, turn * PF + (n + 1))
                        wait(dve, up_ready, turn * (2 * PF) + (2 * n + 2))
                        if f == 0 and (not isinstance(turn, int) or turn * NC + c >= 2):
                            wait(dve, y_ready, turn * PY + 4 * (c - 1))
                        dve.tensor_tensor(hid[:, c % 2, f], b_bank[n % 2][0:FW, :], g_act[:, n % 2], ALU.mult)\
                            .then_inc(hid_ready, 1)
                    for t in range(4):
                        n = c * 4 + t
                        wait(dve, y_ready, turn * PY + (n + 1))
                        if not isinstance(turn, int) or turn >= 1:
                            wait(dve, y_added, turn * PY + (n - PY + 1))
                        dve.scalar_tensor_tensor(out=acc[:, n], in0=y_bank[n % 2][:, :], scalar=gate_e[:, slot, n:n + 1],
                                                 in1=acc[:, n], op0=ALU.mult, op1=ALU.add).then_inc(y_added, 1)

            turns(dve, body)
            dve.wait_ge(x_landed, 16)
            for t in range(QT):
                dve.wait_ge(y_added, E * PY + t + 1)
                dve.scalar_tensor_tensor(out=acc[:, t], in0=acc[:, t], scalar=const["gates"][:, 2 + l:3 + l],
                                         in1=x_in[:, t], op0=ALU.mult, op1=ALU.add).then_inc(final, 1)


def flamingo_kernel(nc, io, out):
    Scope.used.clear()
    scratch = {
        "k": nc.dram_tensor("k_parts", [2, PART, D, S], BF16, kind="Internal").ap(),
        "q": nc.dram_tensor("q_parts", [PART, D, T], BF16, kind="Internal").ap(),
        "v": nc.dram_tensor("v_rows", [2, S, D], F32, kind="Internal").ap(),
    }
    x_mid = [nc.dram_tensor(f"x_mid{n}", [T, D], F32, kind="Internal").ap() for n in range(3)]
    x_of = [io["x"][0]] + x_mid + [out[0]]
    with ExitStack() as ctx:
        sc = Scope(nc, ctx, "keep")
        const = {
            "ident": sc.sb("ident", [P, P], F32), "ident_bf": sc.sb("ident_bf", [P, P], BF16),
            "expert_no": sc.sb("expert_no", [P, QT, E], F32),
            "gates": sc.sb("gates", [P, 4], F32),
            "wq_t": sc.sb("wq_t", [P, 2, DB, D], F32), "wo_t": sc.sb("wo_t", [P, 2, DB, D], F32),
            "bqk": sc.sb("bqk", [P, 4 * DB], F32),
            "bo": sc.sb("bo", [P, 2, D], F32),
        }
        make_constants(nc, io, const)
        prepare_context(nc, io, const, scratch)
        for l in range(2):
            if l:
                clear_semaphores(nc)
            with ExitStack() as part:
                x_nt = Scope(nc, part, f"keep_q{l}").sb("x_nt", [P, DB, T], F32)
                normalise(nc, const, f"norm_q{l}", x_of[2 * l], x_nt)
                project_queries(nc, const, scratch, l, x_nt)
            with ExitStack() as part:
                sp = Scope(nc, part, f"keep_a{l}")
                attn = sp.sb("attn", [P, QT, D], F32)
                row_max = sp.sb("row_max", [P, RING, QT], F32)
                with ExitStack() as masks:
                    mask_q = mask_k = None
                    if l == 0:
                        sm = Scope(nc, masks, "keep_mask")
                        mask_q = sm.sb("mask_q", [P, QT, S], BF16)
                        mask_k = sm.sb("mask_k", [P, KT, T], BF16)
                        prepare_mask(nc, io, const, mask_q, mask_k)
                    attend(nc, const, scratch, l, attn, row_max, mask_q, mask_k)
                project_out(nc, const, l, attn, row_max, x_of[2 * l], x_of[2 * l + 1])
            with ExitStack() as part:
                x_nt = Scope(nc, part, f"keep_f{l}").sb("x_nt", [P, DB, T], F32)
                normalise(nc, const, f"norm_f{l}", x_of[2 * l + 1], x_nt)
                experts(nc, io, const, l, x_nt, x_of[2 * l + 1], x_of[2 * l + 2])


_INS = (["x", "ctx_1024", "mask_BxSxS2_ik0", "g_xattn", "g_ffn"]
        + [f"L{l}_xattn_{k}{w}" for l in range(2) for w in "qkvo" for k in "wb"]
        + [f"L0_ffn_{n}" for n in ("w1s", "w2s", "w3s", "W1", "W2", "W3", "Wg")]
        + [f"L1_ffn_{n}" for n in ("W_gate_router", "expert_bias", "Wg", "Wu", "Wd", "Wg_s", "Wu_s", "Wd_s")])
_OUTS = [((1, T, D), "float32")]


def kernel(**inputs):
    import numpy as _np
    import concourse.bacc as _bacc
    from concourse import mybir as _mybir
    from concourse.bass_utils import run_bass_kernel_spmd as _run

    nc = _bacc.Bacc("TRN2", target_bir_lowering=False, num_devices=1)
    arrays, io = {}, {}
    for name in _INS:
        a = _np.ascontiguousarray(inputs[name])
        arrays[f"in_{name}_dram"] = a
        io[name] = nc.dram_tensor(f"in_{name}_dram", a.shape, _mybir.dt.from_np(a.dtype), kind="ExternalInput").ap()
    (shape, dtype), = _OUTS
    out = nc.dram_tensor("out_0_dram", shape, _mybir.dt.from_np(_np.dtype(dtype)), kind="ExternalOutput").ap()
    flamingo_kernel(nc, io, out)
    r = _run(nc, [arrays], core_ids=[0])
    return r.results[0]["out_0_dram"]
```

```python
from contextlib import ExitStack

import concourse.bass as bass
from concourse import mybir

F32 = mybir.dt.float32
BF16 = mybir.dt.bfloat16
I32 = mybir.dt.int32
ALU = mybir.AluOpType
ACT = mybir.ActivationFunctionType
AX = mybir.AxisListType

P = 128
T = 2048
D = 256
S = 1601
H = 16
DK = D // H
DB = D // P
QT = T // P
KT = -(-S // P)
CH = 512
NC = T // CH
HALF = 1024
PART = 3
ROWS = 6 * DK
AUG = ROWS + PART
PIECES = [(0, 401), (401, 400), (801, 400), (1201, 400)]
NP = len(PIECES)
VW = 32
NEG = -1.0e30
LATE = 3
E = 8
RING = 3
assert sum(n for _, n in PIECES) == S


def keys_of(kt):
    return min(P, S - kt * P)


def wait(eng, sem, value, apart=False):
    if isinstance(value, int):
        if value > 0:
            eng.wait_ge(sem, value)
    else:
        eng.wait_ge(sem, value)
        if apart:
            eng.nop(nofuse=True)


class Scope:

    used = []

    def __init__(self, nc, ctx, stage):
        self.nc, self.ctx, self.stage = nc, ctx, stage

    def sb(self, name, shape, dt):
        return self.ctx.enter_context(self.nc.sbuf_tensor(f"{self.stage}_{name}", shape, dt))

    def ps(self, name, shape, dt):
        return self.ctx.enter_context(self.nc.psum_tensor(f"{self.stage}_{name}", shape, dt))

    def sem(self, name):
        made = self.ctx.enter_context(self.nc.semaphore(f"{self.stage}_{name}"))
        Scope.used.append(made.num)
        return made


def clear_semaphores(nc):
    numbers = sorted(set(Scope.used))
    Scope.used.clear()
    runs = []
    for n in numbers:
        if runs and runs[-1][1] == n:
            runs[-1][1] = n + 1
        else:
            runs.append([n, n + 1])
    with nc.Block() as block:
        @block.gpsimd
        def _(pool):
            for first, end in runs:
                pool.sem_clear(range(first, end))


def make_constants(nc, io, const):
    with ExitStack() as ctx:
        sc = Scope(nc, ctx, "const")
        filled, made, gates_in, gated = sc.sem("filled"), sc.sem("made"), sc.sem("gates_in"), sc.sem("gated")
        raw = sc.sb("raw_gates", [P, 4], F32)
        block = ctx.enter_context(nc.Block())

        @block.gpsimd
        def _(pool):
            pool.memset(const["ident"][:, :], 0.0).then_inc(filled, 1)
            pool.memset(const["ident_bf"][:, :], 0.0).then_inc(filled, 1)
            for n, m in enumerate((const["ident"], const["ident_bf"])):
                pool.wait_ge(filled, n + 1)
                pool.affine_select(out=m[:, :], in_=m[:, :], compare_op=ALU.not_equal, fill=1.0, base=0,
                                   pattern=[[-1, P]], channel_multiplier=1).then_inc(made, 1)
            pool.memset(const["ones"][:, :], 1.0).then_inc(filled, 1)
            pool.memset(const["earlier"][:, :], 1.0).then_inc(filled, 1)
            pool.wait_ge(filled, 4)
            pool.affine_select(out=const["earlier"][:, :], in_=const["earlier"][:, :], compare_op=ALU.is_gt, fill=0.0,
                               base=0, pattern=[[1, P]], channel_multiplier=-1).then_inc(made, 1)
            pool.wait_ge(made, 3)
            for n in range(const["number"].shape[1]):
                pool.memset(const["number"][:, n:n + 1], float(n)).then_inc(made, 1)

        @block.sync
        def _(sp):
            for n, g in enumerate(("g_xattn", "g_ffn")):
                sp.dma_start(raw[:, 2 * n:2 * n + 2],
                             io[g].rearrange("(a n) -> a n", a=1).broadcast_to([P, 2])).then_inc(gates_in, 16)

        @block.scalar
        def _(act):
            act.wait_ge(gates_in, 32)
            act.activation(const["gates"][:, :], raw[:, :], ACT.Tanh).then_inc(gated, 1)


def prepare_context(nc, io, const, scratch):
    with ExitStack() as ctx:
        sc = Scope(nc, ctx, "ctx")
        names = [f"L{l}_xattn_w{w}" for l in range(2) for w in "qkvo"]
        NW = len(names)
        ZR = 4
        zeros = sc.sb("zeros", [P, ZR, D], F32)
        w_nat = sc.sb("w_nat", [P, NW, DB, D], F32)
        b_nat = sc.sb("b_nat", [2 * DB * 2, P], F32)
        c_nat = sc.sb("c_nat", [P, KT, D], F32)
        c_t = sc.sb("c_t", [P, DB, S], F32)
        wk_t = sc.sb("wk_t", [P, 2, DB, D], F32)
        wv_t = sc.sb("wv_t", [P, DB, 2, D], F32)
        bv = sc.sb("bv", [P, 2, D], F32)
        k_full = sc.sb("k_full", [P, DB, S], F32)
        k_rest = sc.sb("k_rest", [P, DB, S], F32)
        k_part = sc.sb("k_part", [P, PART, DB, S], BF16)
        v_out = sc.sb("v_out", [P, KT, 2, D], F32)
        bank = [sc.ps(f"bank{n}", [P, CH], F32) for n in range(8)]
        w_in, b_in, c_in, bv_in = sc.sem("w_in"), sc.sem("b_in"), sc.sem("c_in"), sc.sem("bv_in")
        turned, copied = sc.sem("turned"), sc.sem("copied")
        c_turned, c_copied = sc.sem("c_turned"), sc.sem("c_copied")
        k_ready, k_copied = sc.sem("k_ready"), sc.sem("k_copied")
        v_ready, v_added = sc.sem("v_ready"), sc.sem("v_added")
        split, stored = sc.sem("split"), sc.sem("stored")
        zeroed, cleared = sc.sem("zeroed"), sc.sem("cleared")
        block = ctx.enter_context(nc.Block())
        KCH = PIECES

        @block.gpsimd
        def _(pool):
            pool.memset(zeros[:, :, :], 0.0).then_inc(zeroed, 1)

        @block.sync
        def _(sp):
            for n, name in enumerate(names):
                sp.dma_start(w_nat[:, n], io[name].rearrange("(b p) d -> p b d", p=P)).then_inc(w_in, 16)
            for n, name in enumerate(["L0_xattn_bq", "L0_xattn_bk", "L1_xattn_bq", "L1_xattn_bk"]):
                sp.dma_start(b_nat[DB * n:DB * n + DB, :], io[name].rearrange("(b p) -> b p", p=P)).then_inc(b_in, 16)
            sp.wait_ge(zeroed, 1)
            clears = 0
            for rows in scratch["sorted"]:
                tiles = rows.rearrange("(t p) d -> p t d", p=P)
                for t in range(0, tiles.shape[1], ZR):
                    n = min(ZR, tiles.shape[1] - t)
                    sp.dma_start(tiles[:, t:t + n], zeros[:, 0:n]).then_inc(cleared, 16)
                    clears += 1
            for l in range(2):
                for part in range(PART):
                    sp.wait_ge(split, 5 * l + (1, 3, 5)[part])
                    for b in range(DB):
                        sp.dma_start(scratch["k"][l, part, b * P:(b + 1) * P, :], k_part[:, part, b]).then_inc(stored, 16)
            sp.wait_ge(v_added, KT)
            for l in range(2):
                sp.dma_start(scratch["v"][l, 0:(KT - 1) * P, :].rearrange("(t p) d -> p t d", p=P),
                             v_out[:, 0:KT - 1, l]).then_inc(stored, 16)
                sp.dma_start(scratch["v"][l, (KT - 1) * P:S, :], v_out[0:keys_of(KT - 1), KT - 1, l]).then_inc(stored, 16)
            sp.wait_ge(stored, 16 * (2 * PART * DB + 4))
            sp.wait_ge(cleared, 16 * clears)

        def k_tiles():
            return [(l, b, c) for l in range(2) for b in range(DB) for c in range(len(KCH))]

        @block.tensor
        def _(pe):
            pe.wait_ge(w_in, 16 * NW)
            for n in range(NW):
                if n >= 2:
                    pe.wait_ge(copied, n - 1)
                for db in range(DB):
                    for eb in range(DB):
                        last = pe.transpose(bank[n % 2][:, db * D + eb * P:db * D + (eb + 1) * P],
                                            w_nat[:, n, eb, db * P:(db + 1) * P], const["ident"][:, :])
                last.then_inc(turned, 1)
            pe.wait_ge(b_in, 64)
            last = pe.transpose(bank[2][:, 0:4 * DB], b_nat[:, :], const["ident"][0:4 * DB, 0:4 * DB]).then_inc(turned, 1)
            pe.wait_ge(c_in, 32)
            for kt in range(KT):
                if kt >= 2:
                    pe.wait_ge(c_copied, kt - 1)
                kn = keys_of(kt)
                for db in range(DB):
                    last = pe.transpose(bank[4 + kt % 2][:, db * P:db * P + kn], c_nat[0:kn, kt, db * P:(db + 1) * P],
                                        const["ident"][0:kn, 0:kn])
                last.then_inc(c_turned, 1)
            pe.wait_ge(copied, NW + 1)
            pe.wait_ge(c_copied, KT)
            for n, (l, b, c) in enumerate(k_tiles()):
                if n >= 2:
                    pe.wait_ge(k_copied, n - 1)
                k0, kn = KCH[c]
                for db in range(DB):
                    last = pe.matmul(bank[n % 2][:, 0:kn], wk_t[:, l, db, b * P:(b + 1) * P], c_t[:, db, k0:k0 + kn],
                                     start=(db == 0), stop=(db == DB - 1))
                last.then_inc(k_ready, 1)
            for kt in range(KT):
                if kt >= 2:
                    pe.wait_ge(v_added, kt - 1)
                kn = keys_of(kt)
                for db in range(DB):
                    last = pe.matmul(bank[6 + kt % 2][0:kn, :], c_t[:, db, kt * P:kt * P + kn],
                                     wv_t[:, db].rearrange("p l d -> p (l d)"), start=(db == 0), stop=(db == DB - 1))
                last.then_inc(v_ready, 1)

        @block.scalar
        def _(act):
            act.dma_start(c_nat[:, 0:KT - 1], io["ctx_1024"][0, 0:(KT - 1) * P, :].rearrange("(t p) d -> p t d", p=P))\
                .then_inc(c_in, 16)
            act.dma_start(c_nat[0:keys_of(KT - 1), KT - 1], io["ctx_1024"][0, (KT - 1) * P:S, :]).then_inc(c_in, 16)
            for l in range(2):
                for dst, name in ((bv[:, l], f"L{l}_xattn_bv"), (const["bo"][:, l], f"L{l}_xattn_bo")):
                    act.dma_start(dst, io[name].rearrange("(a n) -> a n", a=1).broadcast_to([P, D])).then_inc(bv_in, 16)
            for n in range(NW):
                l, w = divmod(n, 4)
                dst = (const["wq_t"][:, l], wk_t[:, l], wv_t[:, :, l], const["wo_t"][:, l])[w]
                act.wait_ge(turned, n + 1)
                act.activation(dst, bank[n % 2][:, :].rearrange("p (b d) -> p b d", b=DB), ACT.Copy).then_inc(copied, 1)
            act.wait_ge(turned, NW + 1)
            act.activation(const["bqk"][:, :], bank[2][:, 0:4 * DB], ACT.Copy).then_inc(copied, 1)
            act.wait_ge(copied, NW + 1)
            for n, (l, b, c) in enumerate(k_tiles()):
                k0, kn = KCH[c]
                act.wait_ge(k_ready, n + 1)
                if c == 0 and b == 0 and l == 1:
                    act.wait_ge(split, 2)
                act.activation(k_full[:, b, k0:k0 + kn], bank[n % 2][:, 0:kn], ACT.Identity,
                               bias=const["bqk"][:, (2 * l + 1) * DB + b:(2 * l + 1) * DB + b + 1]).then_inc(k_copied, 1)

        @block.vector
        def _(dve):
            for kt in range(KT):
                kn = keys_of(kt)
                dve.wait_ge(c_turned, kt + 1)
                dve.tensor_copy(c_t[:, :, kt * P:kt * P + kn],
                                bank[4 + kt % 2][:, 0:DB * P].rearrange("p (b k) -> p b k", b=DB)[:, :, 0:kn])\
                    .then_inc(c_copied, 1)

            def split_keys(l):
                dve.wait_ge(k_copied, 2 * 4 * (l + 1))
                if l:
                    dve.wait_ge(stored, 16 * PART * DB)
                split_parts(dve, k_full[:, :, :], k_rest[:, :, :], [k_part[:, n] for n in range(PART)], split, 5 * l)

            split_keys(0)
            dve.wait_ge(bv_in, 64)
            split_keys(1)
            for kt in range(KT):
                kn = keys_of(kt)
                dve.wait_ge(v_ready, kt + 1)
                dve.tensor_tensor(v_out[0:kn, kt].rearrange("p l d -> p (l d)"), bank[6 + kt % 2][0:kn, :],
                                  bv[0:kn].rearrange("p l d -> p (l d)"), ALU.add).then_inc(v_added, 1)


def split_parts(dve, full, rest, parts, split, base):
    dve.tensor_copy(parts[0], full).then_inc(split, 1)
    dve.wait_ge(split, base + 1)
    dve.tensor_tensor(rest, full, parts[0], ALU.subtract).then_inc(split, 1)
    dve.wait_ge(split, base + 2)
    dve.tensor_copy(parts[1], rest).then_inc(split, 1)
    dve.wait_ge(split, base + 3)
    dve.tensor_tensor(rest, rest, parts[1], ALU.subtract).then_inc(split, 1)
    dve.wait_ge(split, base + 4)
    dve.tensor_copy(parts[2], rest).then_inc(split, 1)


def prepare_mask(nc, io, const, mask_q, mask_k):
    with ExitStack() as ctx:
        sc = Scope(nc, ctx, "mask")
        raw = sc.sb("raw", [P, 2, S], I32)
        FIRST = 8
        turn = [sc.ps(f"turn{n}", [P, 2 * FIRST * P], BF16) for n in range(2)]
        landed = [sc.sem("landed0"), sc.sem("landed1")]
        made, turned, copied = sc.sem("made"), sc.sem("turned"), sc.sem("copied")
        block = ctx.enter_context(nc.Block())
        kl = keys_of(KT - 1)

        @block.sync
        def _(sp):
            for t in range(QT):
                if t >= 2:
                    sp.wait_ge(made, t - 1)
                sp.dma_start(raw[:, t % 2], io["mask_BxSxS2_ik0"][0, t * P:(t + 1) * P, :]).then_inc(landed[t % 2], 16)

        @block.vector
        def _(dve):
            for t in range(QT):
                dve.wait_ge(landed[t % 2], 16 * (t // 2 + 1))
                dve.tensor_scalar(mask_q[:, t], raw[:, t % 2], 0.0, NEG, ALU.is_equal, ALU.mult).then_inc(made, 1)

        @block.tensor
        def _(pe):
            for t in range(QT):
                pe.wait_ge(made, t + 1)
                if t >= 2:
                    pe.wait_ge(copied, 3 * (t - 1))
                for kt in range(KT):
                    kn = keys_of(kt)
                    last = pe.transpose(turn[t % 2][0:kn, kt * P:(kt + 1) * P], mask_q[:, t, kt * P:kt * P + kn],
                                        const["ident_bf"][:, :])
                last.then_inc(turned, 1)

        @block.scalar
        def _(act):
            for t in range(QT):
                act.wait_ge(turned, t + 1)
                src = turn[t % 2][:, :].rearrange("p (k q) -> p k q", q=P)
                for p, a, b in ((P, 0, FIRST), (P, FIRST, KT - 1), (kl, KT - 1, KT)):
                    act.activation(mask_k[0:p, a:b, t * P:(t + 1) * P], src[0:p, a:b], ACT.Copy).then_inc(copied, 1)


def normalise(nc, const, stage, src, x_nt, x_n):
    with ExitStack() as ctx:
        sc = Scope(nc, ctx, stage)
        LD = 4
        x_in = sc.sb("x_in", [P, QT, D], F32)
        stats = sc.sb("stats", [P, QT, 6], F32)
        mv = sc.sb("mv", [P, QT, 2], F32)
        var = sc.sb("var", [P, QT], F32)
        std = sc.sb("std", [P, QT], F32)
        inv = sc.sb("inv", [P, QT], F32)
        bank = [sc.ps(f"bank{n}", [P, CH], F32) for n in range(4)]
        landed = [sc.sem(f"landed{n}") for n in range(LD)]
        counted, spread, stable, rooted, inverted = (sc.sem(n) for n in ("counted", "spread", "stable", "rooted", "inverted"))
        scaled, turned = sc.sem("scaled"), sc.sem("turned")
        copied = [sc.sem("copied_dve"), sc.sem("copied_act")]
        block = ctx.enter_context(nc.Block())
        x_tiles = src.rearrange("(t p) d -> p t d", p=P)
        per = QT // LD

        @block.sync
        def _(sp):
            for n in range(LD):
                sp.dma_start(x_in[:, n * per:(n + 1) * per], x_tiles[:, n * per:(n + 1) * per]).then_inc(landed[n], 16)

        def copy_out(n, copy, eng):
            eng.wait_ge(turned, n + 1)
            copy(x_nt[:, :, 2 * n * P:2 * (n + 1) * P].rearrange("p b (t q) -> p t b q", t=2),
                 bank[n % 4][:, :].rearrange("p (t b q) -> p t b q", t=2, b=DB)).then_inc(copied[n % 2], 1)

        @block.vector
        def _(dve):
            for t in range(QT):
                if t % per == 0:
                    dve.wait_ge(landed[t // per], 16)
                dve.bn_stats(stats[:, t], x_in[:, t]).then_inc(counted, 1)
            for t in range(QT):
                dve.wait_ge(counted, t + 1)
                dve.bn_aggr(mv[:, t], stats[:, t]).then_inc(spread, 1)
            dve.wait_ge(spread, QT)
            dve.tensor_scalar(var[:, :], mv[:, :, 1], 1e-5, None, ALU.add).then_inc(stable, 1)
            dve.wait_ge(rooted, 1)
            dve.reciprocal(inv[:, :], std[:, :]).then_inc(inverted, 1)
            dve.wait_ge(inverted, 1)
            for t in range(QT):
                dve.tensor_scalar(x_n[:, t], x_in[:, t], mv[:, t, 0:1], inv[:, t:t + 1], ALU.subtract, ALU.mult)\
                    .then_inc(scaled, 1)
            for n in range(0, QT // 2, 2):
                copy_out(n, dve.tensor_copy, dve)

        @block.scalar
        def _(act):
            act.wait_ge(stable, 1)
            act.activation(std[:, :], var[:, :], ACT.Sqrt).then_inc(rooted, 1)
            for n in range(1, QT // 2, 2):
                copy_out(n, lambda o, i: act.activation(o, i, ACT.Copy), act)

        @block.tensor
        def _(pe):
            for n in range(QT // 2):
                if n >= 4:
                    pe.wait_ge(copied[n % 2], (n - 4) // 2 + 1)
                for t in (2 * n, 2 * n + 1):
                    pe.wait_ge(scaled, t + 1)
                    for b in range(DB):
                        last = pe.transpose(bank[n % 4][:, ((t % 2) * DB + b) * P:((t % 2) * DB + b + 1) * P],
                                            x_n[:, t, b * P:(b + 1) * P], const["ident"][:, :])
                last.then_inc(turned, 1)


def project_queries(nc, const, scratch, l, x_nt):
    with ExitStack() as ctx:
        sc = Scope(nc, ctx, f"q{l}")
        full = sc.sb("full", [P, DB, T], F32)
        rest = sc.sb("rest", [P, DB, T], F32)
        part = sc.sb("part", [P, PART, DB, T], BF16)
        bank = [sc.ps(f"bank{n}", [P, CH], F32) for n in range(4)]
        ready, added, split, stored = sc.sem("ready"), sc.sem("added"), sc.sem("split"), sc.sem("stored")
        block = ctx.enter_context(nc.Block())
        tiles = [(b, c) for b in range(DB) for c in range(NC)]
        scale = float(DK) ** -0.5

        @block.tensor
        def _(pe):
            for n, (b, c) in enumerate(tiles):
                if n >= 4:
                    pe.wait_ge(added, n - 3)
                for db in range(DB):
                    last = pe.matmul(bank[n % 4][:, :], const["wq_t"][:, l, db, b * P:(b + 1) * P],
                                     x_nt[:, db, c * CH:(c + 1) * CH], start=(db == 0), stop=(db == DB - 1))
                last.then_inc(ready, 1)

        @block.vector
        def _(dve):
            for n, (b, c) in enumerate(tiles):
                dve.wait_ge(ready, n + 1)
                dve.tensor_scalar(full[:, b, c * CH:(c + 1) * CH], bank[n % 4][:, :],
                                  const["bqk"][:, 2 * l * DB + b:2 * l * DB + b + 1], scale, ALU.add, ALU.mult)\
                    .then_inc(added, 1)
            for b in range(DB):
                dve.wait_ge(added, NC * (b + 1))
                split_parts(dve, full[:, b], rest[:, b], [part[:, n, b] for n in range(PART)], split, 5 * b)

        @block.sync
        def _(sp):
            for b in range(DB):
                for n in range(PART):
                    sp.wait_ge(split, 5 * b + (1, 3, 5)[n])
                    sp.dma_start(scratch["q"][n, b * P:(b + 1) * P, :], part[:, n, b]).then_inc(stored, 16)
            sp.wait_ge(stored, 16 * DB * PART)


def attend(nc, const, scratch, l, attn, row_max, mask_q=None, mask_k=None):
    masked = mask_q is not None
    with ExitStack() as ctx:
        sc = Scope(nc, ctx, f"attend{l}")
        k_st = sc.sb("k_st", [AUG, RING, S], BF16)
        q_st = sc.sb("q_st", [AUG, RING, T], BF16)
        values = sc.sb("values", [P, KT, D], F32)
        v_st = sc.sb("v_st", [P, RING, KT, VW], F32)
        probs = sc.sb("probs", [P, RING, T], F32)
        piece_max = sc.sb("piece_max", [P, RING, QT, NP], F32)
        junk = sc.sb("junk", [P, RING, 401], BF16)
        m_rest = sc.sb("m_rest", [QT, P], F32)
        m_part = sc.sb("m_part", [QT, RING, PART, P], BF16)
        o_sb = sc.sb("o_sb", [P, CH], F32)
        inv_sum = sc.sb("inv_sum", [P, RING, NC, NC], F32)
        s_bank = [sc.ps(f"s_bank{n}", [P, HALF], F32) for n in range(2)]
        p_bank = [sc.ps(f"p_bank{n}", [P, CH], F32) for n in range(RING)]
        o_bank = sc.ps("o_bank", [P, CH], F32)

        stack_in = [sc.sem(f"stack_in{n}") for n in range(RING)]
        values_in = sc.sem("values_in")
        tail_zero = sc.sem("tail_zero")
        fixed = sc.sem("fixed")
        v_ready = sc.sem("v_ready")
        entry_ready = sc.sem("entry_ready")
        entry_done = sc.sem("entry_done")
        max_ready = sc.sem("max_ready")
        max_split = sc.sem("max_split")
        max_in = sc.sem("max_in")
        score_ready = sc.sem("score_ready")
        exp_done = sc.sem("exp_done")
        pv_done = sc.sem("pv_done")
        o_copied = sc.sem("o_copied")
        inverted = sc.sem("inverted")
        block = ctx.enter_context(nc.Block())

        LOADS = 9
        GROUPS_K = [(0, 3), (3, 2), (5, 1)]
        GROUPS_Q = [(0, 0), (1, 0), (2, 0), (3, 1), (4, 1), (5, 2)]
        PER = QT * NP
        cuts = [PER * s // KT for s in range(KT + 1)]
        ENTRIES = PER + 2
        assert ENTRIES % RING == 0

        def entries(mx, tail, fresh):
            steps, n = [], 0
            for s in range(KT):
                now = list(range(cuts[s], cuts[s + 1])) if mx else []
                now += ["maxima"] * (s == 1 and fresh) + ["sums"] * (s == LATE + 2 and tail)
                steps.append([(what, n + k) for k, what in enumerate(now)])
                n += len(now)
            return steps, n

        def entries_before(i):
            if isinstance(i, int) and i < 2:
                return PER * i
            return i * ENTRIES - 3 if not isinstance(i, int) or i <= H else H * ENTRIES - 1

        def ring_of(i, n):
            return ((entries_before(i) if isinstance(i, int) else 0) + n) % RING

        def bank_of(i, n):
            return p_bank[ring_of(i, n)]

        def iterations(eng, body):
            def once(i):
                body(i, i % RING, i < H, i >= 2, 1 <= i <= H)
            for i in range(4):
                once(i)
            with eng.Fori(4, H - RING + 1, RING) as j:
                for u in range(RING):
                    body(j + u, (4 + u) % RING, True, True, True)
            for i in range(H, H + 2):
                once(i)

        def score_step(i, slot, s, tail, fresh):
            if s < LATE:
                return (i - 2, (slot - 2) % RING, KT - LATE + s) if tail else None
            return (i - 1, (slot - 1) % RING, s - LATE) if fresh and s < KT else None

        def pv_step(i, slot, s, tail, fresh):
            if s <= LATE:
                return (i - 2, (slot - 2) % RING, KT - LATE + s - 1) if tail else None
            return (i - 1, (slot - 1) % RING, s - 1 - LATE) if fresh else None

        @block.sync
        def _(sp):
            def load(h, slot):
                ch = bass.ds(h * DK, DK)
                for g, n in GROUPS_K:
                    sp.dma_start(k_st[g * DK:(g + n) * DK, slot], scratch["k"][l, 0:n, ch, :]).then_inc(stack_in[slot], 16)
                for g, n in GROUPS_Q:
                    sp.dma_start(q_st[g * DK:(g + 1) * DK, slot], scratch["q"][n, ch, :]).then_inc(stack_in[slot], 16)

            load(0, 0)
            sp.dma_start(values[:, 0:KT - 1], scratch["v"][l, 0:(KT - 1) * P, :].rearrange("(t p) d -> p t d", p=P))\
                .then_inc(values_in, 16)
            sp.wait_ge(tail_zero, 1)
            sp.dma_start(values[0:keys_of(KT - 1), KT - 1], scratch["v"][l, (KT - 1) * P:S, :]).then_inc(values_in, 16)

            def body(i, slot, mx, tail, fresh):
                if fresh:
                    wait(sp, max_split, i * 3)
                    prev = (slot - 1) % RING
                    for n in range(PART):
                        sp.dma_start(q_st[ROWS + n:ROWS + n + 1, prev].rearrange("a (t q) -> a t q", q=P),
                                     m_part[:, prev, n, :]).then_inc(max_in, 16)
                if not isinstance(i, int) or i + 1 < H:
                    if tail:
                        wait(sp, score_ready, (i - 1) * (2 * KT), apart=True)
                    load(i + 1, (slot + 1) % RING)

            def loop_body(i, slot, mx, tail, fresh):
                body(i, slot, mx, tail, fresh)

            for i in range(4):
                body(i, i % RING, True, i >= 2, i >= 1)
            with sp.Fori(4, H - RING, RING) as j:
                for u in range(RING):
                    body(j + u, (4 + u) % RING, True, True, True)
            for i in range(H - RING, H + 1):
                body(i, i % RING, True, True, True)

        @block.gpsimd
        def _(pool):
            pool.memset(values[:, KT - 1], 0.0).then_inc(tail_zero, 1)
            pool.wait_ge(tail_zero, 1)
            pool.memset(k_st[ROWS:AUG, :, :], 1.0).then_inc(fixed, 1)
            pool.wait_ge(fixed, 1)
            pool.memset(v_st[:, :, :, DK:DK + 1], 1.0).then_inc(fixed, 1)
            pool.memset(v_st[:, :, :, DK + 1:VW], 0.0).then_inc(fixed, 1)
            pool.wait_ge(values_in, 32)
            pool.wait_ge(tail_zero, 1)

            def body(i, slot, mx, tail, fresh):
                if mx:
                    if not isinstance(i, int) or i >= RING:
                        wait(pool, pv_done, (i - 2) * KT, apart=True)
                    pool.tensor_copy(v_st[:, slot, :, 0:DK], values[:, :, bass.ds(i * DK, DK)]).then_inc(v_ready, 1)

            iterations(pool, body)

        @block.tensor
        def _(pe):
            pe.wait_ge(fixed, 3)

            def entry(i, slot, what, n):
                wait(pe, entry_done, entries_before(i) + (n - RING + 1))
                bank = bank_of(i, n)
                if what == "maxima":
                    wait(pe, max_ready, i)
                    last = pe.transpose(bank[0:QT, 0:P], row_max[:, (slot - 1) % RING, :], const["ident"][:, :])
                elif what == "sums":
                    wait(pe, o_copied, i - 1)
                    for b in range(NC):
                        last = pe.transpose(bank[:, b * P:(b + 1) * P], o_sb[:, b * P:(b + 1) * P],
                                            const["ident"][:, :])
                else:
                    t, c = divmod(what, NP)
                    k0, kn = PIECES[c]
                    last = pe.matmul(bank[:, 0:kn], q_st[0:ROWS, slot, t * P:(t + 1) * P],
                                     k_st[0:ROWS, slot, k0:k0 + kn], start=True, stop=True)
                last.then_inc(entry_ready, 1)

            def scores(h, hs, kt, half):
                kn = keys_of(kt)
                if not isinstance(h, int) or 2 * (KT * h + kt) + half >= 2:
                    wait(pe, exp_done, h * (2 * KT) + (2 * kt + half - 1))
                for c in range(2):
                    q0 = half * HALF + c * CH
                    out = s_bank[half][0:kn, c * CH:(c + 1) * CH]
                    last = pe.matmul(out, k_st[:, hs, kt * P:kt * P + kn], q_st[:, hs, q0:q0 + CH],
                                     start=True, stop=not masked)
                    if masked:
                        last = pe.matmul(out, const["ident_bf"][0:kn, 0:kn], mask_k[0:kn, kt, q0:q0 + CH],
                                         start=False, stop=True)
                last.then_inc(score_ready, 1)

            def times_values(h, hs, kt):
                kn = keys_of(kt)
                if kt == 0:
                    wait(pe, v_ready, h + 1)
                    if not isinstance(h, int) or h >= 1:
                        wait(pe, o_copied, h)
                wait(pe, exp_done, h * (2 * KT) + (2 * kt + 2))
                for c in range(NC):
                    last = pe.matmul(o_bank[c * VW:(c + 1) * VW, :], v_st[0:kn, hs, kt, :],
                                     probs[0:kn, (kt + hs) % RING, c * CH:(c + 1) * CH],
                                     start=(kt == 0), stop=(kt == KT - 1), tile_position=(0, c * VW))
                last.then_inc(pv_done, 1)

            def body(i, slot, mx, tail, fresh):
                if mx:
                    wait(pe, stack_in[slot], (i - slot) * (16 * LOADS // RING) + 16 * LOADS)
                listed, _ = entries(mx, tail, fresh)
                for s in range(KT):
                    now, before = score_step(i, slot, s, tail, fresh), pv_step(i, slot, s, tail, fresh)
                    if now and now[2] == 0:
                        wait(pe, max_in, i * (16 * PART))
                    if now:
                        scores(*now, 0)
                    for what, n in listed[s][0:2]:
                        entry(i, slot, what, n)
                    if now:
                        scores(*now, 1)
                    for what, n in listed[s][2:3]:
                        entry(i, slot, what, n)
                    if before:
                        times_values(*before)
                    for what, n in listed[s][3:]:
                        entry(i, slot, what, n)

            iterations(pe, body)

        def number_of_sums(*heads):
            return next(n for step in entries(*heads)[0] for what, n in step if what == "sums") + 1

        @block.scalar
        def _(act):
            def body(i, slot, mx, tail, fresh):
                sums_at = number_of_sums(not isinstance(i, int) or i <= H, True, True)
                for s in range(KT):
                    now = score_step(i, slot, s, tail, fresh)
                    if now:
                        h, hs, kt = now
                        kn = keys_of(kt)
                        if not isinstance(h, int) or KT * h + kt >= RING:
                            wait(act, pv_done, h * KT + (kt - 2))
                        for half in range(2):
                            wait(act, score_ready, h * (2 * KT) + (2 * kt + half + 1))
                            act.activation(probs[0:kn, (kt + hs) % RING, half * HALF:(half + 1) * HALF],
                                           s_bank[half][0:kn, :], ACT.Exp).then_inc(exp_done, 1)
                    if s == LATE + 1 and tail:
                        wait(act, pv_done, (i - 1) * KT)
                        if not isinstance(i, int) or i >= 3:
                            wait(act, entry_ready, entries_before(i - 1) + sums_at)
                        act.activation(o_sb[:, :], o_bank[:, :], ACT.Copy).then_inc(o_copied, 1)

            iterations(act, body)

        @block.vector
        def _(dve):
            def piece(i, slot, what, n):
                t, c = divmod(what, NP)
                k0, kn = PIECES[c]
                dst = piece_max[:, slot, t, c:c + 1]
                wait(dve, entry_ready, entries_before(i) + (n + 1), apart=masked)
                if masked:
                    dve.tensor_tensor_reduce(junk[:, ring_of(i, n), 0:kn], bank_of(i, n)[:, 0:kn],
                                             mask_q[:, t, k0:k0 + kn], 1.0, -3.0e38, ALU.add, ALU.max, dst)\
                        .then_inc(entry_done, 1)
                else:
                    dve.tensor_reduce(dst, bank_of(i, n)[:, 0:kn], AX.X, ALU.max).then_inc(entry_done, 1)

            def split_max(i, prev, n):
                wait(dve, entry_ready, entries_before(i) + (n + 1))
                turned = bank_of(i, n)[0:QT, 0:P]
                dve.tensor_scalar(m_part[:, prev, 0], turned, -1.0, None, ALU.mult).then_inc(max_split, 1)
                wait(dve, max_split, (i - 1) * 3 + 1)
                dve.scalar_tensor_tensor(out=m_rest[:, :], in0=turned, scalar=-1.0, in1=m_part[:, prev, 0],
                                         op0=ALU.mult, op1=ALU.subtract).then_inc(max_split, 1)
                wait(dve, max_split, (i - 1) * 3 + 2)
                dve.tensor_copy(m_part[:, prev, 1], m_rest[:, :]).then_inc(entry_done, 1)
                wait(dve, entry_done, entries_before(i) + (n + 1))
                dve.tensor_tensor(m_part[:, prev, 2], m_rest[:, :], m_part[:, prev, 1], ALU.subtract)\
                    .then_inc(max_split, 1)

            def norm(i, slot, n):
                wait(dve, entry_ready, entries_before(i) + (n + 1))
                sums = bank_of(i, n)[:, :].rearrange("p (b c v) -> p b c v", b=NC, v=VW)
                dve.reciprocal(inv_sum[:, slot], sums[:, :, :, DK]).then_inc(inverted, 1)
                wait(dve, inverted, i - 1, apart=True)
                out = attn[:, :, bass.ds((i - 2) * DK, DK)].rearrange("p (c b) d -> p b c d", b=NC)
                dve.tensor_tensor(out, sums[:, :, :, 0:DK], inv_sum[:, slot].unsqueeze(3).to_broadcast([P, NC, NC, DK]),
                                  ALU.mult).then_inc(entry_done, 1)

            def body(i, slot, mx, tail, fresh):
                listed, many = entries(mx, tail, fresh)
                for step in listed:
                    for what, n in step:
                        if what == "maxima":
                            split_max(i, (slot - 1) % RING, n)
                        elif what == "sums":
                            norm(i, slot, n)
                        else:
                            piece(i, slot, what, n)
                if mx:
                    wait(dve, entry_done, entries_before(i) + many)
                    dve.tensor_reduce(row_max[:, slot, :], piece_max[:, slot], AX.X, ALU.max).then_inc(max_ready, 1)

            iterations(dve, body)


def project_out(nc, const, l, attn, row_max, x_src, x_dst):
    with ExitStack() as ctx:
        sc = Scope(nc, ctx, f"out{l}")
        x_in = sc.sb("x_in", [P, QT, D], F32)
        a_t = sc.sb("a_t", [P, DB, T], F32)
        biased = sc.sb("biased", [P, 2, D], F32)
        x_out = sc.sb("x_out", [P, QT, D], F32)
        lost = sc.sb("lost", [P, 3, QT], F32)
        t_bank = [sc.ps(f"t_bank{n}", [P, CH], F32) for n in range(4)]
        y_bank = [sc.ps(f"y_bank{n}", [P, D], F32) for n in range(4)]
        landed, marked, turned = sc.sem("landed"), sc.sem("marked"), sc.sem("turned")
        copied = sc.sem("copied")
        ready, with_bias, added, stored = sc.sem("ready"), sc.sem("with_bias"), sc.sem("added"), sc.sem("stored")
        block = ctx.enter_context(nc.Block())
        last_head = (H - 1) % RING

        @block.sync
        def _(sp):
            sp.dma_start(x_in[:, :, :], x_src.rearrange("(t p) d -> p t d", p=P)).then_inc(landed, 16)
            for n in range(4):
                sp.wait_ge(added, 4 * (n + 1))
                sp.dma_start(x_dst.rearrange("(t p) d -> p t d", p=P)[:, 4 * n:4 * n + 4],
                             x_out[:, 4 * n:4 * n + 4]).then_inc(stored, 16)
            sp.wait_ge(stored, 64)

        @block.tensor
        def _(pe):
            def turn(n):
                if n >= 4:
                    pe.wait_ge(copied, n - 3)
                for t in (2 * n, 2 * n + 1):
                    for b in range(DB):
                        last = pe.transpose(t_bank[n % 4][:, ((t % 2) * DB + b) * P:((t % 2) * DB + b + 1) * P],
                                            attn[:, t, b * P:(b + 1) * P], const["ident"][:, :])
                last.then_inc(turned, 1)

            turn(0)
            for n in range(QT // 2):
                if n + 1 < QT // 2:
                    turn(n + 1)
                pe.wait_ge(copied, n + 1)
                for t in (2 * n, 2 * n + 1):
                    if t >= 4:
                        pe.wait_ge(with_bias, t - 3)
                    for b in range(DB):
                        last = pe.matmul(y_bank[t % 4][:, :], a_t[:, b, t * P:(t + 1) * P], const["wo_t"][:, l, b],
                                         start=(b == 0), stop=(b == DB - 1))
                    last.then_inc(ready, 1)

        @block.scalar
        def _(act):
            for n in range(QT // 2):
                act.wait_ge(turned, n + 1)
                act.activation(a_t[:, :, 2 * n * P:2 * (n + 1) * P].rearrange("p b (t q) -> p t b q", t=2),
                               t_bank[n % 4][:, :].rearrange("p (t b q) -> p t b q", t=2, b=DB), ACT.Copy)\
                    .then_inc(copied, 1)

        @block.vector
        def _(dve):
            if l == 0:
                dve.tensor_scalar(lost[:, 0], row_max[:, last_head], NEG / 2, 3.0e38, ALU.is_lt, ALU.mult)\
                    .then_inc(marked, 1)
                dve.wait_ge(marked, 1)
                dve.tensor_scalar(lost[:, 1], lost[:, 0], 3.0e38, None, ALU.mult).then_inc(marked, 1)
                dve.wait_ge(marked, 2)
                dve.tensor_tensor(lost[:, 2], lost[:, 1], lost[:, 1], ALU.subtract).then_inc(marked, 1)
            else:
                dve.memset(lost[:, 2], 0.0).then_inc(marked, 3)
            dve.wait_ge(marked, 3)
            dve.wait_ge(landed, 16)
            for t in range(QT):
                dve.wait_ge(ready, t + 1)
                dve.scalar_tensor_tensor(out=biased[:, t % 2], in0=y_bank[t % 4][:, :], scalar=lost[:, 2, t:t + 1],
                                         in1=const["bo"][:, l], op0=ALU.add, op1=ALU.add).then_inc(with_bias, 1)
                dve.wait_ge(with_bias, t + 1)
                dve.scalar_tensor_tensor(out=x_out[:, t], in0=biased[:, t % 2], scalar=const["gates"][:, l:l + 1],
                                         in1=x_in[:, t], op0=ALU.mult, op1=ALU.add).then_inc(added, 1)


class Moe:

    def __init__(self, l):
        self.l = l
        self.F, self.FW = (1024, 128) if l == 0 else (192, 96)
        self.FT = self.F // self.FW
        self.HW = min(CH, self.F)
        self.HV = self.F // self.HW
        self.K = l + 1
        self.NS = (self.K * T + E * (P - 1)) // P
        self.pre = f"L{l}_ffn_"
        self.up = [("w1s", "W1"), ("w2s", "W2")] if l == 0 else [("Wg_s", "Wg"), ("Wu_s", "Wu")]
        self.down = ("w3s", "W3") if l == 0 else ("Wd_s", "Wd")
        self.router = "Wg" if l == 0 else "W_gate_router"
        self.func = ACT.Gelu if l == 0 else ACT.Silu


def route_and_share(nc, io, const, scratch, m, x_nt, x_n, acc, place, weight, slot_expert):
    l, F, FW, FT, NS, K = m.l, m.F, m.FW, m.FT, m.NS, m.K
    with ExitStack() as ctx:
        sc = Scope(nc, ctx, f"share{l}")
        w_up = sc.sb("w_up", [P, 2, DB, F], F32)
        w_dn = sc.sb("w_dn", [FW, FT, D], F32)
        w_rt = sc.sb("w_rt", [P, DB, E], F32)
        bias = sc.sb("bias", [P, E], F32)
        scores = sc.sb("scores", [P, QT, E], F32)
        biased = sc.sb("biased", [P, QT, E], F32)
        behind = sc.sb("behind", [P, QT, E], F32)
        picked = sc.sb("picked", [P, K, QT, E], F32)
        chosen = sc.sb("chosen", [P, QT, E], F32)
        best = sc.sb("best", [P, 4, QT], F32)
        sums = sc.sb("sums", [P, 2, QT, E], F32)
        total = sc.sb("total", [P, QT, E], F32)
        count = sc.sb("count", [P, E], F32)
        over = sc.sb("over", [P, E, QT], F32)
        slots = sc.sb("slots", [P, E], F32)
        ends = sc.sb("ends", [P, 2, E], F32)
        start = sc.sb("start", [P, E], F32)
        row = sc.sb("row", [P, QT, E], F32)
        mine = sc.sb("mine", [P, K, QT, E], F32)
        row_k = sc.sb("row_k", [P, K, QT], F32)
        passed = sc.sb("passed", [P, NS, E], F32)
        expert = sc.sb("expert", [P, NS], F32)
        g_act = sc.sb("g_act", [FW, 2, CH], F32)
        hid = sc.sb("hid", [FW, 2, FT, CH], F32)
        a_bank = [sc.ps(f"a_bank{n}", [P, CH], F32) for n in range(2)]
        b_bank = [sc.ps(f"b_bank{n}", [P, CH], F32) for n in range(2)]
        y_bank = [sc.ps(f"y_bank{n}", [P, D], F32) for n in range(2)]
        r_bank = sc.ps("r_bank", [P, QT, E], F32)
        c_bank = sc.ps("c_bank", [P, 2, QT, E], F32)
        router_in, w_in = sc.sem("router_in"), sc.sem("w_in")
        logits_ready, logits_act, step_done = sc.sem("logits_ready"), sc.sem("logits_act"), sc.sem("step_done")
        chosen_ready, ranked, placed = sc.sem("chosen_ready"), sc.sem("ranked"), sc.sem("placed")
        gate_up = [sc.sem("gate_ready"), sc.sem("up_ready")]
        activated, hid_ready = sc.sem("activated"), sc.sem("hid_ready")
        y_ready, y_copied = sc.sem("y_ready"), sc.sem("y_copied")
        scattered = const["scattered"][l]
        block = ctx.enter_context(nc.Block())
        tiles = [(c, f) for c in range(NC) for f in range(FT)]

        @block.sync
        def _(sp):
            sp.dma_start(w_rt[:, :, :], io[m.pre + m.router].rearrange("(b p) e -> p b e", p=P)).then_inc(router_in, 16)
            if l == 1:
                sp.dma_start(bias[:, :], io[m.pre + "expert_bias"].rearrange("(a n) -> a n", a=1).broadcast_to([P, E]))\
                    .then_inc(router_in, 16)
            for n in range(2):
                sp.dma_start(w_up[:, n], io[m.pre + m.up[n][0]].rearrange("(b p) f -> p b f", p=P)).then_inc(w_in, 16)
            sp.dma_start(w_dn[:, :, :], io[m.pre + m.down[0]].rearrange("(b p) f -> p b f", p=FW)).then_inc(w_in, 16)

        @block.gpsimd
        def _(pool):
            pool.wait_ge(placed, K)
            for k in range(K):
                for t in range(QT):
                    pool.indirect_dma_start(scratch["sorted"][l][:, :],
                                            bass.IndirectOffsetOnAxis(ap=place[:, k, t:t + 1], axis=0),
                                            x_n[:, t], None).then_inc(scattered, 16)
            pool.wait_ge(scattered, 16 * K * QT)

        @block.tensor
        def _(pe):
            pe.wait_ge(router_in, 16 * (l + 1))
            for t in range(QT):
                for b in range(DB):
                    last = pe.matmul(r_bank[:, t], x_nt[:, b, t * P:(t + 1) * P], w_rt[:, b], start=(b == 0),
                                     stop=(b == DB - 1))
            last.then_inc(logits_ready, 1)
            pe.wait_ge(w_in, 48)
            for c in range(NC):
                for f in range(FT):
                    n = c * FT + f
                    for which, bank, read in ((0, a_bank, activated), (1, b_bank, hid_ready)):
                        if n >= 2:
                            pe.wait_ge(read, n - 1)
                        for b in range(DB):
                            last = pe.matmul(bank[n % 2][0:FW, :], w_up[:, which, b, f * FW:(f + 1) * FW],
                                             x_nt[:, b, c * CH:(c + 1) * CH], start=(b == 0), stop=(b == DB - 1))
                        last.then_inc(gate_up[which], 1)
                for t in range(CH // P):
                    n = c * (CH // P) + t
                    pe.wait_ge(hid_ready, FT * (c + 1))
                    if n >= 2:
                        pe.wait_ge(y_copied, n - 1)
                    for f in range(FT):
                        last = pe.matmul(y_bank[n % 2][:, :], hid[:, c % 2, f, t * P:(t + 1) * P], w_dn[:, f],
                                         start=(f == 0), stop=(f == FT - 1))
                    last.then_inc(y_ready, 1)
                if c == 0:
                    pe.wait_ge(chosen_ready, 1)
                    pe.matmul(c_bank[:, 0].rearrange("p t e -> p (t e)"), const["earlier"][:, :],
                              chosen[:, :, :].rearrange("p t e -> p (t e)"), start=True, stop=True)
                    pe.matmul(c_bank[:, 1].rearrange("p t e -> p (t e)"), const["ones"][:, :],
                              chosen[:, :, :].rearrange("p t e -> p (t e)"), start=True, stop=True).then_inc(ranked, 1)

        @block.scalar
        def _(act):
            act.wait_ge(logits_ready, 1)
            act.activation(scores[:, :, :], r_bank[:, :, :], ACT.Copy if l == 0 else ACT.Sigmoid).then_inc(logits_act, 1)
            for n, (c, f) in enumerate(tiles):
                act.wait_ge(gate_up[0], n + 1)
                if n >= 2:
                    act.wait_ge(hid_ready, n - 1)
                act.activation(g_act[:, n % 2], a_bank[n % 2][0:FW, :], m.func).then_inc(activated, 1)

        @block.vector
        def _(dve):
            step = [0]

            def then(ins):
                ins.then_inc(step_done, 1)
                step[0] += 1
                dve.wait_ge(step_done, step[0])

            wide = [P, QT, E]
            number = const["number"]
            eno = number[:, 0:E].unsqueeze(1).to_broadcast(wide)

            def first_best(vals, k):
                then(dve.tensor_reduce(best[:, 0], vals, AX.X, ALU.max))
                then(dve.tensor_tensor(behind[:, :, :], vals, best[:, 0].unsqueeze(2).to_broadcast(wide), ALU.is_lt))
                then(dve.scalar_tensor_tensor(out=behind[:, :, :], in0=behind[:, :, :], scalar=float(2 * E), in1=eno,
                                              op0=ALU.mult, op1=ALU.add))
                then(dve.tensor_reduce(best[:, 1], behind[:, :, :], AX.X, ALU.min))
                then(dve.tensor_tensor(picked[:, k], eno, best[:, 1].unsqueeze(2).to_broadcast(wide), ALU.is_equal))

            dve.wait_ge(logits_act, 1)
            if l == 0:
                first_best(scores[:, :, :], 0)
                dve.tensor_copy(chosen[:, :, :], picked[:, 0]).then_inc(chosen_ready, 1)
            else:
                dve.wait_ge(router_in, 32)
                then(dve.tensor_tensor(biased[:, :, :], scores[:, :, :], bias[:, :].unsqueeze(1).to_broadcast(wide),
                                       ALU.add))
                first_best(biased[:, :, :], 0)
                then(dve.scalar_tensor_tensor(out=biased[:, :, :], in0=picked[:, 0], scalar=-1.0e30,
                                              in1=biased[:, :, :], op0=ALU.mult, op1=ALU.add))
                first_best(biased[:, :, :], 1)
                dve.tensor_tensor(chosen[:, :, :], picked[:, 0], picked[:, 1], ALU.add).then_inc(chosen_ready, 1)
                for k in range(K):
                    then(dve.tensor_tensor(mine[:, k], picked[:, k], scores[:, :, :], ALU.mult))
                    then(dve.tensor_reduce(row_k[:, k], mine[:, k], AX.X, ALU.add))
                then(dve.tensor_tensor(best[:, 2], row_k[:, 0], row_k[:, 1], ALU.add))
                then(dve.tensor_scalar(best[:, 2], best[:, 2], 1.0e-20, None, ALU.add))
                then(dve.reciprocal(best[:, 3], best[:, 2]))
                for k in range(K):
                    then(dve.tensor_tensor(weight[:, k], row_k[:, k], best[:, 3], ALU.mult))

            def place_tokens():
                dve.wait_ge(ranked, 1)
                then(dve.tensor_copy(total[:, :, :], c_bank[:, 1]))
                src, now = total[:, :, :], 0
                d = 1
                while d < QT:
                    dst = sums[:, now]
                    then(dve.tensor_copy(dst[:, 0:d], src[:, 0:d]))
                    then(dve.tensor_tensor(dst[:, d:QT], src[:, d:QT], src[:, 0:QT - d], ALU.add))
                    src, now, d = dst, 1 - now, 2 * d
                then(dve.tensor_scalar(count[:, :], src[:, QT - 1], 1.0 / P, None, ALU.mult))
                then(dve.tensor_tensor(over[:, :, :], count[:, :].unsqueeze(2).to_broadcast([P, E, QT]),
                                       number[:, 0:QT].unsqueeze(1).to_broadcast([P, E, QT]), ALU.is_gt))
                then(dve.tensor_reduce(slots[:, :], over[:, :, :], AX.X, ALU.add))
                end, k, d = slots[:, :], 0, 1
                while d < E:
                    dst = ends[:, k]
                    then(dve.tensor_copy(dst[:, 0:d], end[:, 0:d]))
                    then(dve.tensor_tensor(dst[:, d:E], end[:, d:E], end[:, 0:E - d], ALU.add))
                    end, k, d = dst, 1 - k, 2 * d
                then(dve.tensor_tensor(start[:, :], end, slots[:, :], ALU.subtract))
                then(dve.tensor_scalar(start[:, :], start[:, :], float(P), None, ALU.mult))
                then(dve.tensor_tensor(row[:, :, :], src, total[:, :, :], ALU.subtract))
                then(dve.tensor_tensor(row[:, :, :], row[:, :, :], start[:, :].unsqueeze(1).to_broadcast(wide), ALU.add))
                then(dve.tensor_tensor(row[:, :, :], c_bank[:, 0], row[:, :, :], ALU.add))
                for k in range(K):
                    then(dve.tensor_tensor(mine[:, k], picked[:, k], row[:, :, :], ALU.mult))
                    then(dve.tensor_reduce(row_k[:, k], mine[:, k], AX.X, ALU.add))
                    dve.tensor_copy(place[:, k], row_k[:, k]).then_inc(placed, 1)
                then(dve.tensor_tensor(passed[:, :, :], end.unsqueeze(1).to_broadcast([P, NS, E]),
                                       number[:, 0:NS].unsqueeze(2).to_broadcast([P, NS, E]), ALU.is_le))
                then(dve.tensor_reduce(expert[:, :], passed[:, :, :], AX.X, ALU.add))
                then(dve.tensor_scalar(expert[:, :], expert[:, :], float(E - 1), None, ALU.min))
                then(dve.tensor_copy(slot_expert[:, :], expert[:, :]))

            for c in range(NC):
                for f in range(FT):
                    n = c * FT + f
                    dve.wait_ge(activated, n + 1)
                    dve.wait_ge(gate_up[1], n + 1)
                    if f == 0 and c >= 2:
                        dve.wait_ge(y_ready, (CH // P) * (c - 1))
                    dve.tensor_tensor(hid[:, c % 2, f], b_bank[n % 2][0:FW, :], g_act[:, n % 2], ALU.mult)\
                        .then_inc(hid_ready, 1)
                for t in range(CH // P):
                    n = c * (CH // P) + t
                    dve.wait_ge(y_ready, n + 1)
                    dve.tensor_copy(acc[:, n], y_bank[n % 2][:, :]).then_inc(y_copied, 1)
                if c == 0:
                    place_tokens()


def run_slots(nc, io, const, scratch, m, slot_expert):
    l, F, FW, FT, HW, HV, NS = m.l, m.F, m.FW, m.FT, m.HW, m.HV, m.NS
    HB = -(-FT * P // CH)
    PB = FT // HB
    with ExitStack() as ctx:
        sc = Scope(nc, ctx, f"slots{l}")
        w_up = sc.sb("w_up", [P, 2, 2, DB, F], F32)
        w_dn = sc.sb("w_dn", [FW, 2, FT, D], F32)
        rows = sc.sb("rows", [P, 2, D], F32)
        x_t = sc.sb("x_t", [P, 2, DB, P], F32)
        g_act = sc.sb("g_act", [P, 2, HW], F32)
        hid = sc.sb("hid", [P, 2, F], F32)
        hid_t = sc.sb("hid_t", [FW, 2, FT, P], F32)
        y_sb = sc.sb("y_sb", [P, 2, D], F32)
        a_bank = [sc.ps(f"a_bank{n}", [P, CH], F32) for n in range(2)]
        b_bank = [sc.ps(f"b_bank{n}", [P, CH], F32) for n in range(2)]
        h_bank = [sc.ps(f"h_bank{n}", [P, CH], F32) for n in range(HB)]
        x_bank = sc.ps("x_bank", [P, CH], F32)
        y_bank = sc.ps("y_bank", [P, CH], F32)
        up_in = [sc.sem("up_in0"), sc.sem("up_in1")]
        down_in = [sc.sem("down_in0"), sc.sem("down_in1")]
        rows_in = [sc.sem("rows_in0"), sc.sem("rows_in1")]
        y_stored = [sc.sem("y_stored0"), sc.sem("y_stored1")]
        x_turned, x_copied = sc.sem("x_turned"), sc.sem("x_copied")
        gate_ready, up_ready = sc.sem("gate_ready"), sc.sem("up_ready")
        activated, hid_ready = sc.sem("activated"), sc.sem("hid_ready")
        h_turned = sc.sem("h_turned")
        h_copied = [sc.sem(f"h_copied{n}") for n in range(HB)]
        y_ready, y_copied = sc.sem("y_ready"), sc.sem("y_copied")
        block = ctx.enter_context(nc.Block())
        assert NS % 2 == 1
        first = lambda s, n=1: isinstance(s, int) and s < n

        def steps(eng, body):
            for s in range(3):
                body(s, s % 2, True, s > 0)
            with eng.Fori(3, NS - 1, 2) as j:
                for u in range(2):
                    body(j + u, (3 + u) % 2, True, True)
            body(NS, NS % 2, False, True)

        @block.sync
        def _(sp):
            def expert_of(s):
                return bass.ds(sp.value_load(slot_expert[0:1, bass.ds(s, 1)], min_val=0, max_val=E - 1), 1)

            def load_rows(s, slot):
                sp.dma_start(rows[:, slot], scratch["sorted"][l][bass.ds(s * P, P), :]).then_inc(rows_in[slot], 16)

            def load_up(s, slot):
                e = expert_of(s)
                for n in range(2):
                    sp.dma_start(w_up[:, slot, n], io[m.pre + m.up[n][1]][e].rearrange("a (b p) f -> p (a b) f", p=P))\
                        .then_inc(up_in[slot], 16)

            def load_down(s, slot):
                sp.dma_start(w_dn[:, slot], io[m.pre + m.down[1]][expert_of(s)]
                             .rearrange("a (b p) f -> p (a b) f", p=FW)).then_inc(down_in[slot], 16)

            def store(s, slot):
                sp.dma_start(scratch["back"][l][bass.ds(s * P, P), :], y_sb[:, slot]).then_inc(y_stored[slot], 16)

            def body(s, slot):
                if not first(s, 2):
                    wait(sp, x_turned, s - 1, apart=True)
                load_rows(s, slot)
                if not first(s, 2):
                    wait(sp, up_ready, s * HV - HV, apart=True)
                load_up(s, slot)
                if not first(s, 3):
                    wait(sp, y_copied, s - 2, apart=True)
                    store(s - 3, 1 - slot)
                if not first(s):
                    load_down(s - 1, 1 - slot)

            for s in range(3):
                body(s, s % 2)
            with sp.Fori(3, NS - 1, 2) as j:
                for u in range(2):
                    body(j + u, (3 + u) % 2)
            for s in range(NS - 3, NS):
                wait(sp, y_copied, s + 1)
                store(s, s % 2)
                if s == NS - 3:
                    load_down(NS - 1, (NS - 1) % 2)
            for n in range(2):
                sp.wait_ge(y_stored[n], 16 * ((NS + 1 - n) // 2))

        @block.tensor
        def _(pe):
            def turn_rows(s, slot):
                wait(pe, rows_in[slot], (s - slot) * 8 + 16)
                if not first(s):
                    wait(pe, x_copied, s)
                for b in range(DB):
                    last = pe.transpose(x_bank[:, b * P:(b + 1) * P], rows[:, slot, b * P:(b + 1) * P],
                                        const["ident"][:, :])
                last.then_inc(x_turned, 1)

            def go_up(s, slot, half):
                k = half if HV == 2 else slot
                for which, bank, used, ready in ((0, a_bank, activated, gate_ready), (1, b_bank, hid_ready, up_ready)):
                    if not (first(s) or (HV == 1 and first(s, 2))):
                        wait(pe, used, s * HV + (half - 1))
                    for b in range(DB):
                        last = pe.matmul(bank[k][:, 0:HW], x_t[:, slot, b],
                                         w_up[:, slot, which, b, half * HW:(half + 1) * HW],
                                         start=(b == 0), stop=(b == DB - 1))
                    last.then_inc(ready, 1)

            def turn_hidden(s, slot):
                wait(pe, hid_ready, s * HV + HV)
                if not first(s):
                    for n in range(HB):
                        wait(pe, h_copied[n], s)
                for f in range(FT):
                    last = pe.transpose(h_bank[f // PB][0:FW, (f % PB) * P:(f % PB + 1) * P],
                                        hid[:, slot, f * FW:(f + 1) * FW], const["ident"][:, :])
                last.then_inc(h_turned, 1)

            def go_down(s, slot):
                wait(pe, down_in[slot], (s - slot) * 8 + 16)
                for n in range(HB):
                    wait(pe, h_copied[n], s + 1)
                if not first(s):
                    wait(pe, y_copied, s)
                for f in range(FT):
                    last = pe.matmul(y_bank[:, 0:D], hid_t[:, slot, f], w_dn[:, slot, f], start=(f == 0),
                                     stop=(f == FT - 1))
                last.then_inc(y_ready, 1)

            def body(s, slot, up, down):
                if up:
                    wait(pe, up_in[slot], (s - slot) * 16 + 32)
                    wait(pe, x_copied, s + 1)
                    go_up(s, slot, 0)
                    if not (isinstance(s, int) and s == NS - 1):
                        turn_rows(s + 1, 1 - slot)
                if down and HV == 2:
                    turn_hidden(s - 1, 1 - slot)
                if up and HV == 2:
                    go_up(s, slot, 1)
                if down:
                    if HV == 1:
                        turn_hidden(s - 1, 1 - slot)
                    go_down(s - 1, 1 - slot)

            turn_rows(0, 0)
            for s in range(3):
                body(s, s % 2, True, s > 0)
            with pe.Fori(3, NS - 3, 2) as j:
                for u in range(2):
                    body(j + u, (3 + u) % 2, True, True)
            for s in range(NS - 2, NS):
                body(s, s % 2, True, True)
            body(NS, NS % 2, False, True)

        def copy_rows(act, s, slot):
            wait(act, x_turned, s + 1)
            if not first(s, 2):
                wait(act, up_ready, s * HV - HV)
            act.activation(x_t[:, slot], x_bank[:, 0:DB * P].rearrange("p (b q) -> p b q", b=DB), ACT.Copy)\
                .then_inc(x_copied, 1)

        def copy_hidden(eng, copy, n, s, slot):
            wait(eng, h_turned, s + 1)
            if not first(s, 2):
                wait(eng, y_ready, s - 1)
            copy(hid_t[:, slot, n * PB:(n + 1) * PB],
                 h_bank[n][0:FW, 0:PB * P].rearrange("p (f q) -> p f q", f=PB)).then_inc(h_copied[n], 1)

        @block.scalar
        def _(act):
            def copy(out, in_):
                return act.activation(out, in_, ACT.Copy)

            def gate(s, slot, half):
                k = half if HV == 2 else slot
                wait(act, gate_ready, s * HV + (half + 1))
                if not (first(s) or (HV == 1 and first(s, 2))):
                    wait(act, hid_ready, s * HV + (half - 1))
                act.activation(g_act[:, k], a_bank[k][:, 0:HW], m.func).then_inc(activated, 1)

            def body(s, slot, up, down):
                if up:
                    gate(s, slot, 0)
                    if not (isinstance(s, int) and s == NS - 1):
                        copy_rows(act, s + 1, 1 - slot)
                if down:
                    copy_hidden(act, copy, 0, s - 1, 1 - slot)
                if up and HV == 2:
                    gate(s, slot, 1)

            copy_rows(act, 0, 0)
            for s in range(3):
                body(s, s % 2, True, s > 0)
            with act.Fori(3, NS - 3, 2) as j:
                for u in range(2):
                    body(j + u, (3 + u) % 2, True, True)
            for s in range(NS - 2, NS):
                body(s, s % 2, True, True)
            body(NS, NS % 2, False, True)

        @block.vector
        def _(dve):
            def hidden(s, slot, half):
                k = half if HV == 2 else slot
                wait(dve, activated, s * HV + (half + 1))
                wait(dve, up_ready, s * HV + (half + 1))
                if not first(s, 2):
                    wait(dve, h_turned, s - 1)
                dve.tensor_tensor(hid[:, slot, half * HW:(half + 1) * HW], b_bank[k][:, 0:HW], g_act[:, k], ALU.mult)\
                    .then_inc(hid_ready, 1)

            def result(s, slot):
                wait(dve, y_ready, s + 1)
                if not first(s, 2):
                    wait(dve, y_stored[slot], (s - slot) * 8)
                dve.tensor_copy(y_sb[:, slot], y_bank[:, 0:D]).then_inc(y_copied, 1)

            def body(s, slot, up, down):
                if up:
                    hidden(s, slot, 0)
                if down and HB == 2:
                    copy_hidden(dve, dve.tensor_copy, 1, s - 1, 1 - slot)
                if up and HV == 2:
                    hidden(s, slot, 1)
                if down:
                    result(s - 1, 1 - slot)

            steps(dve, body)


def collect(nc, const, scratch, m, acc, place, weight, x_src, x_dst):
    l, K = m.l, m.K
    with ExitStack() as ctx:
        sc = Scope(nc, ctx, f"collect{l}")
        back = sc.sb("back", [P, K, QT, D], F32)
        x_in = sc.sb("x_in", [P, QT, D], F32)
        x_landed, summed, final, stored = sc.sem("x_landed"), sc.sem("summed"), sc.sem("final"), sc.sem("stored")
        gathered = const["gathered"][l]
        block = ctx.enter_context(nc.Block())

        @block.gpsimd
        def _(pool):
            for t in range(QT):
                for k in range(K):
                    pool.indirect_dma_start(back[:, k, t], None, scratch["back"][l][:, :],
                                            bass.IndirectOffsetOnAxis(ap=place[:, k, t:t + 1], axis=0))\
                        .then_inc(gathered[t], 16)
            for t in range(QT):
                pool.wait_ge(gathered[t], 16 * K)

        @block.sync
        def _(sp):
            sp.dma_start(x_in[:, :, :], x_src.rearrange("(t p) d -> p t d", p=P)).then_inc(x_landed, 16)
            for n in range(4):
                sp.wait_ge(final, 4 * (n + 1))
                sp.dma_start(x_dst.rearrange("(t p) d -> p t d", p=P)[:, 4 * n:4 * n + 4],
                             acc[:, 4 * n:4 * n + 4]).then_inc(stored, 16)
            sp.wait_ge(stored, 64)

        @block.vector
        def _(dve):
            dve.wait_ge(x_landed, 16)
            for t in range(QT):
                dve.wait_ge(gathered[t], 16 * K)
                for k in range(K):
                    if l == 0:
                        dve.tensor_tensor(acc[:, t], acc[:, t], back[:, k, t], ALU.add).then_inc(summed, 1)
                    else:
                        dve.scalar_tensor_tensor(out=acc[:, t], in0=back[:, k, t], scalar=weight[:, k, t:t + 1],
                                                 in1=acc[:, t], op0=ALU.mult, op1=ALU.add).then_inc(summed, 1)
                    dve.wait_ge(summed, K * t + k + 1)
                dve.scalar_tensor_tensor(out=acc[:, t], in0=acc[:, t], scalar=const["gates"][:, 2 + l:3 + l],
                                         in1=x_in[:, t], op0=ALU.mult, op1=ALU.add).then_inc(final, 1)


def flamingo_kernel(nc, io, out):
    Scope.used.clear()
    scratch = {
        "k": nc.dram_tensor("k_parts", [2, PART, D, S], BF16, kind="Internal").ap(),
        "q": nc.dram_tensor("q_parts", [PART, D, T], BF16, kind="Internal").ap(),
        "v": nc.dram_tensor("v_rows", [2, S, D], F32, kind="Internal").ap(),
        "sorted": [nc.dram_tensor(f"sorted{l}", [Moe(l).NS * P, D], F32, kind="Internal").ap() for l in range(2)],
        "back": [nc.dram_tensor(f"back{l}", [Moe(l).NS * P, D], F32, kind="Internal").ap() for l in range(2)],
    }
    x_mid = [nc.dram_tensor(f"x_mid{n}", [T, D], F32, kind="Internal").ap() for n in range(3)]
    x_of = [io["x"][0]] + x_mid + [out[0]]
    with ExitStack() as ctx:
        sc = Scope(nc, ctx, "keep")
        const = {
            "ident": sc.sb("ident", [P, P], F32), "ident_bf": sc.sb("ident_bf", [P, P], BF16),
            "number": sc.sb("number", [P, Moe(1).NS], F32),
            "ones": sc.sb("ones", [P, P], F32),
            "earlier": sc.sb("earlier", [P, P], F32),
            "scattered": [ctx.enter_context(nc.semaphore(f"scattered{l}")) for l in range(2)],
            "gathered": [[ctx.enter_context(nc.semaphore(f"gathered{l}_{t}")) for t in range(QT)] for l in range(2)],
            "gates": sc.sb("gates", [P, 4], F32),
            "wq_t": sc.sb("wq_t", [P, 2, DB, D], F32), "wo_t": sc.sb("wo_t", [P, 2, DB, D], F32),
            "bqk": sc.sb("bqk", [P, 4 * DB], F32),
            "bo": sc.sb("bo", [P, 2, D], F32),
        }
        make_constants(nc, io, const)
        prepare_context(nc, io, const, scratch)
        for l in range(2):
            if l:
                clear_semaphores(nc)
            with ExitStack() as part:
                keep = Scope(nc, part, f"keep_q{l}")
                x_nt, x_n = keep.sb("x_nt", [P, DB, T], F32), keep.sb("x_n", [P, QT, D], F32)
                normalise(nc, const, f"norm_q{l}", x_of[2 * l], x_nt, x_n)
                project_queries(nc, const, scratch, l, x_nt)
            with ExitStack() as part:
                sp = Scope(nc, part, f"keep_a{l}")
                attn = sp.sb("attn", [P, QT, D], F32)
                row_max = sp.sb("row_max", [P, RING, QT], F32)
                with ExitStack() as masks:
                    mask_q = mask_k = None
                    if l == 0:
                        sm = Scope(nc, masks, "keep_mask")
                        mask_q = sm.sb("mask_q", [P, QT, S], BF16)
                        mask_k = sm.sb("mask_k", [P, KT, T], BF16)
                        prepare_mask(nc, io, const, mask_q, mask_k)
                    attend(nc, const, scratch, l, attn, row_max, mask_q, mask_k)
                project_out(nc, const, l, attn, row_max, x_of[2 * l], x_of[2 * l + 1])
            with ExitStack() as part:
                keep = Scope(nc, part, f"keep_f{l}")
                m = Moe(l)
                acc = keep.sb("acc", [P, QT, D], F32)
                place, weight = keep.sb("place", [P, m.K, QT], I32), keep.sb("weight", [P, m.K, QT], F32)
                slot_expert = keep.sb("slot_expert", [P, m.NS], I32)
                with ExitStack() as rows:
                    keep_x = Scope(nc, rows, f"keep_x{l}")
                    x_nt, x_n = keep_x.sb("x_nt", [P, DB, T], F32), keep_x.sb("x_n", [P, QT, D], F32)
                    normalise(nc, const, f"norm_f{l}", x_of[2 * l + 1], x_nt, x_n)
                    route_and_share(nc, io, const, scratch, m, x_nt, x_n, acc, place, weight, slot_expert)
                run_slots(nc, io, const, scratch, m, slot_expert)
                collect(nc, const, scratch, m, acc, place, weight, x_of[2 * l + 1], x_of[2 * l + 2])


_INS = (["x", "ctx_1024", "mask_BxSxS2_ik0", "g_xattn", "g_ffn"]
        + [f"L{l}_xattn_{k}{w}" for l in range(2) for w in "qkvo" for k in "wb"]
        + [f"L0_ffn_{n}" for n in ("w1s", "w2s", "w3s", "W1", "W2", "W3", "Wg")]
        + [f"L1_ffn_{n}" for n in ("W_gate_router", "expert_bias", "Wg", "Wu", "Wd", "Wg_s", "Wu_s", "Wd_s")])
_OUTS = [((1, T, D), "float32")]


def kernel(**inputs):
    import numpy as _np
    import concourse.bacc as _bacc
    from concourse import mybir as _mybir
    from concourse.bass_utils import run_bass_kernel_spmd as _run

    nc = _bacc.Bacc("TRN2", target_bir_lowering=False, num_devices=1)
    arrays, io = {}, {}
    for name in _INS:
        a = _np.ascontiguousarray(inputs[name])
        arrays[f"in_{name}_dram"] = a
        io[name] = nc.dram_tensor(f"in_{name}_dram", a.shape, _mybir.dt.from_np(a.dtype), kind="ExternalInput").ap()
    (shape, dtype), = _OUTS
    out = nc.dram_tensor("out_0_dram", shape, _mybir.dt.from_np(_np.dtype(dtype)), kind="ExternalOutput").ap()
    flamingo_kernel(nc, io, out)
    r = _run(nc, [arrays], core_ids=[0])
    return r.results[0]["out_0_dram"]
```

```python
from contextlib import ExitStack

import concourse.bass as bass
from concourse import mybir

F32 = mybir.dt.float32
BF16 = mybir.dt.bfloat16
I32 = mybir.dt.int32
ALU = mybir.AluOpType
ACT = mybir.ActivationFunctionType
AX = mybir.AxisListType

P = 128
T = 2048
D = 256
S = 1601
H = 16
DK = D // H
DB = D // P
QT = T // P
KT = -(-S // P)
CH = 512
NC = T // CH
HALF = 1024
PART = 3
ROWS = 6 * DK
AUG = ROWS + PART
PIECES = [(0, 401), (401, 400), (801, 400), (1201, 400)]
VW = 32
NEG = -float(2 ** 100)
WINDOW = CH
E = 8
RING = 3
assert sum(n for _, n in PIECES) == S


def keys_of(kt):
    return min(P, S - kt * P)


def wait(eng, sem, value, apart=False):
    if isinstance(value, int):
        if value > 0:
            eng.wait_ge(sem, value)
    else:
        eng.wait_ge(sem, value)
        if apart:
            eng.nop(nofuse=True)


class Scope:

    used = []

    def __init__(self, nc, ctx, stage):
        self.nc, self.ctx, self.stage = nc, ctx, stage

    def sb(self, name, shape, dt):
        return self.ctx.enter_context(self.nc.sbuf_tensor(f"{self.stage}_{name}", shape, dt))

    def ps(self, name, shape, dt):
        return self.ctx.enter_context(self.nc.psum_tensor(f"{self.stage}_{name}", shape, dt))

    def sem(self, name):
        made = self.ctx.enter_context(self.nc.semaphore(f"{self.stage}_{name}"))
        Scope.used.append(made.num)
        return made


def clear_semaphores(nc):
    numbers = sorted(set(Scope.used))
    Scope.used.clear()
    runs = []
    for n in numbers:
        if runs and runs[-1][1] == n:
            runs[-1][1] = n + 1
        else:
            runs.append([n, n + 1])
    with nc.Block() as block:
        @block.gpsimd
        def _(pool):
            for first, end in runs:
                pool.sem_clear(range(first, end))


def make_constants(nc, io, const):
    with ExitStack() as ctx:
        sc = Scope(nc, ctx, "const")
        filled, made, gates_in, gated = sc.sem("filled"), sc.sem("made"), sc.sem("gates_in"), sc.sem("gated")
        raw = sc.sb("raw_gates", [P, 4], F32)
        block = ctx.enter_context(nc.Block())

        @block.gpsimd
        def _(pool):
            pool.memset(const["ident"][:, :], 0.0).then_inc(filled, 1)
            pool.memset(const["ident_bf"][:, :], 0.0).then_inc(filled, 1)
            for n, m in enumerate((const["ident"], const["ident_bf"])):
                pool.wait_ge(filled, n + 1)
                pool.affine_select(out=m[:, :], in_=m[:, :], compare_op=ALU.not_equal, fill=1.0, base=0,
                                   pattern=[[-1, P]], channel_multiplier=1).then_inc(made, 1)
            pool.memset(const["ones"][:, :], 1.0).then_inc(filled, 1)
            pool.memset(const["zeros"][:, :], 0.0).then_inc(made, 1)
            pool.memset(const["earlier"][:, :], 1.0).then_inc(filled, 1)
            pool.wait_ge(filled, 4)
            pool.affine_select(out=const["earlier"][:, :], in_=const["earlier"][:, :], compare_op=ALU.is_gt, fill=0.0,
                               base=0, pattern=[[1, P]], channel_multiplier=-1).then_inc(made, 1)
            pool.wait_ge(made, 4)
            for n in range(const["number"].shape[1]):
                pool.memset(const["number"][:, n:n + 1], float(n)).then_inc(made, 1)

        @block.sync
        def _(sp):
            for n, g in enumerate(("g_xattn", "g_ffn")):
                sp.dma_start(raw[:, 2 * n:2 * n + 2],
                             io[g].rearrange("(a n) -> a n", a=1).broadcast_to([P, 2])).then_inc(gates_in, 16)

        @block.scalar
        def _(act):
            act.wait_ge(gates_in, 32)
            act.activation(const["gates"][:, :], raw[:, :], ACT.Tanh).then_inc(gated, 1)


def prepare_context(nc, io, const, scratch, mask_q, unseen, x_now, stats):
    with ExitStack() as ctx:
        sc = Scope(nc, ctx, "ctx")
        order = "kvqo"
        names = [f"L{l}_xattn_w{w}" for w in order for l in range(2)]
        NW, WR, LOADS, VR = len(names), 4, 4, 2
        w_nat = sc.sb("w_nat", [P, WR, DB, D], F32)
        b_nat = sc.sb("b_nat", [2 * DB * 2, P], F32)
        c_nat = sc.sb("c_nat", [P, KT, D], F32)
        c_t = sc.sb("c_t", [P, DB, S], F32)
        wk_t = sc.sb("wk_t", [P, 2, DB, D], F32)
        wv_t = sc.sb("wv_t", [P, DB, 2, D], F32)
        bv = sc.sb("bv", [P, 2, D], F32)
        k_full = sc.sb("k_full", [P, DB, S], F32)
        k_rest = sc.sb("k_rest", [P, S], F32)
        k_part = sc.sb("k_part", [P, PART, DB, S], BF16)
        v_out = sc.sb("v_out", [P, VR, 2, D], F32)
        raw = sc.sb("raw", [P, 2, S], I32)
        tile_sum = sc.sb("tile_sum", [P, S], BF16)
        ones = sc.sb("ones", [P, 1], BF16)
        bank = [sc.ps(f"bank{n}", [P, CH], F32) for n in range(4)]
        w_in = [sc.sem(f"w_in_{w}") for w in order]
        b_in, bv_in = sc.sem("b_in"), sc.sem("bv_in")
        c_in = [sc.sem(f"c_in{n}") for n in range(LOADS)]
        turned, copied = sc.sem("turned"), sc.sem("copied")
        b_turned, b_copied = sc.sem("b_turned"), sc.sem("b_copied")
        c_turned, c_copied = sc.sem("c_turned"), sc.sem("c_copied")
        k_ready, k_copied = sc.sem("k_ready"), sc.sem("k_copied")
        v_ready, v_added = sc.sem("v_ready"), sc.sem("v_added")
        v_stored = [sc.sem(f"v_stored{n}") for n in range(VR)]
        split = sc.sem("split")
        x_in, counted = sc.sem("x_in"), sc.sem("counted")
        k_stored = [sc.sem(f"k_stored{b}") for b in range(DB)]
        landed = [sc.sem("landed0"), sc.sem("landed1")]
        made, merged, one_made = sc.sem("made"), sc.sem("merged"), sc.sem("one_made")
        block = ctx.enter_context(nc.Block())
        units = [(l, b) for l in range(2) for b in range(DB)]
        AHEAD = 2
        chunks = [(l, b, c) for l, b in units for c in range(len(PIECES))]
        per = -(-(KT - 1) // LOADS)

        @block.gpsimd
        def _(pool):
            pool.memset(ones[:, :], 1.0).then_inc(one_made, 1)
            pool.wait_ge(made, 1)
            pool.tensor_copy(tile_sum[:, :], mask_q[:, 0]).then_inc(merged, 1)
            for t in range(1, QT):
                pool.wait_ge(made, t + 1)
                pool.wait_ge(merged, t)
                pool.tensor_tensor(tile_sum[:, :], tile_sum[:, :], mask_q[:, t], ALU.add).then_inc(merged, 1)

        @block.sync
        def _(sp):
            def load_mask(t):
                if t >= 2:
                    sp.wait_ge(made, t - 1)
                sp.dma_start(raw[:, t % 2], io["mask_BxSxS2_ik0"][0, t * P:(t + 1) * P, :]).then_inc(landed[t % 2], 16)

            def load_weights(first, end):
                for n in range(first, end):
                    if n >= WR:
                        sp.wait_ge(turned, n - WR + 1)
                    sp.dma_start(w_nat[:, n % WR], io[names[n]].rearrange("(b p) d -> p b d", p=P))\
                        .then_inc(w_in[n // 2], 16)

            load_weights(0, WR)
            load_mask(0)
            load_mask(1)
            for n, (l, b) in enumerate(units):
                for t in range(2 + AHEAD * n, 2 + AHEAD * (n + 1)):
                    load_mask(t)
                for part in range(PART):
                    sp.wait_ge(split, 5 * n + (1, 3, 5)[part])
                    sp.dma_start(scratch["k"][l, part, b * P:(b + 1) * P, :], k_part[:, part, b]).then_inc(k_stored[b], 16)
                if n == 0:
                    load_weights(WR, NW)
                    sp.dma_start(x_now[:, :, :], io["x"][0].rearrange("(t p) d -> p t d", p=P)).then_inc(x_in, 16)
            for kt in range(KT):
                kn = keys_of(kt)
                sp.wait_ge(v_added, kt + 1)
                sp.dma_start(scratch["v"][:, kt * P:kt * P + kn, :].rearrange("l p d -> p l d"), v_out[0:kn, kt % VR])\
                    .then_inc(v_stored[kt % VR], 16)
                if 2 + AHEAD * len(units) + kt < QT:
                    load_mask(2 + AHEAD * len(units) + kt)
            for n in range(VR):
                sp.wait_ge(v_stored[n], 16 * len(range(n, KT, VR)))
            for b in range(DB):
                sp.wait_ge(k_stored[b], 16 * 2 * PART)

        @block.tensor
        def _(pe):
            def turn_weight(n):
                pe.wait_ge(w_in[n // 2], 32)
                if n >= 2:
                    pe.wait_ge(copied, n - 1)
                for db in range(DB):
                    for eb in range(DB):
                        last = pe.transpose(bank[n % 2][:, db * D + eb * P:db * D + (eb + 1) * P],
                                            w_nat[:, n % WR, eb, db * P:(db + 1) * P], const["ident"][:, :])
                last.then_inc(turned, 1)

            for kt in range(KT):
                load = min(kt // per, LOADS - 1)
                pe.wait_ge(c_in[load], 16 if load < LOADS - 1 else 32)
                if kt >= 2:
                    pe.wait_ge(c_copied, kt - 1)
                kn = keys_of(kt)
                for db in range(DB):
                    last = pe.transpose(bank[2 + kt % 2][:, db * P:db * P + kn], c_nat[0:kn, kt, db * P:(db + 1) * P],
                                        const["ident"][0:kn, 0:kn])
                last.then_inc(c_turned, 1)
            pe.wait_ge(b_in, 64)
            pe.transpose(unseen[:, 0:4 * DB], b_nat[:, :], const["ident"][0:4 * DB, 0:4 * DB]).then_inc(b_turned, 1)
            for n in range(4):
                turn_weight(n)
            pe.wait_ge(copied, 4)
            pe.wait_ge(c_copied, KT)
            for n, (l, b, c) in enumerate(chunks):
                if n >= 2:
                    pe.wait_ge(k_copied, n - 1)
                k0, kn = PIECES[c]
                for db in range(DB):
                    last = pe.matmul(bank[n % 2][:, 0:kn], wk_t[:, l, db, b * P:(b + 1) * P], c_t[:, db, k0:k0 + kn],
                                     start=(db == 0), stop=(db == DB - 1))
                last.then_inc(k_ready, 1)
            for kt in range(KT):
                if kt >= 2:
                    pe.wait_ge(v_added, kt - 1)
                kn = keys_of(kt)
                for db in range(DB):
                    last = pe.matmul(bank[2 + kt % 2][0:kn, :], c_t[:, db, kt * P:kt * P + kn],
                                     wv_t[:, db].rearrange("p l d -> p (l d)"), start=(db == 0), stop=(db == DB - 1))
                last.then_inc(v_ready, 1)
            pe.wait_ge(k_copied, len(chunks))
            for n in range(4, NW):
                turn_weight(n)
            pe.wait_ge(one_made, 1)
            pe.wait_ge(b_copied, 1)
            pe.wait_ge(merged, QT)
            for kt in range(KT):
                kn = keys_of(kt)
                pe.matmul(unseen[0:kn, kt:kt + 1], tile_sum[:, kt * P:kt * P + kn], ones[:, :], start=True, stop=True)

        @block.scalar
        def _(act):
            for n in range(LOADS):
                a, b = n * per, min((n + 1) * per, KT - 1)
                act.dma_start(c_nat[:, a:b], io["ctx_1024"][0, a * P:b * P, :].rearrange("(t p) d -> p t d", p=P))\
                    .then_inc(c_in[n], 16)
            act.dma_start(c_nat[0:keys_of(KT - 1), KT - 1], io["ctx_1024"][0, (KT - 1) * P:S, :])\
                .then_inc(c_in[LOADS - 1], 16)
            for n, name in enumerate(["L0_xattn_bq", "L0_xattn_bk", "L1_xattn_bq", "L1_xattn_bk"]):
                act.dma_start(b_nat[DB * n:DB * n + DB, :], io[name].rearrange("(b p) -> b p", p=P)).then_inc(b_in, 16)
            for l in range(2):
                for dst, name in ((bv[:, l], f"L{l}_xattn_bv"), (const["bo"][:, l], f"L{l}_xattn_bo")):
                    act.dma_start(dst, io[name].rearrange("(a n) -> a n", a=1).broadcast_to([P, D])).then_inc(bv_in, 16)

            def copy_weight(n):
                w, l = divmod(n, 2)
                dst = (wk_t[:, l], wv_t[:, :, l], const["wq_t"][:, l], const["wo_t"][:, l])[w]
                act.wait_ge(turned, n + 1)
                act.activation(dst, bank[n % 2][:, :].rearrange("p (b d) -> p b d", b=DB), ACT.Copy).then_inc(copied, 1)

            act.wait_ge(b_turned, 1)
            act.activation(const["bqk"][:, :], unseen[:, 0:4 * DB], ACT.Copy).then_inc(b_copied, 1)
            for n in range(4):
                copy_weight(n)
            act.wait_ge(b_copied, 1)
            for n, (l, b, c) in enumerate(chunks):
                k0, kn = PIECES[c]
                act.wait_ge(k_ready, n + 1)
                if c == 0 and l == 1:
                    act.wait_ge(split, 5 * b + 2)
                act.activation(k_full[:, b, k0:k0 + kn], bank[n % 2][:, 0:kn], ACT.Identity,
                               bias=const["bqk"][:, (2 * l + 1) * DB + b:(2 * l + 1) * DB + b + 1]).then_inc(k_copied, 1)
            for n in range(4, NW):
                copy_weight(n)

        @block.vector
        def _(dve):
            def convert(t):
                dve.wait_ge(landed[t % 2], 16 * (t // 2 + 1))
                dve.tensor_scalar(mask_q[:, t], raw[:, t % 2], 0.0, NEG, ALU.is_equal, ALU.mult).then_inc(made, 1)

            for kt in range(KT):
                kn = keys_of(kt)
                dve.wait_ge(c_turned, kt + 1)
                dve.tensor_copy(c_t[:, :, kt * P:kt * P + kn],
                                bank[2 + kt % 2][:, 0:DB * P].rearrange("p (b k) -> p b k", b=DB)[:, :, 0:kn])\
                    .then_inc(c_copied, 1)
            for n, (l, b) in enumerate(units):
                for t in range(AHEAD * n, AHEAD * (n + 1)):
                    convert(t)
                dve.wait_ge(k_copied, len(PIECES) * (n + 1))
                if l:
                    dve.wait_ge(k_stored[b], 16 * PART)
                split_parts(dve, k_full[:, b], k_rest[:, :], [k_part[:, part, b] for part in range(PART)], split, 5 * n)
            dve.wait_ge(bv_in, 64)
            for kt in range(KT):
                kn = keys_of(kt)
                dve.wait_ge(v_ready, kt + 1)
                if kt >= VR:
                    dve.wait_ge(v_stored[kt % VR], 16 * (kt // VR))
                dve.tensor_tensor(v_out[0:kn, kt % VR].rearrange("p l d -> p (l d)"), bank[2 + kt % 2][0:kn, :],
                                  bv[0:kn].rearrange("p l d -> p (l d)"), ALU.add).then_inc(v_added, 1)
                if AHEAD * len(units) + kt < QT:
                    convert(AHEAD * len(units) + kt)
            dve.wait_ge(x_in, 16)
            for t in range(QT):
                dve.bn_stats(stats[:, t], x_now[:, t]).then_inc(counted, 1)


def split_parts(dve, full, rest, parts, split, base):
    dve.tensor_copy(parts[0], full).then_inc(split, 1)
    dve.wait_ge(split, base + 1)
    dve.tensor_tensor(rest, full, parts[0], ALU.subtract).then_inc(split, 1)
    dve.wait_ge(split, base + 2)
    dve.tensor_copy(parts[1], rest).then_inc(split, 1)
    dve.wait_ge(split, base + 3)
    dve.tensor_tensor(rest, rest, parts[1], ALU.subtract).then_inc(split, 1)
    dve.wait_ge(split, base + 4)
    dve.tensor_copy(parts[2], rest).then_inc(split, 1)


class Keys:

    def __init__(self, first, size, pieces, late, maxima_at):
        self.first, self.S, self.pieces = first, size, pieces
        self.KT = -(-size // P)
        self.late = late
        self.maxima_at = maxima_at
        self.copy_at = late + 1
        self.sums_at = min(late + 2, self.KT - 1)
        assert sum(n for _, n in pieces) == size and self.KT % RING == 1

    def keys_of(self, kt):
        return min(P, self.S - kt * P)

    def slice(self, k0, size):
        return slice(k0, k0 + size) if isinstance(self.first, int) else bass.ds(self.first + k0, size)


FAR = 4096.0


def find_ends(dve, unseen, key, score, ends, numbered, scored):
    kl = keys_of(KT - 1)
    for n, far in enumerate((FAR, -FAR)):
        dve.memset(score[:, n, KT - 1:KT], far).then_inc(scored, 1)
        dve.tensor_scalar(score[:, n, 0:KT - 1], unseen[:, 0:KT - 1], NEG * (T - 0.5), far, ALU.is_lt, ALU.mult)\
            .then_inc(scored, 1)
    dve.wait_ge(scored, 4)
    for n, far in enumerate((FAR, -FAR)):
        dve.tensor_scalar(score[0:kl, n, KT - 1:KT], unseen[0:kl, KT - 1:KT], NEG * (T - 0.5), far, ALU.is_lt, ALU.mult)\
            .then_inc(scored, 1)
    dve.wait_ge(scored, 6)
    dve.wait_ge(numbered, 2)
    for n in range(2):
        dve.tensor_tensor(score[:, n], score[:, n], key[:, :], ALU.add).then_inc(scored, 1)
    dve.wait_ge(scored, 8)
    dve.tensor_reduce(ends[:, 0:1], score[:, 0], AX.X, ALU.min).then_inc(scored, 1)
    dve.tensor_reduce(ends[:, 1:2], score[:, 1], AX.X, ALU.max).then_inc(scored, 1)


def find_window(dve, turned, choice, window, ends_turned, stepped):
    first, last, start, fits, room = (choice[:, n:n + 1] for n in range(5))
    dve.wait_ge(ends_turned, 1)
    dve.tensor_reduce(first, turned[:, 0], AX.X, ALU.min).then_inc(stepped, 1)
    dve.tensor_reduce(last, turned[:, 1], AX.X, ALU.max).then_inc(stepped, 1)
    dve.wait_ge(stepped, 2)
    dve.tensor_scalar(start, first, float(S - WINDOW), None, ALU.min).then_inc(stepped, 1)
    dve.wait_ge(stepped, 3)
    dve.scalar_tensor_tensor(out=room, in0=start, scalar=float(WINDOW), in1=last, op0=ALU.add, op1=ALU.subtract)\
        .then_inc(stepped, 1)
    dve.wait_ge(stepped, 4)
    dve.tensor_scalar(fits, room, 0.0, None, ALU.is_gt).then_inc(stepped, 1)
    dve.wait_ge(stepped, 5)
    dve.tensor_copy(window[:, :], choice[:, 2:4]).then_inc(stepped, 1)


def prepare_mask(nc, const, keys, mask_all, mask_q, mask_k):
    with ExitStack() as ctx:
        sc = Scope(nc, ctx, f"mask{keys.KT}")
        KT = keys.KT
        FIRST = min(8, KT)
        turn = [sc.ps(f"turn{n}", [P, 2 * FIRST * P], BF16) for n in range(2)]
        cut, turned, copied = sc.sem("cut"), sc.sem("turned"), sc.sem("copied")
        block = ctx.enter_context(nc.Block())
        kl = keys.keys_of(KT - 1)
        runs = [(p, a, b) for p, a, b in ((P, 0, min(FIRST, KT - 1)), (P, FIRST, KT - 1), (kl, KT - 1, KT)) if a < b]
        whole = mask_q is mask_all

        @block.vector
        def _(dve):
            if not whole:
                for t in range(QT):
                    dve.tensor_copy(mask_q[:, t], mask_all[:, t, keys.slice(0, keys.S)]).then_inc(cut, 1)

        @block.tensor
        def _(pe):
            for t in range(QT):
                if not whole:
                    pe.wait_ge(cut, t + 1)
                if t >= 2:
                    pe.wait_ge(copied, len(runs) * (t - 1))
                for kt in range(KT):
                    kn = keys.keys_of(kt)
                    last = pe.transpose(turn[t % 2][0:kn, kt * P:(kt + 1) * P], mask_q[:, t, kt * P:kt * P + kn],
                                        const["ident_bf"][:, :])
                last.then_inc(turned, 1)

        @block.scalar
        def _(act):
            for t in range(QT):
                act.wait_ge(turned, t + 1)
                src = turn[t % 2][:, :].rearrange("p (k q) -> p k q", q=P)
                for p, a, b in runs:
                    act.activation(mask_k[0:p, a:b, t * P:(t + 1) * P], src[0:p, a:b], ACT.Copy).then_inc(copied, 1)


def normalise(nc, const, stage, x_in, stats, x_nt, x_n):
    with ExitStack() as ctx:
        sc = Scope(nc, ctx, stage)
        mv = sc.sb("mv", [P, QT, 2], F32)
        var = sc.sb("var", [P, QT], F32)
        std = sc.sb("std", [P, QT], F32)
        inv = sc.sb("inv", [P, QT], F32)
        bank = [sc.ps(f"bank{n}", [P, CH], F32) for n in range(4)]
        spread, stable, rooted, inverted = (sc.sem(n) for n in ("spread", "stable", "rooted", "inverted"))
        scaled, turned = sc.sem("scaled"), sc.sem("turned")
        copied = [sc.sem("copied_dve"), sc.sem("copied_act")]
        block = ctx.enter_context(nc.Block())

        def copy_out(n, copy, eng):
            eng.wait_ge(turned, n + 1)
            copy(x_nt[:, :, 2 * n * P:2 * (n + 1) * P].rearrange("p b (t q) -> p t b q", t=2),
                 bank[n % 4][:, :].rearrange("p (t b q) -> p t b q", t=2, b=DB)).then_inc(copied[n % 2], 1)

        @block.vector
        def _(dve):
            for t in range(QT):
                dve.bn_aggr(mv[:, t], stats[:, t]).then_inc(spread, 1)
            dve.wait_ge(spread, QT)
            dve.tensor_scalar(var[:, :], mv[:, :, 1], 1e-5, None, ALU.add).then_inc(stable, 1)
            dve.wait_ge(rooted, 1)
            dve.reciprocal(inv[:, :], std[:, :]).then_inc(inverted, 1)
            dve.wait_ge(inverted, 1)
            for t in range(QT):
                dve.tensor_scalar(x_n[:, t], x_in[:, t], mv[:, t, 0:1], inv[:, t:t + 1], ALU.subtract, ALU.mult)\
                    .then_inc(scaled, 1)
            for n in range(0, QT // 2, 2):
                copy_out(n, dve.tensor_copy, dve)

        @block.scalar
        def _(act):
            act.wait_ge(stable, 1)
            act.activation(std[:, :], var[:, :], ACT.Sqrt).then_inc(rooted, 1)
            for n in range(1, QT // 2, 2):
                copy_out(n, lambda o, i: act.activation(o, i, ACT.Copy), act)

        @block.tensor
        def _(pe):
            for n in range(QT // 2):
                if n >= 4:
                    pe.wait_ge(copied[n % 2], (n - 4) // 2 + 1)
                for t in (2 * n, 2 * n + 1):
                    pe.wait_ge(scaled, t + 1)
                    for b in range(DB):
                        last = pe.transpose(bank[n % 4][:, ((t % 2) * DB + b) * P:((t % 2) * DB + b + 1) * P],
                                            x_n[:, t, b * P:(b + 1) * P], const["ident"][:, :])
                last.then_inc(turned, 1)


def project_queries(nc, const, scratch, l, x_nt, unseen=None, window=None):
    with ExitStack() as ctx:
        sc = Scope(nc, ctx, f"q{l}")
        full = sc.sb("full", [P, DB, T], F32)
        rest = sc.sb("rest", [P, DB, T], F32)
        part = sc.sb("part", [P, PART, DB, T], BF16)
        bias = sc.sb("bias", [P, DB], F32)
        bank = [sc.ps(f"bank{n}", [P, CH], F32) for n in range(4)]
        ready, added, split, stored = sc.sem("ready"), sc.sem("added"), sc.sem("split"), sc.sem("stored")
        bias_ready, numbered, scored, stepped = (sc.sem(n) for n in ("bias_ready", "numbered", "scored", "stepped"))
        if unseen is not None:
            key_int, key, score = sc.sb("key_int", [P, KT], I32), sc.sb("key", [P, KT], F32), sc.sb("score", [P, 2, KT], F32)
            ends = sc.sb("ends", [P, 2], F32)
            choice = sc.sb("choice", [1, 5], F32)
            turned = unseen[0:1, 2 * P:4 * P].rearrange("a (n p) -> a n p", p=P)
            ends_turned = sc.sem("ends_turned")
        block = ctx.enter_context(nc.Block())
        tiles = [(b, c) for b in range(DB) for c in range(NC)]
        halves = [(b, c) for b in range(DB) for c in range(0, NC, 2)]
        scale = float(DK) ** -0.5

        @block.gpsimd
        def _(pool):
            if unseen is not None:
                pool.iota(key_int[:, :], pattern=[[P, KT]], base=0, channel_multiplier=1).then_inc(numbered, 1)
                pool.wait_ge(numbered, 1)
                pool.tensor_copy(key[:, :], key_int[:, :]).then_inc(numbered, 1)

        @block.tensor
        def _(pe):
            for n, (b, c) in enumerate(tiles):
                if n >= 4:
                    pe.wait_ge(added, n - 3)
                for db in range(DB):
                    last = pe.matmul(bank[n % 4][:, :], const["wq_t"][:, l, db, b * P:(b + 1) * P],
                                     x_nt[:, db, c * CH:(c + 1) * CH], start=(db == 0), stop=(db == DB - 1))
                last.then_inc(ready, 1)
            if unseen is not None:
                pe.wait_ge(scored, 10)
                for n in range(2):
                    last = pe.transpose(turned[:, n], ends[:, n:n + 1], const["ident"][:, :])
                last.then_inc(ends_turned, 1)

        @block.scalar
        def _(act):
            act.activation(bias[:, :], const["bqk"][:, 2 * l * DB:(2 * l + 1) * DB], ACT.Copy, scale=scale)\
                .then_inc(bias_ready, 1)
            act.wait_ge(bias_ready, 1)
            for n, (b, c) in enumerate(tiles):
                act.wait_ge(ready, n + 1)
                act.activation(full[:, b, c * CH:(c + 1) * CH], bank[n % 4][:, :], ACT.Identity, bias=bias[:, b:b + 1],
                               scale=scale).then_inc(added, 1)

        @block.vector
        def _(dve):
            if unseen is not None:
                find_ends(dve, unseen, key, score, ends, numbered, scored)
            for n, (b, c) in enumerate(halves):
                at = slice(c * CH, (c + 2) * CH)
                dve.wait_ge(added, 2 * (n + 1))
                split_parts(dve, full[:, b, at], rest[:, b, at], [part[:, k, b, at] for k in range(PART)], split, 5 * n)
            if unseen is not None:
                find_window(dve, turned, choice, window, ends_turned, stepped)

        @block.sync
        def _(sp):
            for n, (b, c) in enumerate(halves):
                at = slice(c * CH, (c + 2) * CH)
                for k in range(PART):
                    sp.wait_ge(split, 5 * n + (1, 3, 5)[k])
                    sp.dma_start(scratch["q"][k, b * P:(b + 1) * P, at], part[:, k, b, at]).then_inc(stored, 16)
            sp.wait_ge(stored, 16 * len(halves) * PART)


def attend(nc, const, scratch, l, keys, attn, row_max, mask_q=None, mask_k=None):
    masked = mask_q is not None
    S, KT, LATE, PIECES, NP, keys_of = keys.S, keys.KT, keys.late, keys.pieces, len(keys.pieces), keys.keys_of
    tail_rows = S - (KT - 1) * P
    NS = Moe(l).NS
    with ExitStack() as ctx:
        sc = Scope(nc, ctx, f"attend{l}_{KT}")
        k_st = sc.sb("k_st", [AUG, RING, S], BF16)
        q_st = sc.sb("q_st", [AUG, RING, T], BF16)
        values = sc.sb("values", [P, KT, D], F32)
        v_st = sc.sb("v_st", [P, RING, KT, VW], F32)
        probs = sc.sb("probs", [P, RING, T], F32)
        piece_max = sc.sb("piece_max", [P, RING, QT, NP], F32)
        junk = sc.sb("junk", [P, RING, PIECES[0][1]], BF16)
        m_rest = sc.sb("m_rest", [QT, P], F32)
        m_part = sc.sb("m_part", [QT, RING, PART, P], BF16)
        o_sb = sc.sb("o_sb", [P, CH], F32)
        inv_sum = sc.sb("inv_sum", [P, RING, NC, NC], F32)
        s_bank = [sc.ps(f"s_bank{n}", [P, HALF], F32) for n in range(2)]
        p_bank = [sc.ps(f"p_bank{n}", [P, CH], F32) for n in range(RING)]
        o_bank = sc.ps("o_bank", [P, CH], F32)

        stack_in = [sc.sem(f"stack_in{n}") for n in range(RING)]
        values_in = sc.sem("values_in")
        cleared = sc.sem("cleared")
        tail_zero = sc.sem("tail_zero")
        fixed = sc.sem("fixed")
        v_ready = sc.sem("v_ready")
        entry_ready = sc.sem("entry_ready")
        entry_done = sc.sem("entry_done")
        max_ready = sc.sem("max_ready")
        max_split = sc.sem("max_split")
        max_in = sc.sem("max_in")
        score_ready = sc.sem("score_ready")
        exp_done = sc.sem("exp_done")
        pv_done = sc.sem("pv_done")
        o_copied = sc.sem("o_copied")
        inverted = sc.sem("inverted")
        block = ctx.enter_context(nc.Block())

        LOADS = 9
        GROUPS_K = [(0, 3), (3, 2), (5, 1)]
        GROUPS_Q = [(0, 0), (1, 0), (2, 0), (3, 1), (4, 1), (5, 2)]
        PER = QT * NP
        cuts = [PER * s // KT for s in range(KT + 1)]
        ENTRIES = PER + 2
        assert ENTRIES % RING == 0

        def entries(mx, tail, fresh):
            steps, n = [], 0
            for s in range(KT):
                now = list(range(cuts[s], cuts[s + 1])) if mx else []
                if fresh and s == keys.maxima_at[0]:
                    now.insert(keys.maxima_at[1] if mx else 0, "maxima")
                now += ["sums"] * (s == keys.sums_at and tail)
                steps.append([(what, n + k) for k, what in enumerate(now)])
                n += len(now)
            return steps, n

        def entries_before(i):
            if isinstance(i, int) and i < 2:
                return PER * i
            return i * ENTRIES - 3 if not isinstance(i, int) or i <= H else H * ENTRIES - 1

        def ring_of(i, n):
            return ((entries_before(i) if isinstance(i, int) else 0) + n) % RING

        def bank_of(i, n):
            return p_bank[ring_of(i, n)]

        def iterations(eng, body):
            def once(i):
                body(i, i % RING, i < H, i >= 2, 1 <= i <= H)
            for i in range(4):
                once(i)
            with eng.Fori(4, H - RING + 1, RING) as j:
                for u in range(RING):
                    body(j + u, (4 + u) % RING, True, True, True)
            for i in range(H, H + 2):
                once(i)

        def score_step(i, slot, s, tail, fresh):
            if s < LATE:
                return (i - 2, (slot - 2) % RING, KT - LATE + s) if tail else None
            return (i - 1, (slot - 1) % RING, s - LATE) if fresh and s < KT else None

        def pv_step(i, slot, s, tail, fresh):
            if s <= LATE:
                return (i - 2, (slot - 2) % RING, KT - LATE + s - 1) if tail else None
            return (i - 1, (slot - 1) % RING, s - 1 - LATE) if fresh else None

        @block.sync
        def _(sp):
            def load(h, slot):
                ch = bass.ds(h * DK, DK)
                for g, n in GROUPS_K:
                    sp.dma_start(k_st[g * DK:(g + n) * DK, slot], scratch["k"][l, 0:n, ch, keys.slice(0, S)]).then_inc(stack_in[slot], 16)
                for g, n in GROUPS_Q:
                    sp.dma_start(q_st[g * DK:(g + 1) * DK, slot], scratch["q"][n, ch, :]).then_inc(stack_in[slot], 16)

            load(0, 0)
            for kt in range(KT):
                if kt == KT - 1 and tail_rows < P:
                    sp.wait_ge(tail_zero, 1)
                sp.dma_start(values[0:keys_of(kt), kt], scratch["v"][l, keys.slice(kt * P, keys_of(kt)), :])\
                    .then_inc(values_in, 16)

            def body(i, slot, mx, tail, fresh):
                if fresh:
                    wait(sp, max_split, i * 3)
                    prev = (slot - 1) % RING
                    for n in range(PART):
                        sp.dma_start(q_st[ROWS + n:ROWS + n + 1, prev].rearrange("a (t q) -> a t q", q=P),
                                     m_part[:, prev, n, :]).then_inc(max_in, 16)
                if not isinstance(i, int) or i + 1 < H:
                    if tail:
                        wait(sp, score_ready, (i - 1) * (2 * KT), apart=True)
                    load(i + 1, (slot + 1) % RING)

            def loop_body(i, slot, mx, tail, fresh):
                body(i, slot, mx, tail, fresh)

            clears = [(t, min(8, NS - t)) for t in range(0, NS, 8)]
            for i in range(4):
                body(i, i % RING, True, i >= 2, i >= 1)
                for t, n in clears[2 * i:2 * i + 2]:
                    sp.dma_start(scratch["sorted"][l][t * P:(t + n) * P, :].rearrange("(t p) d -> p t d", p=P),
                                 const["zeros"][:, :].unsqueeze(1).to_broadcast([P, n, D])).then_inc(cleared, 16)
            with sp.Fori(4, H - RING, RING) as j:
                for u in range(RING):
                    body(j + u, (4 + u) % RING, True, True, True)
            for i in range(H - RING, H + 1):
                body(i, i % RING, True, True, True)
            sp.wait_ge(cleared, 16 * len(clears))

        @block.gpsimd
        def _(pool):
            if tail_rows < P:
                pool.memset(values[:, KT - 1], 0.0).then_inc(tail_zero, 1)
                pool.wait_ge(tail_zero, 1)
            pool.memset(k_st[ROWS:AUG, :, :], 1.0).then_inc(fixed, 1)
            pool.wait_ge(fixed, 1)
            pool.memset(v_st[:, :, :, DK:DK + 1], 1.0).then_inc(fixed, 1)
            pool.memset(v_st[:, :, :, DK + 1:VW], 0.0).then_inc(fixed, 1)
            pool.wait_ge(values_in, 16 * KT)

            def body(i, slot, mx, tail, fresh):
                if mx:
                    if not isinstance(i, int) or i >= RING:
                        wait(pool, pv_done, (i - 2) * KT, apart=True)
                    pool.tensor_copy(v_st[:, slot, :, 0:DK], values[:, :, bass.ds(i * DK, DK)]).then_inc(v_ready, 1)

            iterations(pool, body)

        @block.tensor
        def _(pe):
            pe.wait_ge(fixed, 3)

            def entry(i, slot, what, n):
                wait(pe, entry_done, entries_before(i) + (n - RING + 1))
                bank = bank_of(i, n)
                if what == "maxima":
                    wait(pe, max_ready, i)
                    last = pe.transpose(bank[0:QT, 0:P], row_max[:, (slot - 1) % RING, :], const["ident"][:, :])
                elif what == "sums":
                    wait(pe, o_copied, i - 1)
                    for b in range(NC):
                        last = pe.transpose(bank[:, b * P:(b + 1) * P], o_sb[:, b * P:(b + 1) * P],
                                            const["ident"][:, :])
                else:
                    t, c = divmod(what, NP)
                    k0, kn = PIECES[c]
                    last = pe.matmul(bank[:, 0:kn], q_st[0:ROWS, slot, t * P:(t + 1) * P],
                                     k_st[0:ROWS, slot, k0:k0 + kn], start=True, stop=True)
                last.then_inc(entry_ready, 1)

            def scores(h, hs, kt, half):
                kn = keys_of(kt)
                if not isinstance(h, int) or 2 * (KT * h + kt) + half >= 2:
                    wait(pe, exp_done, h * (2 * KT) + (2 * kt + half - 1))
                for c in range(2):
                    q0 = half * HALF + c * CH
                    out = s_bank[half][0:kn, c * CH:(c + 1) * CH]
                    last = pe.matmul(out, k_st[:, hs, kt * P:kt * P + kn], q_st[:, hs, q0:q0 + CH],
                                     start=True, stop=not masked)
                    if masked:
                        last = pe.matmul(out, const["ident_bf"][0:kn, 0:kn], mask_k[0:kn, kt, q0:q0 + CH],
                                         start=False, stop=True)
                last.then_inc(score_ready, 1)

            def times_values(h, hs, kt):
                kn = keys_of(kt)
                if kt == 0:
                    wait(pe, v_ready, h + 1)
                    if not isinstance(h, int) or h >= 1:
                        wait(pe, o_copied, h)
                wait(pe, exp_done, h * (2 * KT) + (2 * kt + 2))
                for c in range(NC):
                    last = pe.matmul(o_bank[c * VW:(c + 1) * VW, :], v_st[0:kn, hs, kt, :],
                                     probs[0:kn, (kt + hs) % RING, c * CH:(c + 1) * CH],
                                     start=(kt == 0), stop=(kt == KT - 1), tile_position=(0, c * VW))
                last.then_inc(pv_done, 1)

            def body(i, slot, mx, tail, fresh):
                if mx:
                    wait(pe, stack_in[slot], (i - slot) * (16 * LOADS // RING) + 16 * LOADS)
                listed, _ = entries(mx, tail, fresh)
                for s in range(KT):
                    now, before = score_step(i, slot, s, tail, fresh), pv_step(i, slot, s, tail, fresh)
                    if now and now[2] == 0:
                        wait(pe, max_in, i * (16 * PART))
                    if now:
                        scores(*now, 0)
                    for what, n in listed[s][0:2]:
                        entry(i, slot, what, n)
                    if now:
                        scores(*now, 1)
                    for what, n in listed[s][2:3]:
                        entry(i, slot, what, n)
                    if before:
                        times_values(*before)
                    for what, n in listed[s][3:]:
                        entry(i, slot, what, n)

            iterations(pe, body)

        def number_of_sums(*heads):
            return next(n for step in entries(*heads)[0] for what, n in step if what == "sums") + 1

        @block.scalar
        def _(act):
            def body(i, slot, mx, tail, fresh):
                sums_at = number_of_sums(not isinstance(i, int) or i <= H, True, True)
                for s in range(KT):
                    now = score_step(i, slot, s, tail, fresh)
                    if s == keys.copy_at and tail:
                        wait(act, pv_done, (i - 1) * KT)
                        if not isinstance(i, int) or i >= 3:
                            wait(act, entry_ready, entries_before(i - 1) + sums_at)
                        act.activation(o_sb[:, :], o_bank[:, :], ACT.Copy).then_inc(o_copied, 1)
                    if now:
                        h, hs, kt = now
                        kn = keys_of(kt)
                        if not isinstance(h, int) or KT * h + kt >= RING:
                            wait(act, pv_done, h * KT + (kt - 2))
                        for half in range(2):
                            wait(act, score_ready, h * (2 * KT) + (2 * kt + half + 1))
                            act.activation(probs[0:kn, (kt + hs) % RING, half * HALF:(half + 1) * HALF],
                                           s_bank[half][0:kn, :], ACT.Exp).then_inc(exp_done, 1)

            iterations(act, body)

        @block.vector
        def _(dve):
            def piece(i, slot, what, n):
                t, c = divmod(what, NP)
                k0, kn = PIECES[c]
                dst = piece_max[:, slot, t, c:c + 1]
                wait(dve, entry_ready, entries_before(i) + (n + 1), apart=masked)
                if masked:
                    dve.tensor_tensor_reduce(junk[:, ring_of(i, n), 0:kn], bank_of(i, n)[:, 0:kn],
                                             mask_q[:, t, k0:k0 + kn], 1.0, -3.0e38, ALU.add, ALU.max, dst)\
                        .then_inc(entry_done, 1)
                else:
                    dve.tensor_reduce(dst, bank_of(i, n)[:, 0:kn], AX.X, ALU.max).then_inc(entry_done, 1)

            def split_max(i, prev, n):
                wait(dve, entry_ready, entries_before(i) + (n + 1))
                turned = bank_of(i, n)[0:QT, 0:P]
                dve.tensor_scalar(m_part[:, prev, 0], turned, -1.0, None, ALU.mult).then_inc(max_split, 1)
                wait(dve, max_split, (i - 1) * 3 + 1)
                dve.scalar_tensor_tensor(out=m_rest[:, :], in0=turned, scalar=-1.0, in1=m_part[:, prev, 0],
                                         op0=ALU.mult, op1=ALU.subtract).then_inc(max_split, 1)
                wait(dve, max_split, (i - 1) * 3 + 2)
                dve.tensor_copy(m_part[:, prev, 1], m_rest[:, :]).then_inc(entry_done, 1)
                wait(dve, entry_done, entries_before(i) + (n + 1))
                dve.tensor_tensor(m_part[:, prev, 2], m_rest[:, :], m_part[:, prev, 1], ALU.subtract)\
                    .then_inc(max_split, 1)

            def norm(i, slot, n):
                wait(dve, entry_ready, entries_before(i) + (n + 1))
                sums = bank_of(i, n)[:, :].rearrange("p (b c v) -> p b c v", b=NC, v=VW)
                dve.reciprocal(inv_sum[:, slot], sums[:, :, :, DK]).then_inc(inverted, 1)
                wait(dve, inverted, i - 1, apart=True)
                out = attn[:, :, bass.ds((i - 2) * DK, DK)].rearrange("p (c b) d -> p b c d", b=NC)
                dve.tensor_tensor(out, sums[:, :, :, 0:DK], inv_sum[:, slot].unsqueeze(3).to_broadcast([P, NC, NC, DK]),
                                  ALU.mult).then_inc(entry_done, 1)

            def body(i, slot, mx, tail, fresh):
                listed, many = entries(mx, tail, fresh)
                for step in listed:
                    for what, n in step:
                        if what == "maxima":
                            split_max(i, (slot - 1) % RING, n)
                        elif what == "sums":
                            norm(i, slot, n)
                        else:
                            piece(i, slot, what, n)
                if mx:
                    wait(dve, entry_done, entries_before(i) + many)
                    dve.tensor_reduce(row_max[:, slot, :], piece_max[:, slot], AX.X, ALU.max).then_inc(max_ready, 1)

            iterations(dve, body)


def enter_branch(nc):
    for eng in (nc.sync, nc.gpsimd, nc.tensor, nc.scalar, nc.vector):
        eng.nop(nofuse=True)


def attend_masked(nc, const, scratch, everything, attn, row_max, mask_all, window):
    start = nc.values_load(window[0:1, 0:1], min_val=0, max_val=S - WINDOW)
    fits = nc.values_load(window[0:1, 1:2], min_val=0, max_val=1)
    clear_semaphores(nc)
    with nc.If(fits == 1):
        enter_branch(nc)
        with ExitStack() as masks:
            keys = Keys(start, WINDOW, [(0, WINDOW)], 2, (0, 2))
            sm = Scope(nc, masks, "window")
            mask_q, mask_k = sm.sb("mask_q", [P, QT, keys.S], BF16), sm.sb("mask_k", [P, keys.KT, T], BF16)
            prepare_mask(nc, const, keys, mask_all, mask_q, mask_k)
            attend(nc, const, scratch, 0, keys, attn, row_max, mask_q, mask_k)
    with nc.Else():
        enter_branch(nc)
        with ExitStack() as masks:
            sm = Scope(nc, masks, "everything")
            mask_k = sm.sb("mask_k", [P, KT, T], BF16)
            prepare_mask(nc, const, everything, mask_all, mask_all, mask_k)
            attend(nc, const, scratch, 0, everything, attn, row_max, mask_all, mask_k)
    clear_semaphores(nc)


def project_out(nc, const, l, attn, row_max, x_src, x_now, stats):
    with ExitStack() as ctx:
        sc = Scope(nc, ctx, f"out{l}")
        x_in = x_now if x_src is None else sc.sb("x_in", [P, QT, D], F32)
        a_t = sc.sb("a_t", [P, DB, T], F32)
        biased = sc.sb("biased", [P, 2, D], F32)
        lost = sc.sb("lost", [P, 3, QT], F32)
        t_bank = [sc.ps(f"t_bank{n}", [P, CH], F32) for n in range(4)]
        y_bank = [sc.ps(f"y_bank{n}", [P, D], F32) for n in range(4)]
        landed = [sc.sem(f"landed{n}") for n in range(4)]
        marked, turned = sc.sem("marked"), sc.sem("turned")
        copied = sc.sem("copied")
        ready, with_bias, added, counted = sc.sem("ready"), sc.sem("with_bias"), sc.sem("added"), sc.sem("counted")
        block = ctx.enter_context(nc.Block())
        last_head = (H - 1) % RING

        @block.sync
        def _(sp):
            if x_src is not None:
                for n in range(4):
                    sp.dma_start(x_in[:, 4 * n:4 * n + 4], x_src.rearrange("(t p) d -> p t d", p=P)[:, 4 * n:4 * n + 4])\
                        .then_inc(landed[n], 16)

        @block.tensor
        def _(pe):
            def turn(n):
                if n >= 4:
                    pe.wait_ge(copied, n - 3)
                for t in (2 * n, 2 * n + 1):
                    for b in range(DB):
                        last = pe.transpose(t_bank[n % 4][:, ((t % 2) * DB + b) * P:((t % 2) * DB + b + 1) * P],
                                            attn[:, t, b * P:(b + 1) * P], const["ident"][:, :])
                last.then_inc(turned, 1)

            turn(0)
            for n in range(QT // 2):
                if n + 1 < QT // 2:
                    turn(n + 1)
                pe.wait_ge(copied, n + 1)
                for t in (2 * n, 2 * n + 1):
                    if t >= 4:
                        pe.wait_ge(with_bias, t - 3)
                    for b in range(DB):
                        last = pe.matmul(y_bank[t % 4][:, :], a_t[:, b, t * P:(t + 1) * P], const["wo_t"][:, l, b],
                                         start=(b == 0), stop=(b == DB - 1))
                    last.then_inc(ready, 1)

        @block.scalar
        def _(act):
            for n in range(QT // 2):
                act.wait_ge(turned, n + 1)
                act.activation(a_t[:, :, 2 * n * P:2 * (n + 1) * P].rearrange("p b (t q) -> p t b q", t=2),
                               t_bank[n % 4][:, :].rearrange("p (t b q) -> p t b q", t=2, b=DB), ACT.Copy)\
                    .then_inc(copied, 1)

        @block.vector
        def _(dve):
            if l == 0:
                dve.tensor_scalar(lost[:, 0], row_max[:, last_head], NEG / 2, 3.0e38, ALU.is_lt, ALU.mult)\
                    .then_inc(marked, 1)
                dve.wait_ge(marked, 1)
                dve.tensor_scalar(lost[:, 1], lost[:, 0], 3.0e38, None, ALU.mult).then_inc(marked, 1)
                dve.wait_ge(marked, 2)
                dve.tensor_tensor(lost[:, 2], lost[:, 1], lost[:, 1], ALU.subtract).then_inc(marked, 1)
            else:
                dve.memset(lost[:, 2], 0.0).then_inc(marked, 3)
            dve.wait_ge(marked, 3)
            for t in range(QT):
                dve.wait_ge(ready, t + 1)
                if x_src is not None and t % 4 == 0:
                    dve.wait_ge(landed[t // 4], 16)
                dve.scalar_tensor_tensor(out=biased[:, t % 2], in0=y_bank[t % 4][:, :], scalar=lost[:, 2, t:t + 1],
                                         in1=const["bo"][:, l], op0=ALU.add, op1=ALU.add).then_inc(with_bias, 1)
                dve.wait_ge(with_bias, t + 1)
                dve.scalar_tensor_tensor(out=x_now[:, t], in0=biased[:, t % 2], scalar=const["gates"][:, l:l + 1],
                                         in1=x_in[:, t], op0=ALU.mult, op1=ALU.add).then_inc(added, 1)
                dve.wait_ge(added, t + 1)
                dve.bn_stats(stats[:, t], x_now[:, t]).then_inc(counted, 1)


class Moe:

    def __init__(self, l):
        self.l = l
        self.F, self.FW = (1024, 128) if l == 0 else (192, 96)
        self.FT = self.F // self.FW
        self.HW = min(CH, self.F)
        self.HV = self.F // self.HW
        self.K = l + 1
        self.NS = (self.K * T + E * (P - 1)) // P
        self.pre = f"L{l}_ffn_"
        self.up = [("w1s", "W1"), ("w2s", "W2")] if l == 0 else [("Wg_s", "Wg"), ("Wu_s", "Wu")]
        self.down = ("w3s", "W3") if l == 0 else ("Wd_s", "Wd")
        self.router = "Wg" if l == 0 else "W_gate_router"
        self.func = ACT.Gelu if l == 0 else ACT.Silu


def route_and_share(nc, io, const, scratch, m, x_nt, x_n, acc, place, weight, slot_expert, resident=None):
    l, F, FW, FT, NS, K = m.l, m.F, m.FW, m.FT, m.NS, m.K
    with ExitStack() as ctx:
        sc = Scope(nc, ctx, f"share{l}")
        w_up = sc.sb("w_up", [P, 2, DB, F], F32)
        w_dn = sc.sb("w_dn", [FW, FT, D], F32)
        w_rt = sc.sb("w_rt", [P, DB, E], F32)
        bias = sc.sb("bias", [P, E], F32)
        scores = sc.sb("scores", [P, QT, E], F32)
        biased = sc.sb("biased", [P, QT, E], F32)
        behind = sc.sb("behind", [P, QT, E], F32)
        picked = sc.sb("picked", [P, K, QT, E], F32)
        chosen = sc.sb("chosen", [P, QT, E], F32)
        best = sc.sb("best", [P, 4, QT], F32)
        sums = sc.sb("sums", [P, 2, QT, E], F32)
        total = sc.sb("total", [P, QT, E], F32)
        count = sc.sb("count", [P, E], F32)
        over = sc.sb("over", [P, E, QT], F32)
        slots = sc.sb("slots", [P, E], F32)
        ends = sc.sb("ends", [P, 2, E], F32)
        start = sc.sb("start", [P, E], F32)
        row = sc.sb("row", [P, QT, E], F32)
        mine = sc.sb("mine", [P, K, QT, E], F32)
        row_k = sc.sb("row_k", [P, K, QT], F32)
        passed = sc.sb("passed", [P, NS, E], F32)
        expert = sc.sb("expert", [P, NS], F32)
        g_act = sc.sb("g_act", [FW, 2, CH], F32)
        hid = sc.sb("hid", [FW, 2, FT, CH], F32)
        a_bank = [sc.ps(f"a_bank{n}", [P, CH], F32) for n in range(2)]
        b_bank = [sc.ps(f"b_bank{n}", [P, CH], F32) for n in range(2)]
        y_bank = [sc.ps(f"y_bank{n}", [P, D], F32) for n in range(2)]
        r_bank = sc.ps("r_bank", [P, QT, E], F32)
        c_bank = sc.ps("c_bank", [P, 2, QT, E], F32)
        router_in, w_in = sc.sem("router_in"), sc.sem("w_in")
        logits_ready, logits_act, step_done = sc.sem("logits_ready"), sc.sem("logits_act"), sc.sem("step_done")
        chosen_ready, ranked, placed = sc.sem("chosen_ready"), sc.sem("ranked"), sc.sem("placed")
        gate_up = [sc.sem("gate_ready"), sc.sem("up_ready")]
        activated, hid_ready = sc.sem("activated"), sc.sem("hid_ready")
        y_ready, y_copied = sc.sem("y_ready"), sc.sem("y_copied")
        resident_in = sc.sem("resident_in")
        scattered = const["scattered"][l]
        block = ctx.enter_context(nc.Block())

        @block.sync
        def _(sp):
            sp.dma_start(w_rt[:, :, :], io[m.pre + m.router].rearrange("(b p) e -> p b e", p=P)).then_inc(router_in, 16)
            if l == 1:
                sp.dma_start(bias[:, :], io[m.pre + "expert_bias"].rearrange("(a n) -> a n", a=1).broadcast_to([P, E]))\
                    .then_inc(router_in, 16)
            for n in range(2):
                sp.dma_start(w_up[:, n], io[m.pre + m.up[n][0]].rearrange("(b p) f -> p b f", p=P)).then_inc(w_in, 16)
            sp.dma_start(w_dn[:, :, :], io[m.pre + m.down[0]].rearrange("(b p) f -> p b f", p=FW)).then_inc(w_in, 16)
            if resident:
                for e in range(E):
                    for n in range(2):
                        sp.dma_start(resident["up"][:, e, :, n], io[m.pre + m.up[n][1]][e].rearrange("(b p) f -> p b f", p=P))\
                            .then_inc(resident_in, 16)
                    sp.dma_start(resident["down"][:, e], io[m.pre + m.down[1]][e].rearrange("(b p) d -> p b d", p=FW))\
                        .then_inc(resident_in, 16)
                sp.wait_ge(resident_in, 16 * 3 * E)

        @block.gpsimd
        def _(pool):
            for k in range(K):
                pool.wait_ge(placed, k + 1)
                for t in range(QT):
                    pool.indirect_dma_start(scratch["sorted"][l][:, :],
                                            bass.IndirectOffsetOnAxis(ap=place[:, k, t:t + 1], axis=0),
                                            x_n[:, t], None).then_inc(scattered, 16)
            pool.wait_ge(scattered, 16 * K * QT)

        @block.tensor
        def _(pe):
            def rank():
                pe.wait_ge(chosen_ready, 1)
                pe.matmul(c_bank[:, 0].rearrange("p t e -> p (t e)"), const["earlier"][:, :],
                          chosen[:, :, :].rearrange("p t e -> p (t e)"), start=True, stop=True)
                pe.matmul(c_bank[:, 1].rearrange("p t e -> p (t e)"), const["ones"][:, :],
                          chosen[:, :, :].rearrange("p t e -> p (t e)"), start=True, stop=True).then_inc(ranked, 1)

            pe.wait_ge(router_in, 16 * (l + 1))
            for t in range(QT):
                for b in range(DB):
                    last = pe.matmul(r_bank[:, t], x_nt[:, b, t * P:(t + 1) * P], w_rt[:, b], start=(b == 0),
                                     stop=(b == DB - 1))
            last.then_inc(logits_ready, 1)
            pe.wait_ge(w_in, 48)
            for c in range(NC):
                for f in range(FT):
                    n = c * FT + f
                    for which, bank, read in ((0, a_bank, activated), (1, b_bank, hid_ready)):
                        if n >= 2:
                            pe.wait_ge(read, n - 1)
                        for b in range(DB):
                            last = pe.matmul(bank[n % 2][0:FW, :], w_up[:, which, b, f * FW:(f + 1) * FW],
                                             x_nt[:, b, c * CH:(c + 1) * CH], start=(b == 0), stop=(b == DB - 1))
                        last.then_inc(gate_up[which], 1)
                if c == 0:
                    rank()
                for t in range(CH // P):
                    n = c * (CH // P) + t
                    pe.wait_ge(hid_ready, FT * (c + 1))
                    if n >= 2:
                        pe.wait_ge(y_copied, n - 1)
                    for f in range(FT):
                        last = pe.matmul(y_bank[n % 2][:, :], hid[:, c % 2, f, t * P:(t + 1) * P], w_dn[:, f],
                                         start=(f == 0), stop=(f == FT - 1))
                    last.then_inc(y_ready, 1)

        @block.scalar
        def _(act):
            act.wait_ge(logits_ready, 1)
            act.activation(scores[:, :, :], r_bank[:, :, :], ACT.Copy if l == 0 else ACT.Sigmoid).then_inc(logits_act, 1)
            for c in range(NC):
                for f in range(FT):
                    n = c * FT + f
                    act.wait_ge(gate_up[0], n + 1)
                    if n >= 2:
                        act.wait_ge(hid_ready, n - 1)
                    act.activation(g_act[:, n % 2], a_bank[n % 2][0:FW, :], m.func).then_inc(activated, 1)
                for n in range(c * (CH // P), (c + 1) * (CH // P)):
                    act.wait_ge(y_ready, n + 1)
                    act.activation(acc[:, n], y_bank[n % 2][:, :], ACT.Copy).then_inc(y_copied, 1)

        @block.vector
        def _(dve):
            step = [0]

            def then(ins):
                ins.then_inc(step_done, 1)
                step[0] += 1
                dve.wait_ge(step_done, step[0])

            wide = [P, QT, E]
            number = const["number"]
            eno = number[:, 0:E].unsqueeze(1).to_broadcast(wide)

            def first_best(vals, k):
                then(dve.tensor_reduce(best[:, 0], vals, AX.X, ALU.max))
                then(dve.tensor_tensor(behind[:, :, :], vals, best[:, 0].unsqueeze(2).to_broadcast(wide), ALU.is_lt))
                then(dve.scalar_tensor_tensor(out=behind[:, :, :], in0=behind[:, :, :], scalar=float(2 * E), in1=eno,
                                              op0=ALU.mult, op1=ALU.add))
                then(dve.tensor_reduce(best[:, 1], behind[:, :, :], AX.X, ALU.min))
                then(dve.tensor_tensor(picked[:, k], eno, best[:, 1].unsqueeze(2).to_broadcast(wide), ALU.is_equal))

            dve.wait_ge(logits_act, 1)
            if l == 0:
                first_best(scores[:, :, :], 0)
                dve.tensor_copy(chosen[:, :, :], picked[:, 0]).then_inc(chosen_ready, 1)
            else:
                dve.wait_ge(router_in, 32)
                then(dve.tensor_tensor(biased[:, :, :], scores[:, :, :], bias[:, :].unsqueeze(1).to_broadcast(wide),
                                       ALU.add))
                first_best(biased[:, :, :], 0)
                then(dve.scalar_tensor_tensor(out=biased[:, :, :], in0=picked[:, 0], scalar=-1.0e30,
                                              in1=biased[:, :, :], op0=ALU.mult, op1=ALU.add))
                first_best(biased[:, :, :], 1)
                dve.tensor_tensor(chosen[:, :, :], picked[:, 0], picked[:, 1], ALU.add).then_inc(chosen_ready, 1)
                for k in range(K):
                    then(dve.tensor_tensor(mine[:, k], picked[:, k], scores[:, :, :], ALU.mult))
                    then(dve.tensor_reduce(row_k[:, k], mine[:, k], AX.X, ALU.add))
                then(dve.tensor_tensor(best[:, 2], row_k[:, 0], row_k[:, 1], ALU.add))
                then(dve.tensor_scalar(best[:, 2], best[:, 2], 1.0e-20, None, ALU.add))
                then(dve.reciprocal(best[:, 3], best[:, 2]))
                for k in range(K):
                    then(dve.tensor_tensor(weight[:, k], row_k[:, k], best[:, 3], ALU.mult))

            def place_tokens():
                dve.wait_ge(ranked, 1)
                then(dve.tensor_copy(total[:, :, :], c_bank[:, 1]))
                src, now = total[:, :, :], 0
                d = 1
                while d < QT:
                    dst = sums[:, now]
                    then(dve.tensor_copy(dst[:, 0:d], src[:, 0:d]))
                    then(dve.tensor_tensor(dst[:, d:QT], src[:, d:QT], src[:, 0:QT - d], ALU.add))
                    src, now, d = dst, 1 - now, 2 * d
                then(dve.tensor_scalar(count[:, :], src[:, QT - 1], 1.0 / P, None, ALU.mult))
                then(dve.tensor_tensor(over[:, :, :], count[:, :].unsqueeze(2).to_broadcast([P, E, QT]),
                                       number[:, 0:QT].unsqueeze(1).to_broadcast([P, E, QT]), ALU.is_gt))
                then(dve.tensor_reduce(slots[:, :], over[:, :, :], AX.X, ALU.add))
                end, k, d = slots[:, :], 0, 1
                while d < E:
                    dst = ends[:, k]
                    then(dve.tensor_copy(dst[:, 0:d], end[:, 0:d]))
                    then(dve.tensor_tensor(dst[:, d:E], end[:, d:E], end[:, 0:E - d], ALU.add))
                    end, k, d = dst, 1 - k, 2 * d
                then(dve.tensor_tensor(start[:, :], end, slots[:, :], ALU.subtract))
                then(dve.tensor_scalar(start[:, :], start[:, :], float(P), None, ALU.mult))
                then(dve.tensor_tensor(row[:, :, :], src, total[:, :, :], ALU.subtract))
                then(dve.tensor_tensor(row[:, :, :], row[:, :, :], start[:, :].unsqueeze(1).to_broadcast(wide), ALU.add))
                then(dve.tensor_tensor(row[:, :, :], c_bank[:, 0], row[:, :, :], ALU.add))
                for k in range(K):
                    then(dve.tensor_tensor(mine[:, k], picked[:, k], row[:, :, :], ALU.mult))
                    then(dve.tensor_reduce(row_k[:, k], mine[:, k], AX.X, ALU.add))
                    dve.tensor_copy(place[:, k], row_k[:, k]).then_inc(placed, 1)
                then(dve.tensor_tensor(passed[:, :, :], end.unsqueeze(1).to_broadcast([P, NS, E]),
                                       number[:, 0:NS].unsqueeze(2).to_broadcast([P, NS, E]), ALU.is_le))
                then(dve.tensor_reduce(expert[:, :], passed[:, :, :], AX.X, ALU.add))
                then(dve.tensor_scalar(expert[:, :], expert[:, :], float(E - 1), None, ALU.min))
                then(dve.tensor_copy(slot_expert[:, :], expert[:, :]))

            for c in range(NC):
                for f in range(FT):
                    n = c * FT + f
                    dve.wait_ge(activated, n + 1)
                    dve.wait_ge(gate_up[1], n + 1)
                    if f == 0 and c >= 2:
                        dve.wait_ge(y_ready, (CH // P) * (c - 1))
                    dve.tensor_tensor(hid[:, c % 2, f], b_bank[n % 2][0:FW, :], g_act[:, n % 2], ALU.mult)\
                        .then_inc(hid_ready, 1)
                if c == 0:
                    place_tokens()


def run_slots(nc, io, const, scratch, m, slot_expert):
    l, F, FW, FT, HW, HV, NS = m.l, m.F, m.FW, m.FT, m.HW, m.HV, m.NS
    HB = -(-FT * P // CH)
    PB = FT // HB
    with ExitStack() as ctx:
        sc = Scope(nc, ctx, f"slots{l}")
        w_up = sc.sb("w_up", [P, 2, 2, DB, F], F32)
        w_dn = sc.sb("w_dn", [FW, 2, FT, D], F32)
        rows = sc.sb("rows", [P, 2, D], F32)
        x_t = sc.sb("x_t", [P, 2, DB, P], F32)
        g_act = sc.sb("g_act", [P, 2, HW], F32)
        hid = sc.sb("hid", [P, 2, F], F32)
        hid_t = sc.sb("hid_t", [FW, 2, FT, P], F32)
        y_sb = sc.sb("y_sb", [P, 2, D], F32)
        a_bank = [sc.ps(f"a_bank{n}", [P, CH], F32) for n in range(2)]
        b_bank = [sc.ps(f"b_bank{n}", [P, CH], F32) for n in range(2)]
        h_bank = [sc.ps(f"h_bank{n}", [P, CH], F32) for n in range(HB)]
        x_bank = sc.ps("x_bank", [P, CH], F32)
        y_bank = sc.ps("y_bank", [P, CH], F32)
        up_in = [sc.sem("up_in0"), sc.sem("up_in1")]
        down_in = [sc.sem("down_in0"), sc.sem("down_in1")]
        rows_in = [sc.sem("rows_in0"), sc.sem("rows_in1")]
        y_stored = [sc.sem("y_stored0"), sc.sem("y_stored1")]
        x_turned, x_copied = sc.sem("x_turned"), sc.sem("x_copied")
        gate_ready, up_ready = sc.sem("gate_ready"), sc.sem("up_ready")
        activated, hid_ready = sc.sem("activated"), sc.sem("hid_ready")
        h_turned = sc.sem("h_turned")
        h_copied = [sc.sem(f"h_copied{n}") for n in range(HB)]
        y_ready, y_copied = sc.sem("y_ready"), sc.sem("y_copied")
        block = ctx.enter_context(nc.Block())
        assert NS % 2 == 1
        first = lambda s, n=1: isinstance(s, int) and s < n

        def steps(eng, body):
            for s in range(3):
                body(s, s % 2, True, s > 0)
            with eng.Fori(3, NS - 1, 2) as j:
                for u in range(2):
                    body(j + u, (3 + u) % 2, True, True)
            body(NS, NS % 2, False, True)

        @block.sync
        def _(sp):
            def expert_of(s):
                return bass.ds(sp.value_load(slot_expert[0:1, bass.ds(s, 1)], min_val=0, max_val=E - 1), 1)

            def load_rows(s, slot):
                sp.dma_start(rows[:, slot], scratch["sorted"][l][bass.ds(s * P, P), :]).then_inc(rows_in[slot], 16)

            def load_up(s, slot):
                e = expert_of(s)
                for n in range(2):
                    sp.dma_start(w_up[:, slot, n], io[m.pre + m.up[n][1]][e].rearrange("a (b p) f -> p (a b) f", p=P))\
                        .then_inc(up_in[slot], 16)

            def load_down(s, slot):
                sp.dma_start(w_dn[:, slot], io[m.pre + m.down[1]][expert_of(s)]
                             .rearrange("a (b p) f -> p (a b) f", p=FW)).then_inc(down_in[slot], 16)

            def store(s, slot):
                sp.dma_start(scratch["back"][l][bass.ds(s * P, P), :], y_sb[:, slot]).then_inc(y_stored[slot], 16)

            def body(s, slot):
                if not first(s, 2):
                    wait(sp, x_turned, s - 1, apart=True)
                load_rows(s, slot)
                if not first(s, 2):
                    wait(sp, up_ready, s * HV - HV, apart=True)
                load_up(s, slot)
                if not first(s, 3):
                    wait(sp, y_copied, s - 2, apart=True)
                    store(s - 3, 1 - slot)
                if not first(s):
                    load_down(s - 1, 1 - slot)

            for s in range(3):
                body(s, s % 2)
            with sp.Fori(3, NS - 1, 2) as j:
                for u in range(2):
                    body(j + u, (3 + u) % 2)
            for s in range(NS - 3, NS):
                wait(sp, y_copied, s + 1)
                store(s, s % 2)
                if s == NS - 3:
                    load_down(NS - 1, (NS - 1) % 2)
            for n in range(2):
                sp.wait_ge(y_stored[n], 16 * ((NS + 1 - n) // 2))

        @block.tensor
        def _(pe):
            def turn_rows(s, slot):
                wait(pe, rows_in[slot], (s - slot) * 8 + 16)
                if not first(s):
                    wait(pe, x_copied, s)
                for b in range(DB):
                    last = pe.transpose(x_bank[:, b * P:(b + 1) * P], rows[:, slot, b * P:(b + 1) * P],
                                        const["ident"][:, :])
                last.then_inc(x_turned, 1)

            def go_up(s, slot, half):
                k = half if HV == 2 else slot
                for which, bank, used, ready in ((0, a_bank, activated, gate_ready), (1, b_bank, hid_ready, up_ready)):
                    if not (first(s) or (HV == 1 and first(s, 2))):
                        wait(pe, used, s * HV + (half - 1))
                    for b in range(DB):
                        last = pe.matmul(bank[k][:, 0:HW], x_t[:, slot, b],
                                         w_up[:, slot, which, b, half * HW:(half + 1) * HW],
                                         start=(b == 0), stop=(b == DB - 1))
                    last.then_inc(ready, 1)

            def turn_hidden(s, slot):
                wait(pe, hid_ready, s * HV + HV)
                if not first(s):
                    for n in range(HB):
                        wait(pe, h_copied[n], s)
                for f in range(FT):
                    last = pe.transpose(h_bank[f // PB][0:FW, (f % PB) * P:(f % PB + 1) * P],
                                        hid[:, slot, f * FW:(f + 1) * FW], const["ident"][:, :])
                last.then_inc(h_turned, 1)

            def go_down(s, slot):
                wait(pe, down_in[slot], (s - slot) * 8 + 16)
                for n in range(HB):
                    wait(pe, h_copied[n], s + 1)
                if not first(s):
                    wait(pe, y_copied, s)
                for f in range(FT):
                    last = pe.matmul(y_bank[:, 0:D], hid_t[:, slot, f], w_dn[:, slot, f], start=(f == 0),
                                     stop=(f == FT - 1))
                last.then_inc(y_ready, 1)

            def body(s, slot, up, down):
                if up:
                    wait(pe, up_in[slot], (s - slot) * 16 + 32)
                    wait(pe, x_copied, s + 1)
                    go_up(s, slot, 0)
                    if not (isinstance(s, int) and s == NS - 1):
                        turn_rows(s + 1, 1 - slot)
                if down and HV == 2:
                    turn_hidden(s - 1, 1 - slot)
                if up and HV == 2:
                    go_up(s, slot, 1)
                if down:
                    if HV == 1:
                        turn_hidden(s - 1, 1 - slot)
                    go_down(s - 1, 1 - slot)

            turn_rows(0, 0)
            for s in range(3):
                body(s, s % 2, True, s > 0)
            with pe.Fori(3, NS - 3, 2) as j:
                for u in range(2):
                    body(j + u, (3 + u) % 2, True, True)
            for s in range(NS - 2, NS):
                body(s, s % 2, True, True)
            body(NS, NS % 2, False, True)

        def copy_rows(act, s, slot):
            wait(act, x_turned, s + 1)
            if not first(s, 2):
                wait(act, up_ready, s * HV - HV)
            act.activation(x_t[:, slot], x_bank[:, 0:DB * P].rearrange("p (b q) -> p b q", b=DB), ACT.Copy)\
                .then_inc(x_copied, 1)

        def copy_hidden(eng, copy, n, s, slot):
            wait(eng, h_turned, s + 1)
            if not first(s, 2):
                wait(eng, y_ready, s - 1)
            copy(hid_t[:, slot, n * PB:(n + 1) * PB],
                 h_bank[n][0:FW, 0:PB * P].rearrange("p (f q) -> p f q", f=PB)).then_inc(h_copied[n], 1)

        @block.scalar
        def _(act):
            def copy(out, in_):
                return act.activation(out, in_, ACT.Copy)

            def gate(s, slot, half):
                k = half if HV == 2 else slot
                wait(act, gate_ready, s * HV + (half + 1))
                if not (first(s) or (HV == 1 and first(s, 2))):
                    wait(act, hid_ready, s * HV + (half - 1))
                act.activation(g_act[:, k], a_bank[k][:, 0:HW], m.func).then_inc(activated, 1)

            def body(s, slot, up, down):
                if up:
                    gate(s, slot, 0)
                    if not (isinstance(s, int) and s == NS - 1):
                        copy_rows(act, s + 1, 1 - slot)
                if down:
                    copy_hidden(act, copy, 0, s - 1, 1 - slot)
                if up and HV == 2:
                    gate(s, slot, 1)

            copy_rows(act, 0, 0)
            for s in range(3):
                body(s, s % 2, True, s > 0)
            with act.Fori(3, NS - 3, 2) as j:
                for u in range(2):
                    body(j + u, (3 + u) % 2, True, True)
            for s in range(NS - 2, NS):
                body(s, s % 2, True, True)
            body(NS, NS % 2, False, True)

        @block.vector
        def _(dve):
            def hidden(s, slot, half):
                k = half if HV == 2 else slot
                wait(dve, activated, s * HV + (half + 1))
                wait(dve, up_ready, s * HV + (half + 1))
                if not first(s, 2):
                    wait(dve, h_turned, s - 1)
                dve.tensor_tensor(hid[:, slot, half * HW:(half + 1) * HW], b_bank[k][:, 0:HW], g_act[:, k], ALU.mult)\
                    .then_inc(hid_ready, 1)

            def result(s, slot):
                wait(dve, y_ready, s + 1)
                if not first(s, 2):
                    wait(dve, y_stored[slot], (s - slot) * 8)
                dve.tensor_copy(y_sb[:, slot], y_bank[:, 0:D]).then_inc(y_copied, 1)

            def body(s, slot, up, down):
                if up:
                    hidden(s, slot, 0)
                if down and HB == 2:
                    copy_hidden(dve, dve.tensor_copy, 1, s - 1, 1 - slot)
                if up and HV == 2:
                    hidden(s, slot, 1)
                if down:
                    result(s - 1, 1 - slot)

            steps(dve, body)


def run_resident_slots(nc, const, scratch, m, slot_expert, resident):
    l, F, FW, FT, NS = m.l, m.F, m.FW, m.FT, m.NS
    HEAD, GROUP = 5, 3
    with ExitStack() as ctx:
        sc = Scope(nc, ctx, f"slots{l}")
        rows = sc.sb("rows", [P, NS, D], F32)
        stage = sc.sb("stage", [P, 2, D], F32)
        x_t = sc.sb("x_t", [P, 2, DB, P], F32)
        g_act = sc.sb("g_act", [P, 2, F], F32)
        hid = sc.sb("hid", [P, 2, F], F32)
        hid_t = sc.sb("hid_t", [FW, 2, FT, P], F32)
        y = sc.sb("y", [P, NS, D], F32)
        x_bank, u_bank, h_bank, y_bank = ([sc.ps(f"{n}_bank{k}", [P, CH], F32) for k in range(2)] for n in "xuhy")
        head_in, rest_in, staged = sc.sem("head_in"), sc.sem("rest_in"), sc.sem("staged")
        x_turned, x_copied = sc.sem("x_turned"), sc.sem("x_copied")
        up_ready, activated, hid_ready = sc.sem("up_ready"), sc.sem("activated"), sc.sem("hid_ready")
        h_turned, h_copied = sc.sem("h_turned"), sc.sem("h_copied")
        y_ready, y_copied, y_stored = sc.sem("y_ready"), sc.sem("y_copied"), sc.sem("y_stored")
        block = ctx.enter_context(nc.Block())
        assert NS % 2 == 1 and NS % GROUP == 0

        def steps(eng, body):
            for s in range(3):
                body(s, s % 2)
            with eng.Fori(3, NS - 3, 2) as j:
                for u in range(2):
                    body(j + u, (3 + u) % 2)
            for s in range(NS - 2, NS + 2):
                body(s, s % 2)

        def is_slot(s):
            return not isinstance(s, int) or 0 <= s < NS

        def again(s):
            return not isinstance(s, int) or s >= 2

        @block.sync
        def _(sp):
            tiles = scratch["sorted"][l].rearrange("(t p) d -> p t d", p=P)
            sp.dma_start(rows[:, 0:HEAD], tiles[:, 0:HEAD]).then_inc(head_in, 16)
            for a in range(HEAD, NS, 12):
                b = min(NS, a + 12)
                sp.dma_start(rows[:, a:b], tiles[:, a:b]).then_inc(rest_in, 16)
            with sp.Fori(0, NS - GROUP + 1, GROUP) as j:
                wait(sp, y_copied, j + GROUP, apart=True)
                sp.dma_start(scratch["back"][l][bass.ds(j * P, GROUP * P), :].rearrange("(t p) d -> p t d", p=P),
                             y[:, bass.ds(j, GROUP)]).then_inc(y_stored, 16)
            sp.wait_ge(y_stored, 16 * (NS // GROUP))

        @block.gpsimd
        def _(pool):
            def body(s, k):
                if again(s):
                    wait(pool, x_turned, s - 1, apart=True)
                pool.tensor_copy(stage[:, k], rows[:, bass.ds(s, 1)].rearrange("p a d -> p (a d)")).then_inc(staged, 1)

            pool.wait_ge(head_in, 16)
            for s in range(HEAD):
                body(s, s % 2)
            pool.wait_ge(rest_in, 16 * -(-(NS - HEAD) // 12))
            with pool.Fori(HEAD, NS - 1, 2) as j:
                for u in range(2):
                    body(j + u, (HEAD + u) % 2)

        @block.tensor
        def _(pe):
            def expert_of(s):
                return bass.ds(pe.value_load(slot_expert[0:1, bass.ds(s, 1)], min_val=0, max_val=E - 1), 1)

            def turn_rows(s, k):
                wait(pe, staged, s + 1)
                if again(s):
                    wait(pe, x_copied, s - 1)
                for b in range(DB):
                    last = pe.transpose(x_bank[k][:, b * P:(b + 1) * P], stage[:, k, b * P:(b + 1) * P],
                                        const["ident"][:, :])
                last.then_inc(x_turned, 1)

            def go_up(s, k, e):
                wait(pe, x_copied, s + 1, apart=True)
                if again(s):
                    wait(pe, hid_ready, s - 1, apart=True)
                for b in range(DB):
                    last = pe.matmul(u_bank[k][:, 0:2 * F], x_t[:, k, b],
                                     resident["up"][:, e, b].rearrange("p a n f -> p (a n f)"), start=(b == 0),
                                     stop=(b == DB - 1))
                last.then_inc(up_ready, 1)

            def turn_hidden(s, k):
                wait(pe, hid_ready, s + 1)
                if again(s):
                    wait(pe, h_copied, s - 1)
                for f in range(FT):
                    last = pe.transpose(h_bank[k][0:FW, f * P:(f + 1) * P], hid[:, k, f * FW:(f + 1) * FW],
                                        const["ident"][:, :])
                last.then_inc(h_turned, 1)

            def go_down(s, k, e):
                wait(pe, h_copied, s + 1, apart=True)
                if again(s):
                    wait(pe, y_copied, s - 1, apart=True)
                for f in range(FT):
                    last = pe.matmul(y_bank[k][:, 0:D], hid_t[:, k, f],
                                     resident["down"][:, e, f].rearrange("p a d -> p (a d)"), start=(f == 0),
                                     stop=(f == FT - 1))
                last.then_inc(y_ready, 1)

            def body(s, k):
                up = expert_of(s) if is_slot(s) else None
                down = expert_of(s - 2) if is_slot(s - 2) else None
                if is_slot(s):
                    go_up(s, k, up)
                if is_slot(s + 1):
                    turn_rows(s + 1, 1 - k)
                if is_slot(s - 1):
                    turn_hidden(s - 1, 1 - k)
                if is_slot(s - 2):
                    go_down(s - 2, k, down)

            turn_rows(0, 0)
            steps(pe, body)

        @block.scalar
        def _(act):
            def copy_rows(s, k):
                wait(act, x_turned, s + 1)
                if again(s):
                    wait(act, up_ready, s - 1)
                act.activation(x_t[:, k], x_bank[k][:, 0:DB * P].rearrange("p (b q) -> p b q", b=DB), ACT.Copy)\
                    .then_inc(x_copied, 1)

            def body(s, k):
                if is_slot(s):
                    wait(act, up_ready, s + 1)
                    if again(s):
                        wait(act, hid_ready, s - 1)
                    act.activation(g_act[:, k], u_bank[k][:, 0:F], m.func).then_inc(activated, 1)
                if is_slot(s + 1):
                    copy_rows(s + 1, 1 - k)

            copy_rows(0, 0)
            steps(act, body)

        @block.vector
        def _(dve):
            def body(s, k):
                if is_slot(s):
                    wait(dve, activated, s + 1)
                    if again(s):
                        wait(dve, h_turned, s - 1)
                    dve.tensor_tensor(hid[:, k], u_bank[k][:, F:2 * F], g_act[:, k], ALU.mult).then_inc(hid_ready, 1)
                if is_slot(s - 1):
                    wait(dve, h_turned, s)
                    if again(s - 1):
                        wait(dve, y_ready, s - 2)
                    dve.tensor_copy(hid_t[:, 1 - k], h_bank[1 - k][0:FW, 0:FT * P].rearrange("p (f q) -> p f q", f=FT))\
                        .then_inc(h_copied, 1)
                if is_slot(s - 2):
                    wait(dve, y_ready, s - 1, apart=True)
                    dve.tensor_copy(y[:, bass.ds(s - 2, 1)].rearrange("p a d -> p (a d)"), y_bank[k][:, 0:D])\
                        .then_inc(y_copied, 1)

            steps(dve, body)


def collect(nc, const, scratch, m, acc, place, weight, x_now, stats, x_dst):
    l, K = m.l, m.K
    with ExitStack() as ctx:
        sc = Scope(nc, ctx, f"collect{l}")
        back = sc.sb("back", [P, K, QT, D], F32)
        summed, final, stored, counted = sc.sem("summed"), sc.sem("final"), sc.sem("stored"), sc.sem("counted")
        gathered = const["gathered"][l]
        block = ctx.enter_context(nc.Block())

        @block.gpsimd
        def _(pool):
            for t in range(QT):
                for k in range(K):
                    pool.indirect_dma_start(back[:, k, t], None, scratch["back"][l][:, :],
                                            bass.IndirectOffsetOnAxis(ap=place[:, k, t:t + 1], axis=0))\
                        .then_inc(gathered[t], 16)
            for t in range(QT):
                pool.wait_ge(gathered[t], 16 * K)

        @block.sync
        def _(sp):
            if x_dst is not None:
                for n in range(4):
                    sp.wait_ge(final, 4 * (n + 1))
                    sp.dma_start(x_dst.rearrange("(t p) d -> p t d", p=P)[:, 4 * n:4 * n + 4],
                                 x_now[:, 4 * n:4 * n + 4]).then_inc(stored, 16)
                sp.wait_ge(stored, 64)

        @block.vector
        def _(dve):
            for t in range(QT):
                dve.wait_ge(gathered[t], 16 * K)
                for k in range(K):
                    if l == 0:
                        dve.tensor_tensor(acc[:, t], acc[:, t], back[:, k, t], ALU.add).then_inc(summed, 1)
                    else:
                        dve.scalar_tensor_tensor(out=acc[:, t], in0=back[:, k, t], scalar=weight[:, k, t:t + 1],
                                                 in1=acc[:, t], op0=ALU.mult, op1=ALU.add).then_inc(summed, 1)
                    dve.wait_ge(summed, K * t + k + 1)
                dve.scalar_tensor_tensor(out=x_now[:, t], in0=acc[:, t], scalar=const["gates"][:, 2 + l:3 + l],
                                         in1=x_now[:, t], op0=ALU.mult, op1=ALU.add).then_inc(final, 1)
                if x_dst is None:
                    dve.wait_ge(final, t + 1)
                    dve.bn_stats(stats[:, t], x_now[:, t]).then_inc(counted, 1)


def flamingo_kernel(nc, io, out):
    Scope.used.clear()
    scratch = {
        "k": nc.dram_tensor("k_parts", [2, PART, D, S], BF16, kind="Internal").ap(),
        "q": nc.dram_tensor("q_parts", [PART, D, T], BF16, kind="Internal").ap(),
        "v": nc.dram_tensor("v_rows", [2, S, D], F32, kind="Internal").ap(),
        "sorted": [nc.dram_tensor(f"sorted{l}", [Moe(l).NS * P, D], F32, kind="Internal").ap() for l in range(2)],
        "back": [nc.dram_tensor(f"back{l}", [Moe(l).NS * P, D], F32, kind="Internal").ap() for l in range(2)],
    }
    with ExitStack() as ctx:
        sc = Scope(nc, ctx, "keep")
        const = {
            "ident": sc.sb("ident", [P, P], F32), "ident_bf": sc.sb("ident_bf", [P, P], BF16),
            "number": sc.sb("number", [P, Moe(1).NS], F32),
            "ones": sc.sb("ones", [P, P], F32), "zeros": sc.sb("zeros", [P, D], F32),
            "earlier": sc.sb("earlier", [P, P], F32),
            "scattered": [ctx.enter_context(nc.semaphore(f"scattered{l}")) for l in range(2)],
            "gathered": [[ctx.enter_context(nc.semaphore(f"gathered{l}_{t}")) for t in range(QT)] for l in range(2)],
            "gates": sc.sb("gates", [P, 4], F32),
            "wq_t": sc.sb("wq_t", [P, 2, DB, D], F32), "wo_t": sc.sb("wo_t", [P, 2, DB, D], F32),
            "bqk": sc.sb("bqk", [P, 4 * DB], F32),
            "bo": sc.sb("bo", [P, 2, D], F32),
        }
        x_now, stats = sc.sb("x_now", [P, QT, D], F32), sc.sb("stats", [P, QT, 6], F32)
        make_constants(nc, io, const)
        everything = Keys(0, S, PIECES, 4, (1, 2))
        for l in range(2):
            if l:
                clear_semaphores(nc)
            with ExitStack() as part:
                layer = Scope(nc, part, f"keep_a{l}")
                mask_all = unseen = window = None
                if l == 0:
                    mask_all, window = layer.sb("mask_all", [P, QT, S], BF16), layer.sb("window", [1, 2], I32)
                with ExitStack() as queries:
                    keep = Scope(nc, queries, f"keep_q{l}")
                    if l == 0:
                        unseen = keep.ps("unseen", [P, CH], F32)
                        prepare_context(nc, io, const, scratch, mask_all, unseen, x_now, stats)
                    x_nt, x_n = keep.sb("x_nt", [P, DB, T], F32), keep.sb("x_n", [P, QT, D], F32)
                    normalise(nc, const, f"norm_q{l}", x_now, stats, x_nt, x_n)
                    project_queries(nc, const, scratch, l, x_nt, unseen, window)
                attn = layer.sb("attn", [P, QT, D], F32) if l else x_now
                row_max = layer.sb("row_max", [P, RING, QT], F32)
                if l == 0:
                    attend_masked(nc, const, scratch, everything, attn, row_max, mask_all, window)
                else:
                    attend(nc, const, scratch, l, everything, attn, row_max)
                project_out(nc, const, l, attn, row_max, io["x"][0] if l == 0 else None, x_now, stats)
            with ExitStack() as part:
                keep = Scope(nc, part, f"keep_f{l}")
                m = Moe(l)
                acc = keep.sb("acc", [P, QT, D], F32)
                place, weight = keep.sb("place", [P, m.K, QT], I32), keep.sb("weight", [P, m.K, QT], F32)
                slot_expert = keep.sb("slot_expert", [P, m.NS], I32)
                resident = None
                if l == 1:
                    resident = {"up": keep.sb("up", [P, E, DB, 2, m.F], F32),
                                "down": keep.sb("down", [m.FW, E, m.FT, D], F32)}
                with ExitStack() as rows:
                    keep_x = Scope(nc, rows, f"keep_x{l}")
                    x_nt, x_n = keep_x.sb("x_nt", [P, DB, T], F32), keep_x.sb("x_n", [P, QT, D], F32)
                    normalise(nc, const, f"norm_f{l}", x_now, stats, x_nt, x_n)
                    route_and_share(nc, io, const, scratch, m, x_nt, x_n, acc, place, weight, slot_expert, resident)
                if resident:
                    run_resident_slots(nc, const, scratch, m, slot_expert, resident)
                else:
                    run_slots(nc, io, const, scratch, m, slot_expert)
                collect(nc, const, scratch, m, acc, place, weight, x_now, stats, out[0] if l == 1 else None)


_INS = (["x", "ctx_1024", "mask_BxSxS2_ik0", "g_xattn", "g_ffn"]
        + [f"L{l}_xattn_{k}{w}" for l in range(2) for w in "qkvo" for k in "wb"]
        + [f"L0_ffn_{n}" for n in ("w1s", "w2s", "w3s", "W1", "W2", "W3", "Wg")]
        + [f"L1_ffn_{n}" for n in ("W_gate_router", "expert_bias", "Wg", "Wu", "Wd", "Wg_s", "Wu_s", "Wd_s")])
_OUTS = [((1, T, D), "float32")]


def kernel(**inputs):
    import numpy as _np
    import concourse.bacc as _bacc
    from concourse import mybir as _mybir
    from concourse.bass_utils import run_bass_kernel_spmd as _run

    nc = _bacc.Bacc("TRN2", target_bir_lowering=False, num_devices=1)
    arrays, io = {}, {}
    for name in _INS:
        a = _np.ascontiguousarray(inputs[name])
        arrays[f"in_{name}_dram"] = a
        io[name] = nc.dram_tensor(f"in_{name}_dram", a.shape, _mybir.dt.from_np(a.dtype), kind="ExternalInput").ap()
    (shape, dtype), = _OUTS
    out = nc.dram_tensor("out_0_dram", shape, _mybir.dt.from_np(_np.dtype(dtype)), kind="ExternalOutput").ap()
    flamingo_kernel(nc, io, out)
    r = _run(nc, [arrays], core_ids=[0])
    return r.results[0]["out_0_dram"]
```
